# Optimizing a Trainium2 kernel written in Bass

```python
import numpy as np
import jax
import jax.numpy as jnp

def _softmax(x, axis=-1):
    return jax.nn.softmax(x, axis=axis)

def _gelu(x):
    return jax.nn.gelu(x, approximate=True)

def _silu(x):
    return jax.nn.silu(x)

def _sigmoid(x):
    return jax.nn.sigmoid(x)

def _layernorm(x, axis=-1, eps=1e-05):
    m = jnp.mean(x, axis=axis, keepdims=True)
    v = jnp.var(x, axis=axis, keepdims=True)
    return (x - m) / jnp.sqrt(v + eps)

def _scatter_add(tgt, idx, src, axis=0):
    return tgt.at[idx].add(src)

def _segment_sum(src, seg, n):
    return jax.ops.segment_sum(src, seg, n)
kernel_name = 'mk_prb_d2_jaxref_r8_6e8930'

def setup_inputs(seed: int=0):
    np.random.seed(seed)
    _w = jnp.asarray

    def _L0_attn_setup():
        import jax, jax.numpy as jnp
        import numpy as np
        from jax import lax
        B, S, D = (4, 512, 128)
        EPS = 1e-06

        def gate_loop_operator(k, v, q, a):

            def binary_operator(e_i, e_j):
                a_i, kv_i = e_i
                a_j, kv_j = e_j
                return (a_j * a_i, a_j * kv_i + kv_j)
            kv = (k * v).astype(jnp.complex64)
            _, y = lax.associative_scan(binary_operator, (a, kv), axis=1)
            return q * jnp.real(y)
        key = jax.random.key(seed)
        ks = jax.random.split(key, 8)
        std = 0.01
        return {'x': jax.random.normal(ks[0], (B, S, D), dtype=jnp.float32), 'wq': jax.random.normal(ks[1], (D, D), dtype=jnp.float32) * std, 'wk': jax.random.normal(ks[2], (D, D), dtype=jnp.float32) * std, 'wv': jax.random.normal(ks[3], (D, D), dtype=jnp.float32) * std, 'wa': jax.random.normal(ks[4], (D, 2 * D), dtype=jnp.float32) * std, 'wg': jax.random.normal(ks[5], (D, D), dtype=jnp.float32) * std, 'wo': jax.random.normal(ks[6], (D, D), dtype=jnp.float32) * std, 'rms_scale': jnp.ones((D,), dtype=jnp.float32)}
    _L0_attn_in = _L0_attn_setup()

    def _L0_ffn_setup():
        import jax, jax.numpy as jnp
        import numpy as np
        TOP_K = 2
        key = jax.random.key(seed)
        k1, k2, k3, k4 = jax.random.split(key, 4)
        B, S, H, F, E = (2, 256, 128, 352, 8)
        hidden_states = jax.random.normal(k1, (B, S, H), dtype=jnp.float32)
        wqkv = jax.random.normal(k2, (3 * E, H), dtype=jnp.float32) * 0.02
        w1 = jax.random.normal(k3, (E, 2 * F, H), dtype=jnp.float32) * 0.02
        w2 = jax.random.normal(k4, (E, H, F), dtype=jnp.float32) * 0.02
        return {'hidden_states': hidden_states, 'wqkv': wqkv, 'w1': w1, 'w2': w2}
    _L0_ffn_in = _L0_ffn_setup()

    def _L1_attn_setup():
        import jax, jax.numpy as jnp
        import numpy as np
        B, T, H, N = (4, 256, 128, 16)
        DT_MIN, DT_MAX = (0.001, 0.1)
        A_INIT_MIN, A_INIT_MAX = (0.5, 2.0)

        def _inv_softplus(x):
            return x + jnp.log(-jnp.expm1(-x))

        def _reference_tuple_inner(x, A_log, B_mat, C_mat, D_vec, W_dt, b_dt):
            u = x
            A = -jnp.exp(A_log)
            dt = jax.nn.softplus(jnp.einsum('bth,gh->btg', u, W_dt) + b_dt)
            state0 = jnp.zeros((u.shape[0], A_log.shape[0], A_log.shape[1]), dtype=u.dtype)

            def step(state, inp):
                dt_t, u_t = inp
                dtA = dt_t[..., None]
                A_bar = jnp.exp(dtA * A)
                state = A_bar * state + dtA * B_mat * u_t[..., None]
                y_t = jnp.einsum('bhn,hn->bh', state, C_mat) + D_vec * u_t
                return (state, y_t)
            state_final, ys = jax.lax.scan(step, state0, (dt.transpose(1, 0, 2), u.transpose(1, 0, 2)))
            out = ys.transpose(1, 0, 2)
            return (out, state_final)
        key = jax.random.key(seed)
        kx, ka, kb, kc, kw, kdt = jax.random.split(key, 6)
        x = jax.random.normal(kx, (B, T, H), dtype=jnp.float32)
        A_log = jax.random.uniform(ka, (H, N), minval=np.log(A_INIT_MIN), maxval=np.log(A_INIT_MAX), dtype=jnp.float32)
        B_mat = 0.02 * jax.random.normal(kb, (H, N), dtype=jnp.float32)
        C_mat = 0.02 * jax.random.normal(kc, (H, N), dtype=jnp.float32)
        D_vec = jnp.ones((H,), dtype=jnp.float32)
        W_dt = 0.02 * jax.random.normal(kw, (H, H), dtype=jnp.float32)
        b_dt = _inv_softplus(jax.random.uniform(kdt, (H,), minval=DT_MIN, maxval=DT_MAX, dtype=jnp.float32))
        return {'x': x, 'A_log': A_log, 'B_mat': B_mat, 'C_mat': C_mat, 'D_vec': D_vec, 'W_dt': W_dt, 'b_dt': b_dt}
    _L1_attn_in = _L1_attn_setup()

    def _L1_ffn_setup():
        import jax, jax.numpy as jnp
        import numpy as np
        B, S, D = (4, 64, 128)
        E, K, H = (64, 8, 32)
        ES, HS = (2, 256)
        key = jax.random.key(seed)
        ks = jax.random.split(key, 8)
        scale = 0.02
        rn = lambda k, shape, s: jax.random.normal(k, shape, jnp.float32) * s
        return {'x': rn(ks[0], (B, S, D), 1.0), 'router_w': rn(ks[1], (D, E), scale), 'router_b': jnp.zeros((E,), jnp.float32), 'w1': rn(ks[2], (E, D, H), scale), 'b1': jnp.zeros((E, H), jnp.float32), 'w2': rn(ks[3], (E, H, D), scale), 'b2': jnp.zeros((E, D), jnp.float32), 'sw1': rn(ks[4], (ES, D, HS), scale), 'sb1': jnp.zeros((ES, HS), jnp.float32), 'sw2': rn(ks[5], (ES, HS, D), scale), 'sb2': jnp.zeros((ES, D), jnp.float32)}
    _L1_ffn_in = _L1_ffn_setup()
    _d = {'L0_attn_x': _L0_attn_in['x'], 'L0_attn_wq': _L0_attn_in['wq'], 'L0_attn_wk': _L0_attn_in['wk'], 'L0_attn_wv': _L0_attn_in['wv'], 'L0_attn_wa': _L0_attn_in['wa'], 'L0_attn_wg': _L0_attn_in['wg'], 'L0_attn_wo': _L0_attn_in['wo'], 'L0_attn_rms_scale': _L0_attn_in['rms_scale'], 'L0_ffn_wqkv': _L0_ffn_in['wqkv'], 'L0_ffn_w1': _L0_ffn_in['w1'], 'L0_ffn_w2': _L0_ffn_in['w2'], 'L1_attn_A_log': _L1_attn_in['A_log'], 'L1_attn_B_mat': _L1_attn_in['B_mat'], 'L1_attn_C_mat': _L1_attn_in['C_mat'], 'L1_attn_D_vec': _L1_attn_in['D_vec'], 'L1_attn_W_dt': _L1_attn_in['W_dt'], 'L1_attn_b_dt': _L1_attn_in['b_dt'], 'L1_ffn_router_w': _L1_ffn_in['router_w'], 'L1_ffn_router_b': _L1_ffn_in['router_b'], 'L1_ffn_w1': _L1_ffn_in['w1'], 'L1_ffn_b1': _L1_ffn_in['b1'], 'L1_ffn_w2': _L1_ffn_in['w2'], 'L1_ffn_b2': _L1_ffn_in['b2'], 'L1_ffn_sw1': _L1_ffn_in['sw1'], 'L1_ffn_sb1': _L1_ffn_in['sb1'], 'L1_ffn_sw2': _L1_ffn_in['sw2'], 'L1_ffn_sb2': _L1_ffn_in['sb2']}
    _x0 = _d['L0_attn_x']
    _d['L0_attn_x'] = jax.random.normal(jax.random.fold_in(jax.random.key(seed), 1), (4, 512, 128), dtype=_x0.dtype)
    del _x0
    return _d

def reference(L0_attn_x, L0_attn_wq, L0_attn_wk, L0_attn_wv, L0_attn_wa, L0_attn_wg, L0_attn_wo, L0_attn_rms_scale, L0_ffn_wqkv, L0_ffn_w1, L0_ffn_w2, L1_attn_A_log, L1_attn_B_mat, L1_attn_C_mat, L1_attn_D_vec, L1_attn_W_dt, L1_attn_b_dt, L1_ffn_router_w, L1_ffn_router_b, L1_ffn_w1, L1_ffn_b1, L1_ffn_w2, L1_ffn_b2, L1_ffn_sw1, L1_ffn_sb1, L1_ffn_sw2, L1_ffn_sb2):

    def _L0_attn_ref(x, wq, wk, wv, wa, wg, wo, rms_scale):
        import jax, jax.numpy as jnp
        import numpy as np
        from jax import lax
        B, S, D = (4, 512, 128)
        EPS = 1e-06

        def gate_loop_operator(k, v, q, a):

            def binary_operator(e_i, e_j):
                a_i, kv_i = e_i
                a_j, kv_j = e_j
                return (a_j * a_i, a_j * kv_i + kv_j)
            kv = (k * v).astype(jnp.complex64)
            _, y = lax.associative_scan(binary_operator, (a, kv), axis=1)
            return q * jnp.real(y)
        xn = x * lax.rsqrt(jnp.mean(x * x, axis=-1, keepdims=True) + EPS) * rms_scale
        q = xn @ wq
        k = xn @ wk
        v = xn @ wv
        a = xn @ wa
        g = xn @ wg
        a_r, a_i = jnp.split(a, 2, axis=-1)
        a_c = lax.complex(a_r, a_i)
        magnitude = jax.nn.sigmoid(jnp.abs(a_c))
        phase = jnp.angle(a_c)
        a_c = magnitude * jnp.exp(1j * phase)
        y = gate_loop_operator(k, v, q, a_c)
        y = y * jax.nn.silu(g)
        return y @ wo

    def _L0_ffn_ref(hidden_states, wqkv, w1, w2):
        import jax, jax.numpy as jnp
        import numpy as np
        TOP_K = 2
        b, s, h = hidden_states.shape
        E = w1.shape[0]
        mixed = hidden_states @ wqkv.T
        q, k, v = jnp.split(mixed, 3, axis=-1)
        q = q.astype(jnp.float32)
        k = k.astype(jnp.float32)
        v = v.astype(jnp.float32)
        attn = jax.nn.softmax(q[..., :, None] * k[..., None, :], axis=-1)
        logits = jnp.einsum('bsej,bsj->bse', attn, v).reshape(-1, E)
        top_logits, idx = jax.lax.top_k(logits, TOP_K)
        scores = jax.nn.softmax(top_logits.astype(jnp.float32), axis=-1).astype(hidden_states.dtype)
        N = b * s
        x = hidden_states.reshape(N, h)
        token_ids = jnp.repeat(jnp.arange(N), TOP_K)
        expert_ids = idx.reshape(-1)
        x_rep = x[token_ids]
        out = jnp.zeros_like(x_rep)
        for e in range(E):
            h1 = x_rep @ w1[e].T
            a, g = jnp.split(h1, 2, axis=-1)
            he = jax.nn.silu(a) * g @ w2[e].T
            out = out + jnp.where((expert_ids == e)[:, None], he, jnp.zeros((), out.dtype))
        out = out * scores.reshape(-1, 1)
        combined = out.reshape(N, TOP_K, h).sum(axis=1)
        return combined.reshape(b, s, h)

    def _L1_attn_ref(x, A_log, B_mat, C_mat, D_vec, W_dt, b_dt):
        import jax, jax.numpy as jnp
        import numpy as np
        B, T, H, N = (4, 256, 128, 16)
        DT_MIN, DT_MAX = (0.001, 0.1)
        A_INIT_MIN, A_INIT_MAX = (0.5, 2.0)

        def _inv_softplus(x):
            return x + jnp.log(-jnp.expm1(-x))

        def _reference_tuple_inner(x, A_log, B_mat, C_mat, D_vec, W_dt, b_dt):
            u = x
            A = -jnp.exp(A_log)
            dt = jax.nn.softplus(jnp.einsum('bth,gh->btg', u, W_dt) + b_dt)
            state0 = jnp.zeros((u.shape[0], A_log.shape[0], A_log.shape[1]), dtype=u.dtype)

            def step(state, inp):
                dt_t, u_t = inp
                dtA = dt_t[..., None]
                A_bar = jnp.exp(dtA * A)
                state = A_bar * state + dtA * B_mat * u_t[..., None]
                y_t = jnp.einsum('bhn,hn->bh', state, C_mat) + D_vec * u_t
                return (state, y_t)
            state_final, ys = jax.lax.scan(step, state0, (dt.transpose(1, 0, 2), u.transpose(1, 0, 2)))
            out = ys.transpose(1, 0, 2)
            return (out, state_final)
        return _reference_tuple_inner(x, A_log, B_mat, C_mat, D_vec, W_dt, b_dt)[0]

    def _L1_ffn_ref(x, router_w, router_b, w1, b1, w2, b2, sw1, sb1, sw2, sb2):
        import jax, jax.numpy as jnp
        import numpy as np
        B, S, D = (4, 64, 128)
        E, K, H = (64, 8, 32)
        ES, HS = (2, 256)
        b_, s_, d_ = x.shape
        xf = x.reshape(-1, d_)
        probs = jax.nn.softmax(xf @ router_w + router_b, axis=-1)
        tw, ti = jax.lax.top_k(probs, K)
        tw = tw / jnp.sum(tw, axis=-1, keepdims=True)

        def body(acc, p):
            W1, B1, W2, B2, e = p
            h = jax.nn.silu(xf @ W1 + B1) @ W2 + B2
            cw = jnp.sum(jnp.where(ti == e, tw, 0.0), axis=-1)
            return (acc + cw[:, None] * h, None)
        routed, _ = jax.lax.scan(body, jnp.zeros_like(xf), (w1, b1, w2, b2, jnp.arange(w1.shape[0])))

        def shared_mlp(W1, B1, W2, B2):
            return jax.nn.silu(xf @ W1 + B1) @ W2 + B2
        shared = jnp.sum(jax.vmap(shared_mlp)(sw1, sb1, sw2, sb2), axis=0)
        return (routed + shared).reshape(b_, s_, d_)
    x = L0_attn_x
    xn = _layernorm(x, axis=-1)
    x = x + _L0_attn_ref(xn, L0_attn_wq, L0_attn_wk, L0_attn_wv, L0_attn_wa, L0_attn_wg, L0_attn_wo, L0_attn_rms_scale) + _L0_ffn_ref(xn, L0_ffn_wqkv, L0_ffn_w1, L0_ffn_w2)
    xn = _layernorm(x, axis=-1)
    x = x + _L1_attn_ref(xn, L1_attn_A_log, L1_attn_B_mat, L1_attn_C_mat, L1_attn_D_vec, L1_attn_W_dt, L1_attn_b_dt) + _L1_ffn_ref(xn, L1_ffn_router_w, L1_ffn_router_b, L1_ffn_w1, L1_ffn_b1, L1_ffn_w2, L1_ffn_b2, L1_ffn_sw1, L1_ffn_sb1, L1_ffn_sw2, L1_ffn_sb2)
    return x

_drawn_inputs = setup_inputs


def setup_inputs(seed=0):
    import zlib

    import numpy as np

    out = dict(_drawn_inputs(seed))
    spreads = {'L0_attn_rms_scale': (1.0, 0.6),
     'L1_attn_D_vec': (1.0, 0.2),
     'L1_ffn_router_b': (0.0, 0.586),
     'L1_ffn_b1': (0.0, 0.8),
     'L1_ffn_b2': (0.0, 0.442),
     'L1_ffn_sb1': (0.0, 1.916),
     'L1_ffn_sb2': (0.0, 0.334)}
    factors = {'L0_attn_wq': 8.0,
     'L0_attn_wk': 8.0,
     'L0_attn_wv': 8.0,
     'L0_attn_wa': 8.0,
     'L0_attn_wg': 8.0,
     'L0_attn_wo': 8.0,
     'L0_ffn_wqkv': 8.0,
     'L0_ffn_w1': 8.0,
     'L0_ffn_w2': 8.0,
     'L1_attn_A_log': 8.0,
     'L1_attn_B_mat': 64.0,
     'L1_attn_C_mat': 64.0,
     'L1_attn_W_dt': 64.0,
     'L1_attn_b_dt': 64.0,
     'L1_ffn_router_w': 3.553,
     'L1_ffn_w1': 8.0,
     'L1_ffn_w2': 8.0,
     'L1_ffn_sw1': 5.927}
    for name, (base, spread) in spreads.items():
        noise = np.random.default_rng([zlib.crc32(name.encode()), seed]).standard_normal(out[name].shape)
        drawn = base * np.exp(spread * noise) if base else spread * noise
        out[name] = jnp.asarray(drawn.astype(out[name].dtype))
    for name, factor in factors.items():
        out[name] = (out[name] * factor).astype(out[name].dtype)
    return out
```

```python
import math
from contextlib import ExitStack

import concourse.bass as bass
from concourse import mybir

ALU = mybir.AluOpType
ACT = mybir.ActivationFunctionType
AX = mybir.AxisListType.X
F32 = mybir.dt.float32
F32R = mybir.dt.float32r
BF16 = mybir.dt.bfloat16

P = 128
TB = 512
ROUND_TURN = 1.5 * 2.0 ** 10
ROUND_INT = 1.5 * 2.0 ** 23

V_RMS, V_D, V_BDT, V_SB2, V_SB1, V_B1 = 0, 1, 2, 3, 5, 9
N_VEC = 25


class Chain:

    def __init__(self, eng, sem, at=0):
        self.eng, self.sem, self.base, self.n = eng, sem, at, 0

    def __call__(self, ins):
        ins.then_inc(self.sem, 1)
        self.n += 1
        self.wait()

    def wait(self):
        self.eng.wait_ge(self.sem, self.base + self.n)


def program(nc, x, wq, wk, wv, wa, wg, wo, rms_scale, wqkv, w1, w2, A_log, B_mat, C_mat, D_vec, W_dt, b_dt,
            router_w, router_b, rw1, rb1, rw2, rb2, sw1, sb1, sw2, sb2, out):
    NB, T, D = x.shape
    NTOK = NB * T
    NT = NTOK // P
    TPB = TB // P
    E0, F2, _ = w1.shape
    F = F2 // 2
    FT = [(s, min(P, F - s)) for s in range(0, F, P)]
    NF = len(FT)
    E1, _, H1 = rw1.shape
    GE = P // H1
    NG = E1 // GE
    NS = A_log.shape[1]
    ES, _, HS = sw1.shape
    NSH = ES * HS // P
    LN_EPS, RMS_EPS = 1e-5, 1e-6
    assert D == P and T == TB and NS == NG and E0 == 2 * NB and NF == 3

    x_v = x.rearrange("b (c p) d -> p (b c) d", p=P)
    out_v = out.rearrange("b (c p) d -> p (b c) d", p=P)

    def row(a):
        return a.rearrange("(a d) -> a d", a=1)

    with ExitStack() as ctx:
        def sb(name, shape, dt=F32):
            return ctx.enter_context(nc.sbuf_tensor(name, shape, dt))

        def sem(name):
            return ctx.enter_context(nc.semaphore(name))

        ident = sb("ident", [P, P])
        sel = sb("sel", [P, NG * P], BF16)
        earlier = sb("earlier", [P, E0, E0])
        ones = sb("ones", [P, TB])
        half_pi = sb("half_pi", [P, 1])
        proj_raw = sb("proj_raw", [P, 6, P])
        proj_hi = sb("proj_hi", [P, 6, P], F32R)
        proj_lo = sb("proj_lo", [P, 6, P], F32R)
        wo_sb = sb("wo_sb", [P, P])
        turn_raw = sb("turn_raw", [P, 2, P])
        turn_hi = sb("turn_hi", [P, 2, P], F32R)
        turn_lo = sb("turn_lo", [P, 2, P], F32R)
        rout_raw = sb("rout_raw", [P, E1])
        rout_hi = sb("rout_hi", [P, E1], F32R)
        rout_lo = sb("rout_lo", [P, E1], F32R)
        rbias = sb("rbias", [P, E1])
        sw1_raw = sb("sw1_raw", [P, ES, HS])
        sw1_hi = sb("sw1_hi", [P, ES, HS], F32R)
        sw1_lo = sb("sw1_lo", [P, ES, HS], F32R)
        sw2_sb = sb("sw2_sb", [P, NSH, P])
        b2_sb = sb("b2_sb", [E1, P])
        vec_raw = sb("vec_raw", [N_VEC, P])
        vec_t = sb("vec_t", [P, N_VEC])
        b1_half = sb("b1_half", [P, NG])
        sb2_sum = sb("sb2_sum", [P, 1])
        ssm_raw = sb("ssm_raw", [P, 3, NS])
        ssm_a = sb("ssm_a", [P, NS])
        ssm_cb = sb("ssm_cb", [P, NS])

        res = sb("res", [P, NT, P])
        xn_tok = sb("xn_tok", [P, NT, P])
        xr_tok = sb("xr_tok", [P, NT, P])
        xn_hi = sb("xn_hi", [P, NTOK], F32R)
        xn_lo = sb("xn_lo", [P, NTOK], F32R)
        xr_hi = sb("xr_hi", [P, NTOK], F32R)
        xr_lo = sb("xr_lo", [P, NTOK], F32R)
        stats = sb("stats", [P, NT, 6])
        mv = sb("mv", [P, NT, 2])
        nrm = sb("nrm", [P, 6, NT])
        qkv = sb("qkv", [P, NT, 3 * E0])
        pair = sb("pair", [P, NT, E0 * E0])
        pair2 = sb("pair2", [P, NT, E0 * E0])
        rsm = sb("rsm", [P, 4, NT, E0])
        rrow = sb("rrow", [P, 3, NT])
        score0 = sb("score0", [P, NT, E0])
        e_raw1 = [sb(f"e_raw1_{j}", [P, 2 * NF, P]) for j in range(2)]
        e_raw2 = [sb(f"e_raw2_{j}", [P, F]) for j in range(2)]
        e_hi = [sb(f"e_hi_{j}", [P, F2], F32R) for j in range(2)]
        e_lo = [sb(f"e_lo_{j}", [P, F2], F32R) for j in range(2)]
        e_w2 = [sb(f"e_w2_{j}", [P, NF, P]) for j in range(2)]
        sil = sb("sil", [P, 2, TB])
        hid = sb("hid", [P, 2, NF, TB])
        at = {n: sb(f"at_{n}", [P, TB]) for n in (
            "k", "kv", "ar", "ai", "sq", "m2", "mag", "decay", "theta", "neg", "coarse", "fine",
            "cos", "sin", "zr", "zi")}
        u_t = xr_tok[:].rearrange("p a b -> p (a b)")
        y_t = xn_tok[:].rearrange("p a b -> p (a b)")
        dt_t = sb("dt_t", [P, NTOK])
        win_t = sb("win_t", [P, NTOK])
        cwt = sb("cwt", [P, TB])
        cw_b2 = sb("cw_b2", [E1, 2, TB])
        cw_hm = sb("cw_hm", [P, NTOK], BF16)
        cw_l = sb("cw_l", [P, NTOK], BF16)
        cw_mid = sb("cw_mid", [P, TB], BF16)
        g_raw1 = [sb(f"g_raw1_{j}", [P, GE, H1]) for j in range(2)]
        g_hi = [sb(f"g_hi_{j}", [P, P], F32R) for j in range(2)]
        g_lo = [sb(f"g_lo_{j}", [P, P], F32R) for j in range(2)]
        g_w2 = [sb(f"g_w2_{j}", [P, P]) for j in range(2)]

        ps = [ctx.enter_context(nc.psum_tensor(f"ps{i}", [P, TB], F32)) for i in range(8)]

        x_in = [sem(f"x_in{b}") for b in range(NB)]
        turn_in, proj_in, late_in = sem("turn_in"), sem("proj_in"), sem("late_in")
        e_in = [sem(f"e_in{j}") for j in range(2)]
        g_in = [sem(f"g_in{j}") for j in range(2)]
        g_w2_in = [sem(f"g_w2_in{j}") for j in range(2)]
        dve_own, act_own, pool_own = sem("dve_own"), sem("act_own"), sem("pool_own")
        out_done = sem("out_done")
        consts_ready = sem("consts_ready")
        var_ready, root_ready = sem("var_ready"), sem("root_ready")
        tok_ready = sem("tok_ready")
        small_turned, small_copied = sem("small_turned"), sem("small_copied")
        weights_split = sem("weights_split")
        turned, hi_ready, lo_ready = sem("turned"), sem("hi_ready"), sem("lo_ready")
        qkv_made, qkv_copied = sem("qkv_made"), sem("qkv_copied")
        r0_arg, r0_exp = sem("r0_arg"), sem("r0_exp")
        e_turned, e_hi_ready, e_lo_ready = sem("e_turned"), sem("e_hi_ready"), sem("e_lo_ready")
        a_made, g_made, silu_done, gated = sem("a_made"), sem("g_made"), sem("silu_done"), sem("gated")
        o_made, o_added = sem("o_made"), sem("o_added")
        att_pe, att_act, att_dve = sem("att_pe"), sem("att_act"), sem("att_dve")
        u_ready = sem("u_ready")
        dt_made, sp_exp, sp_poly, win_ready = sem("dt_made"), sem("sp_exp"), sem("sp_poly"), sem("win_ready")
        logits_made, r1_arg, r1_exp = sem("logits_made"), sem("r1_arg"), sem("r1_exp")
        cw_ready, cw_turned, cw_copied, cw_split = sem("cw_ready"), sem("cw_turned"), sem("cw_copied"), sem("cw_split")
        sh_made, sh_silu, sh_used, b2_used = sem("sh_made"), sem("sh_silu"), sem("sh_used"), sem("b2_used")
        g_split, h_made, cwx_made = sem("g_split"), sem("h_made"), sem("cwx_made")
        tanh_done, c1_done, hid_done, g_out = sem("tanh_done"), sem("c1_done"), sem("hid_done"), sem("g_out")
        decay_ready, scanned, weighted, y_added = sem("decay_ready"), sem("scanned"), sem("weighted"), sem("y_added")
        y_done, sum_ready, sum_turned, x2_ready = (
            sem("y_done"), sem("sum_ready"), sem("sum_turned"), sem("x2_ready"))

        def product(pe, acc, w_hi, w_lo, m_hi, m_lo):
            pe.matmul(acc, w_hi, m_hi, start=True, stop=False)
            pe.matmul(acc, w_lo, m_hi, start=False, stop=False)
            return pe.matmul(acc, w_hi, m_lo, start=False, stop=True)

        def blk(buf, b):
            return buf[:, b * TB:(b + 1) * TB]

        act_passed, pool_passed = sem("act_passed"), sem("pool_passed")

        NBLK = NB
        EPI = 2
        STEPS = EPI * NBLK * NF
        OUTS = EPI * NBLK
        N_ATT_PE, N_ATT_ACT, N_ATT_DVE = 7, 14, 29
        PREP_HI, PREP_LO = 4, 2
        GPI = 2
        GSTEPS = GPI * NBLK
        hid_ring = [hid[:, r, 0, :] for r in range(2)]
        c1_ring = [hid[:, r, 1, :] for r in range(2)]
        RING = 4
        decay_ring = [at[n] for n in ("k", "kv", "m2", "mag")]
        state_ring = [at[n] for n in ("ar", "ai", "zr", "zi")]
        term_ring = [at[n] for n in ("sq", "coarse")]
        softplus_bufs = [[at[n] for n in names] for names in (
            ("cos", "zr", "sin"), ("m2", "decay", "mag"), ("k", "kv", "ar"), ("ai", "coarse", "fine"))]

        block = ctx.enter_context(nc.Block())

        @block.sync
        def _(sp):
            def load_expert(e, j):
                for half in range(2):
                    r0 = half * F
                    sp.dma_start(e_raw1[j][:, half * NF:half * NF + 2, :],
                                 w1[e, r0:r0 + 2 * P, :].rearrange("... (c p) d -> ... p c d", p=P)
                                 ).then_inc(e_in[j], 16)
                    sp.dma_start(e_raw1[j][0:FT[2][1], half * NF + 2, :],
                                 w1[e, r0 + 2 * P:r0 + F, :]).then_inc(e_in[j], 16)
                sp.dma_start(e_raw2[j][:, :], w2[e, :, :]).then_inc(e_in[j], 16)

            def load_group(g, j):
                load_group_w1(g, j)
                load_group_w2(g, j)

            def load_group_w1(g, j):
                sp.dma_start(g_raw1[j][:, :, :], rw1[bass.ds(g * GE, GE), :, :].rearrange("e d h -> d e h")
                             ).then_inc(g_in[j], 16)

            def load_group_w2(g, j):
                sp.dma_start(g_w2[j][:, :], rw2[bass.ds(g * GE, GE), :, :].rearrange("e h d -> (e h) d")
                             ).then_inc(g_w2_in[j], 16)

            for b in range(NB):
                sp.dma_start(res[:, b * TPB:(b + 1) * TPB, :], x_v[:, b * TPB:(b + 1) * TPB, :]).then_inc(x_in[b], 16)
                if b == 0:
                    sp.dma_start(turn_raw[0:3 * E0, 0, :], wqkv).then_inc(turn_in, 16)
                    sp.dma_start(turn_raw[:, 1, :], W_dt).then_inc(turn_in, 16)
                    sp.dma_start(vec_raw[V_RMS:V_RMS + 1, :], row(rms_scale)).then_inc(turn_in, 16)
                    sp.dma_start(vec_raw[V_D:V_D + 1, :], row(D_vec)).then_inc(turn_in, 16)
                    sp.dma_start(vec_raw[V_BDT:V_BDT + 1, :], row(b_dt)).then_inc(turn_in, 16)
                    sp.dma_start(vec_raw[V_SB2:V_SB2 + ES, :], sb2).then_inc(turn_in, 16)
                    sp.dma_start(vec_raw[V_SB1:V_SB1 + NSH, :], sb1.rearrange("e (c h) -> (e c) h", h=P)
                                 ).then_inc(turn_in, 16)
                    sp.dma_start(vec_raw[V_B1:V_B1 + NG, :], rb1.rearrange("(g e) h -> g (e h)", e=GE)
                                 ).then_inc(turn_in, 16)
            load_expert(0, 0)
            for n, w in enumerate((wk, wv, None, None, wg, wq)):
                if w is not None:
                    sp.dma_start(proj_raw[:, n, :], w).then_inc(proj_in, 16)
            sp.dma_start(proj_raw[:, 2:4, :], wa.rearrange("d (c h) -> d c h", h=P)).then_inc(proj_in, 16)
            sp.dma_start(wo_sb[:, :], wo).then_inc(proj_in, 16)
            load_expert(1, 1)
            sp.dma_start(rout_raw[:, :], router_w).then_inc(late_in, 16)
            sp.dma_start(rbias[:, :], row(router_b).to_broadcast([P, E1])).then_inc(late_in, 16)
            sp.dma_start(sw1_raw[:, :, :], sw1.rearrange("e d h -> d e h")).then_inc(late_in, 16)
            sp.dma_start(sw2_sb[:, :, :], sw2.rearrange("e (c h) d -> h (e c) d", h=P)).then_inc(late_in, 16)
            sp.dma_start(b2_sb[:, :], rb2).then_inc(late_in, 16)
            for n, w in enumerate((A_log, B_mat, C_mat)):
                sp.dma_start(ssm_raw[:, n, :], w).then_inc(late_in, 16)
            load_group(0, 0)
            load_group(1, 1)
            with sp.Fori(0, NB - 1) as i:
                sp.wait_ge(e_turned, i * 6 + 3)
                load_expert(i * 2 + 2, 0)
                sp.wait_ge(e_turned, i * 6 + 6)
                load_expert(i * 2 + 3, 1)
            sp.wait_ge(e_turned, (NB - 1) * 6 + 3)
            load_expert(0, 0)
            with sp.Fori(0, NG // GPI - 1) as i:
                for j in range(GPI):
                    sp.wait_ge(g_split, i * GPI + j + 1)
                    load_group_w1(i * GPI + GPI + j, j)
                for j in range(GPI):
                    sp.wait_ge(g_out, i * GSTEPS + (j + 1) * NBLK + 2)
                    load_group_w2(i * GPI + GPI + j, j)
            for b in range(NB):
                sp.wait_ge(x2_ready, b + 1)
                sp.dma_start(out_v[:, b * TPB:(b + 1) * TPB, :], res[:, b * TPB:(b + 1) * TPB, :]
                             ).then_inc(out_done, 16)
            sp.wait_ge(out_done, 16 * NB)

        @block.gpsimd
        def _(pool):
            own = Chain(pool, pool_own)
            own(pool.memset(ident[:, :], 0.0))
            own(pool.affine_select(out=ident[:, :], in_=ident[:, :], compare_op=ALU.not_equal, fill=1.0,
                                   base=0, pattern=[[-1, P]], channel_multiplier=1))
            pool.nop().then_inc(consts_ready, 1)
            own(pool.memset(earlier[:, :, :], 0.0))
            own(pool.affine_select(out=earlier[:, :, :], in_=earlier[:, :, :], compare_op=ALU.is_ge, fill=1.0,
                                   base=0, pattern=[[-1, E0], [1, E0]], channel_multiplier=0))
            own(pool.memset(ones[:, :], 1.0))
            own(pool.memset(half_pi[:, :], math.pi / 2))
            pool.nop().then_inc(consts_ready, 1)

            def split(src, hi, lo):
                own(pool.tensor_scalar(hi, src, 1.0, 0.0, ALU.mult, ALU.add))
                own(pool.tensor_tensor(lo, src, hi.bitcast(F32), ALU.subtract))

            pool.wait_ge(proj_in, 16 * 6)
            split(proj_raw[:, :, :], proj_hi[:, :, :], proj_lo[:, :, :])
            pool.nop().then_inc(weights_split, 1)
            own(pool.memset(sel[:, :], 0.0))
            sel_v = sel[:, :].rearrange("p (c h) -> p c h", h=H1)
            for first in (0, E1):
                own(pool.affine_select(out=sel_v, in_=sel_v, compare_op=ALU.not_equal, fill=1.0,
                                       base=-first, pattern=[[-1, E1], [0, H1]], channel_multiplier=1))
            own(pool.memset(cw_l[:, :], 0.0))
            pool.wait_ge(late_in, 16 * 8)
            split(rout_raw[:, :], rout_hi[:, :], rout_lo[:, :])
            split(sw1_raw[:, :, :], sw1_hi[:, :, :], sw1_lo[:, :, :])
            own(pool.tensor_tensor(ssm_cb[:, :], ssm_raw[:, 1, :], ssm_raw[:, 2, :], ALU.mult))
            pool.nop().then_inc(weights_split, 1)

            def split_group(j):
                split(g_raw1[j][:, :, :].rearrange("p e h -> p (e h)"), g_hi[j][:, :], g_lo[j][:, :])
                pool.nop().then_inc(g_split, 1)

            for j in range(GPI):
                pool.wait_ge(g_in[j], 16)
                split_group(j)

            for b in range(NBLK):
                pool.wait_ge(sp_exp, b + 1)
                e, _, p = softplus_bufs[b]
                own(pool.tensor_scalar(p[:, :], e[:, :], -1.0 / 4, 1.0 / 3, ALU.mult, ALU.add))
                own(pool.tensor_tensor(p[:, :], p[:, :], e[:, :], ALU.mult))
                own(pool.tensor_scalar(p[:, :], p[:, :], 1.0, -1.0 / 2, ALU.mult, ALU.add))
                own(pool.tensor_tensor(p[:, :], p[:, :], e[:, :], ALU.mult))
                own(pool.tensor_scalar(p[:, :], p[:, :], 1.0, 1.0, ALU.mult, ALU.add))
                own(pool.tensor_tensor(p[:, :], p[:, :], e[:, :], ALU.mult))
                pool.nop().then_inc(sp_poly, 1)
            pool.wait_ge(cw_turned, NBLK)
            own(pool.tensor_scalar(y_t, u_t, vec_t[:, V_D:V_D + 1], 0.0, ALU.mult, ALU.add))

            n0 = own.n

            def turn(i, last):
                own = Chain(pool, pool_own, i * (GSTEPS + 2 * GPI) + n0)
                for s in range(GSTEPS):
                    j, tb = divmod(s, NBLK)
                    pool.wait_ge(weighted, i * GSTEPS + s + 1 + RING)
                    pool.nop().then_inc(pool_passed, 1)
                    own(pool.tensor_tensor(blk(y_t, tb), blk(y_t, tb), term_ring[s % 2][:, :], ALU.add))
                    pool.nop().then_inc(y_added, 1)
                    if s % NBLK == NBLK - 1 and not last:
                        pool.wait_ge(g_in[j], i * 16 + 32)
                        pool.wait_ge(h_made, i * GSTEPS + (j + 1) * NBLK)
                        own_split(own, j)

            def own_split(own, j):
                src = g_raw1[j][:, :, :].rearrange("p e h -> p (e h)")
                pool.nop().then_inc(pool_passed, 1)
                own(pool.tensor_scalar(g_hi[j][:, :], src, 1.0, 0.0, ALU.mult, ALU.add))
                own(pool.tensor_tensor(g_lo[j][:, :], src, g_hi[j][:, :].bitcast(F32), ALU.subtract))
                pool.nop().then_inc(g_split, 1)

            pool.nop().then_inc(y_added, 2)
            with pool.Fori(0, NG // GPI - 1) as i:
                turn(i, False)
            turn(NG // GPI - 1, True)
            pool.nop().then_inc(y_done, 1)

        @block.scalar
        def _(act):
            act.wait_ge(var_ready, 1)
            act.activation(nrm[:, 1, :], nrm[:, 0, :], ACT.Sqrt).then_inc(root_ready, 1)
            act.wait_ge(var_ready, 2)
            act.activation(nrm[:, 4, :], nrm[:, 3, :], ACT.Sqrt).then_inc(root_ready, 1)
            for b in range(NBLK):
                act.wait_ge(turned, b + 1)
                act.activation(blk(xn_hi, b), ps[b][:, :], ACT.Copy).then_inc(hi_ready, 1)

            def prep_w1(j, base):
                n = base * 3
                act.wait_ge(e_turned, n + 1)
                act.activation(e_hi[j][:, 0:F], ps[6][:, 0:F], ACT.Copy).then_inc(e_hi_ready, 1)
                act.wait_ge(e_turned, n + 2)
                act.activation(e_hi[j][:, F:F2], ps[7][:, 0:F], ACT.Copy).then_inc(e_hi_ready, 1)

            def prep_w2(j, base):
                act.wait_ge(e_turned, base * 3 + 3)
                act.activation(e_w2[j][:, 0:2, :], ps[6][:, 0:2 * P].rearrange("p (c d) -> p c d", d=P),
                               ACT.Copy).then_inc(e_hi_ready, 1)
                act.activation(e_w2[j][0:FT[2][1], 2, :], ps[6][0:FT[2][1], 2 * P:3 * P],
                               ACT.Copy).then_inc(e_hi_ready, 1)

            for b in range(NBLK):
                act.wait_ge(turned, NBLK + b + 1)
                act.activation(blk(xr_hi, b), ps[4 + b][:, :], ACT.Identity,
                               scale=vec_t[:, V_RMS:V_RMS + 1]).then_inc(hi_ready, 1)
            prep_w1(0, 0)
            prep_w2(0, 0)
            for n in range(2):
                act.wait_ge(r0_arg, n + 1)
                if n == 0:
                    act.activation(pair[:, :, :], pair[:, :, :], ACT.Exp).then_inc(r0_exp, 1)
                else:
                    act.activation(rsm[:, 1, :, :], rsm[:, 1, :, :], ACT.Exp).then_inc(r0_exp, 1)

            act.nop().then_inc(silu_done, 2)
            act.nop().then_inc(att_act, 1)
            act.wait_ge(consts_ready, 2)
            with act.Fori(0, NB) as i:
                own = Chain(act, att_act, i * N_ATT_ACT + 1)

                def pe_step(n):
                    act.wait_ge(att_pe, i * N_ATT_PE + n)

                def dve_step(n):
                    act.wait_ge(att_dve, i * N_ATT_DVE + 1 + n)

                for s in range(STEPS):
                    if s == 6:
                        act.wait_ge(o_made, i * OUTS + 2)
                        prep_w1(1, i * 2 + 1)
                    if s == 8:
                        prep_w2(1, i * 2 + 1)
                    if s == 14:
                        act.wait_ge(o_made, i * OUTS + NBLK + 2)
                        prep_w1(0, i * 2 + 2)
                    if s == 16:
                        prep_w2(0, i * 2 + 2)
                    if s == 0:
                        pe_step(1)
                        own(act.activation(at["k"][:, :], ps[6][:, :], ACT.Copy))
                    if s == 2:
                        pe_step(3)
                        own(act.activation(at["ar"][:, :], ps[6][:, :], ACT.Copy))
                    if s == 3:
                        pe_step(4)
                        own(act.activation(at["ai"][:, :], ps[7][:, :], ACT.Copy))
                        own(act.activation(at["sq"][:, :], at["ar"][:, :], ACT.Square))
                        own(act.activation(at["m2"][:, :], at["ai"][:, :], ACT.Square))
                        own(act.activation(at["neg"][:, :], at["ar"][:, :], ACT.Abs))
                    if s == 6:
                        dve_step(3)
                        own(act.activation(at["mag"][:, :], at["m2"][:, :], ACT.Sqrt))
                    if s == 8:
                        own(act.activation(at["decay"][:, :], at["mag"][:, :], ACT.Sigmoid))
                        dve_step(6)
                        own(act.activation(at["theta"][:, :], at["k"][:, :], ACT.Arctan))
                    if s == 14:
                        dve_step(17)
                        own(act.activation(at["m2"][:, :], at["theta"][:, :], ACT.Abs))
                        own(act.activation(at["mag"][:, :], at["theta"][:, :], ACT.Sin, scale=math.pi))
                        own(act.activation(at["k"][:, :], at["m2"][:, :], ACT.Sin, scale=-math.pi,
                                           bias=half_pi[:, 0:1]))
                        own(act.activation(at["sq"][:, :], at["mag"][:, :], ACT.Square))
                    if s == 18:
                        pe_step(5)
                        own(act.activation(at["m2"][:, :], ps[6][:, :], ACT.Silu))
                    M = FT[s % NF][1]
                    act.wait_ge(a_made, i * STEPS + s + 1)
                    act.wait_ge(gated, i * STEPS + s + 1)
                    act.activation(sil[0:M, s % 2, :], ps[s % 2][0:M, :], ACT.Silu).then_inc(silu_done, 1)
                assert own.n == N_ATT_ACT

            act.wait_ge(late_in, 16 * 8)
            act.wait_ge(var_ready, 3)
            act.activation(nrm[:, 1, :], nrm[:, 0, :], ACT.Sqrt).then_inc(root_ready, 1)
            for b in range(NBLK):
                act.wait_ge(turned, 2 * NBLK + b + 1)
                act.activation(blk(u_t, b), ps[b][:, :], ACT.Copy).then_inc(u_ready, 1)
            own = Chain(act, act_own)
            own(act.activation(ssm_a[:, :], ssm_raw[:, 0, :], ACT.Exp))
            own(act.activation(ssm_a[:, :], ssm_a[:, :], ACT.Copy, scale=-1.0))
            own(act.activation(b1_half[:, :], vec_t[:, V_B1:V_B1 + NG], ACT.Copy, scale=0.5))
            for b in range(NBLK):
                e, l, _ = softplus_bufs[b]
                act.wait_ge(dt_made, b + 1)
                own(act.activation(blk(dt_t, b), ps[4 + b][:, :], ACT.Identity, bias=vec_t[:, V_BDT:V_BDT + 1]))
                own(act.activation(e[:, :], blk(dt_t, b), ACT.Abs))
                own(act.activation(e[:, :], e[:, :], ACT.Exp, scale=-1.0))
                own(act.activation(l[:, :], e[:, :], ACT.Ln, bias=1.0))
                act.nop().then_inc(sp_exp, 1)
            for c in range(NSH * NBLK):
                k, tb = divmod(c, NBLK)
                if c == NSH * NBLK // 4:
                    act.wait_ge(r1_arg, 1)
                    act.activation(pair[:, :, :], pair[:, :, :], ACT.Exp).then_inc(r1_exp, 1)
                act.wait_ge(sh_made, c + 1)
                if c >= 2:
                    act.wait_ge(sh_used, c - 1)
                act.activation(hid[:, c % 2, 2, :], ps[2 + c % 2][:, :], ACT.Silu,
                               bias=vec_t[:, V_SB1 + k:V_SB1 + k + 1]).then_inc(sh_silu, 1)
            for b in range(NBLK):
                act.wait_ge(cw_turned, b + 1)
                if b >= 2:
                    act.wait_ge(b2_used, b - 1)
                act.activation(cw_b2[:, b % 2, :], ps[b % 2][0:E1, :], ACT.Copy, scale=2.0).then_inc(cw_copied, 1)

            act.activation(nrm[:, 5, 0:1], nrm[:, 0, 0:1], ACT.Exp)
            act.nop().then_inc(tanh_done, 2)
            act.nop().then_inc(weighted, RING)

            def decay(i, s):
                act.wait_ge(scanned, i * GSTEPS + s + 1)
                act.nop().then_inc(act_passed, 1)
                act.activation(decay_ring[s % RING][:, :], blk(dt_t, s % NBLK), ACT.Exp,
                               scale=ssm_a[:, bass.ds(i * GPI + s // NBLK, 1)]).then_inc(decay_ready, 1)

            def group_turn(i, last):
                for s in range(GSTEPS):
                    g = i * GPI + s // NBLK
                    act.wait_ge(h_made, i * GSTEPS + s + 1)
                    act.wait_ge(c1_done, i * GSTEPS + s + 1)
                    act.nop().then_inc(act_passed, 1)
                    act.activation(sil[:, s % 2, :], ps[s % 2][:, :], ACT.Tanh, scale=0.5,
                                   bias=b1_half[:, bass.ds(g, 1)]).then_inc(tanh_done, 1)
                    if s + 2 < GSTEPS:
                        decay(i, s + 2)
                    elif not last:
                        decay(i + 1, s + 2 - GSTEPS)
                    act.wait_ge(scanned, i * GSTEPS + s + 1 + RING)
                    act.wait_ge(y_added, i * GSTEPS + s + 1)
                    act.nop().then_inc(act_passed, 1)
                    act.activation(term_ring[s % 2][:, :], state_ring[s % RING][:, :], ACT.Copy,
                                   scale=ssm_cb[:, bass.ds(g, 1)]).then_inc(weighted, 1)

            act.wait_ge(win_ready, NBLK)
            for s in range(2):
                decay(0, s)
            with act.Fori(0, NG // GPI - 1) as i:
                group_turn(i, False)
            group_turn(NG // GPI - 1, True)

        @block.vector
        def _(dve):
            own = Chain(dve, dve_own)

            def norm_stats(layer):
                for t in range(NT):
                    if layer == 0 and t % TPB == 0:
                        dve.wait_ge(x_in[t // TPB], 16)
                    dve.bn_stats(stats[:, t, :], res[:, t, :]).then_inc(dve_own, 1)
                own.n += NT
                own.wait()
                for t in range(NT):
                    dve.bn_aggr(mv[:, t, :], stats[:, t, :]).then_inc(dve_own, 1)
                own.n += NT
                own.wait()
                own(dve.tensor_scalar(nrm[:, 0, :], mv[:, :, 1], LN_EPS, None, ALU.add))
                dve.nop().then_inc(var_ready, 1)

            norm_stats(0)
            dve.wait_ge(root_ready, 1)
            own(dve.reciprocal(nrm[:, 2, :], nrm[:, 1, :]))
            own(dve.tensor_tensor(nrm[:, 3, :], mv[:, :, 1], nrm[:, 2, :], ALU.mult))
            own(dve.tensor_tensor(nrm[:, 3, :], nrm[:, 3, :], nrm[:, 2, :], ALU.mult))
            own(dve.tensor_scalar(nrm[:, 3, :], nrm[:, 3, :], RMS_EPS, None, ALU.add))
            dve.nop().then_inc(var_ready, 1)
            for t in range(NT):
                dve.tensor_scalar(xn_tok[:, t, :], res[:, t, :], mv[:, t, 0:1], nrm[:, 2, t:t + 1],
                                  ALU.subtract, ALU.mult).then_inc(tok_ready, 1)
            dve.wait_ge(root_ready, 2)
            own(dve.reciprocal(nrm[:, 5, :], nrm[:, 4, :]))
            own(dve.tensor_tensor(nrm[:, 5, :], nrm[:, 5, :], nrm[:, 2, :], ALU.mult))
            for t in range(NT):
                dve.tensor_scalar(xr_tok[:, t, :], res[:, t, :], mv[:, t, 0:1], nrm[:, 5, t:t + 1],
                                  ALU.subtract, ALU.mult).then_inc(tok_ready, 1)
            dve.wait_ge(small_turned, 1)
            own(dve.tensor_copy(vec_t[:, :], ps[7][:, 0:N_VEC]))
            own(dve.tensor_copy(turn_hi[:, 0, 0:3 * E0], ps[7][:, P:P + 3 * E0]))
            own(dve.tensor_copy(turn_hi[:, 1, :], ps[7][:, 2 * P:3 * P]))
            own(dve.tensor_tensor(turn_lo[:, 0, 0:3 * E0], ps[7][:, P:P + 3 * E0],
                                  turn_hi[:, 0, 0:3 * E0].bitcast(F32), ALU.subtract))
            own(dve.tensor_tensor(turn_lo[:, 1, :], ps[7][:, 2 * P:3 * P], turn_hi[:, 1, :].bitcast(F32),
                                  ALU.subtract))
            own(dve.tensor_tensor(sb2_sum[:, :], vec_t[:, V_SB2:V_SB2 + 1], vec_t[:, V_SB2 + 1:V_SB2 + 2], ALU.add))
            dve.nop().then_inc(small_copied, 1)
            for b in range(NBLK):
                dve.wait_ge(hi_ready, b + 1)
                dve.tensor_tensor(blk(xn_lo, b), ps[b][:, :], blk(xn_hi, b).bitcast(F32), ALU.subtract
                                  ).then_inc(lo_ready, 1)
            dve.wait_ge(qkv_made, 1)
            own(dve.tensor_copy(qkv[:, :, :].rearrange("p t c -> p (t c)"), ps[0][:, 0:NT * 3 * E0]))
            dve.nop().then_inc(qkv_copied, 1)
            for b in range(NBLK):
                dve.wait_ge(hi_ready, NBLK + b + 1)
                dve.scalar_tensor_tensor(blk(xr_lo, b), ps[4 + b][:, :], vec_t[:, V_RMS:V_RMS + 1],
                                         blk(xr_hi, b).bitcast(F32), ALU.mult, ALU.subtract).then_inc(lo_ready, 1)

            def prep(base, j):
                for half in range(2):
                    dve.wait_ge(e_hi_ready, base * PREP_HI + half + 1)
                    dve.tensor_tensor(e_lo[j][:, half * F:(half + 1) * F], ps[6 + half][:, 0:F],
                                      e_hi[j][:, half * F:(half + 1) * F].bitcast(F32), ALU.subtract
                                      ).then_inc(e_lo_ready, 1)

            prep(0, 0)

            def over_e(a):
                return a[:, :, :, None].to_broadcast([P, NT, E0, E0])

            def over_j(a):
                return a[:, :, None, :].to_broadcast([P, NT, E0, E0])

            pr = pair[:, :, :].rearrange("p t (e j) -> p t e j", j=E0)
            pr2 = pair2[:, :, :].rearrange("p t (e j) -> p t e j", j=E0)
            q, k, v = (qkv[:, :, n * E0:(n + 1) * E0] for n in range(3))
            lg, ex, den, rank = (rsm[:, n, :, :] for n in range(4))
            own(dve.tensor_tensor(pr, over_e(q), over_j(k), ALU.mult))
            own(dve.tensor_reduce(den, pr, AX, ALU.max))
            own(dve.tensor_tensor(pr, pr, over_e(den), ALU.subtract))
            dve.nop().then_inc(r0_arg, 1)
            dve.wait_ge(r0_exp, 1)
            own(dve.tensor_reduce(den, pr, AX, ALU.add))
            own(dve.tensor_tensor(pr, pr, over_j(v), ALU.mult))
            own(dve.tensor_reduce(lg, pr, AX, ALU.add))
            own(dve.reciprocal(den, den))
            own(dve.tensor_tensor(lg, lg, den, ALU.mult))
            own(dve.tensor_tensor(pr, over_j(lg), over_e(lg), ALU.is_gt))
            own(dve.tensor_tensor(pr2, over_j(lg), over_e(lg), ALU.is_equal))
            dve.wait_ge(consts_ready, 2)
            own(dve.tensor_tensor(pr2, pr2, earlier[:, None, :, :].to_broadcast([P, NT, E0, E0]), ALU.mult))
            own(dve.tensor_tensor(pr, pr, pr2, ALU.add))
            own(dve.tensor_reduce(rank, pr, AX, ALU.add))
            own(dve.tensor_scalar(rank, rank, 1.5, None, ALU.is_lt))
            own(dve.tensor_reduce(rrow[:, 0, :], lg, AX, ALU.max))
            own(dve.tensor_tensor(ex, lg, rrow[:, 0, :, None].to_broadcast([P, NT, E0]), ALU.subtract))
            dve.nop().then_inc(r0_arg, 1)
            dve.wait_ge(r0_exp, 2)
            own(dve.tensor_tensor(ex, ex, rank, ALU.mult))
            own(dve.tensor_reduce(rrow[:, 1, :], ex, AX, ALU.add))
            own(dve.reciprocal(rrow[:, 2, :], rrow[:, 1, :]))
            own(dve.tensor_tensor(score0[:, :, :], ex, rrow[:, 2, :, None].to_broadcast([P, NT, E0]), ALU.mult))

            dve.nop().then_inc(gated, 2)
            dve.nop().then_inc(o_added, 2)
            dve.nop().then_inc(att_dve, 1)
            with dve.Fori(0, NB) as i:
                att = Chain(dve, att_dve, i * N_ATT_DVE + 1)
                A = {n: a[:, :] for n, a in at.items()}

                def pe_step(n):
                    dve.wait_ge(att_pe, i * N_ATT_PE + n)

                def act_step(n):
                    dve.wait_ge(att_act, i * N_ATT_ACT + 1 + n)

                def attention(s):
                    if s == 1:
                        pe_step(2)
                        act_step(1)
                        att(dve.tensor_tensor(A["kv"], ps[7][:, :], A["k"], ALU.mult))
                    if s == 4:
                        act_step(5)
                        att(dve.tensor_tensor(A["m2"], A["m2"], A["sq"], ALU.add))
                        att(dve.tensor_scalar(A["m2"], A["m2"], 2.0 ** -110, 2.0 ** 117, ALU.max, ALU.min))
                    if s == 6:
                        act_step(7)
                        att(dve.tensor_tensor(A["k"], A["neg"], A["mag"], ALU.add))
                        att(dve.reciprocal(A["m2"], A["k"]))
                    if s == 7:
                        att(dve.tensor_tensor(A["k"], A["ai"], A["m2"], ALU.mult))
                        att(dve.tensor_scalar(A["neg"], A["ar"], 0.0, -2.0, ALU.is_lt, ALU.mult))
                    if s == 8:
                        act_step(9)
                        att(dve.scalar_tensor_tensor(A["theta"], A["neg"], 1.0, A["theta"], ALU.add, ALU.mult))
                    if s == 9:
                        att(dve.scalar_tensor_tensor(A["theta"], A["neg"], -math.pi / 4, A["theta"],
                                                     ALU.mult, ALU.add))
                        att(dve.tensor_scalar(A["theta"], A["theta"], 1.0 / math.pi, None, ALU.mult))
                    if s == 10:
                        att(dve.tensor_scalar(A["coarse"], A["theta"], ROUND_TURN, ROUND_TURN, ALU.add, ALU.subtract))
                        att(dve.tensor_tensor(A["fine"], A["theta"], A["coarse"], ALU.subtract))
                    if s == 11:
                        att(dve.tensor_tensor_scan(A["zr"], ones[:, :], A["coarse"], 0.0, ALU.mult, ALU.add))
                    if s == 12:
                        att(dve.tensor_tensor_scan(A["zi"], ones[:, :], A["fine"], 0.0, ALU.mult, ALU.add))
                        att(dve.tensor_scalar(A["coarse"], A["zr"], ROUND_INT, ROUND_INT, ALU.add, ALU.subtract))
                    if s == 13:
                        att(dve.tensor_tensor(A["zr"], A["zr"], A["coarse"], ALU.subtract))
                        att(dve.tensor_tensor(A["theta"], A["zr"], A["zi"], ALU.add))
                    if s == 15:
                        act_step(13)
                        att(dve.scalar_tensor_tensor(A["sin"], A["mag"], 2.0, A["k"], ALU.mult, ALU.mult))
                        att(dve.tensor_scalar(A["cos"], A["sq"], -2.0, 1.0, ALU.mult, ALU.add))
                    if s == 16:
                        att(dve.tensor_tensor(A["zr"], A["kv"], A["cos"], ALU.mult))
                        att(dve.tensor_tensor(A["zi"], A["kv"], A["sin"], ALU.mult))
                    if s == 17:
                        att(dve.tensor_tensor_scan(A["coarse"], A["decay"], A["zr"], 0.0, ALU.mult, ALU.add))
                        att(dve.tensor_tensor_scan(A["fine"], A["decay"], A["zi"], 0.0, ALU.mult, ALU.add))
                    if s == 18:
                        att(dve.tensor_tensor(A["coarse"], A["coarse"], A["cos"], ALU.mult))
                        att(dve.tensor_tensor(A["fine"], A["fine"], A["sin"], ALU.mult))
                    if s == 19:
                        att(dve.tensor_tensor(A["coarse"], A["coarse"], A["fine"], ALU.add))
                    if s == 20:
                        pe_step(6)
                        act_step(14)
                        att(dve.tensor_tensor(A["coarse"], ps[7][:, :], A["coarse"], ALU.mult))
                        att(dve.tensor_tensor(A["kv"], A["coarse"], A["m2"], ALU.mult))
                    if s == 23:
                        pe_step(7)
                        dve.wait_ge(o_added, i * OUTS + OUTS + 1)
                        r = res[:, bass.ds(i * TPB, TPB), :].rearrange("p t d -> p (t d)")
                        att(dve.tensor_tensor(r, r, ps[6][:, :], ALU.add))

                def add_output(o):
                    j, tb = divmod(o, NBLK)
                    dve.wait_ge(o_made, i * OUTS + o + 3)
                    dve.wait_ge(o_added, i * OUTS + o + 1)
                    for n in range(TPB):
                        t = tb * TPB + n
                        ins = dve.scalar_tensor_tensor(
                            res[:, t, :], ps[4 + o % 2][:, n * P:(n + 1) * P],
                            score0[:, t, bass.ds(i * EPI + j, 1)], res[:, t, :], ALU.mult, ALU.add)
                    ins.then_inc(o_added, 1)

                for s in range(STEPS):
                    tb, ft = divmod(s % (NBLK * NF), NF)
                    M = FT[ft][1]
                    dve.wait_ge(g_made, i * STEPS + s + 1)
                    dve.wait_ge(silu_done, i * STEPS + s + 3)
                    dve.wait_ge(o_made, i * OUTS + s // NF + 1)
                    dve.tensor_tensor(hid[0:M, tb % 2, ft, :], sil[0:M, s % 2, :], ps[2 + s % 2][0:M, :],
                                      ALU.mult).then_inc(gated, 1)
                    if s % NF == 2 and s >= 5:
                        add_output((s - 5) // NF)
                    attention(s)
                    if s == 6:
                        prep(i * 2 + 1, 1)
                    if s == 14:
                        prep(i * 2 + 2, 0)
                add_output(OUTS - 1)
                assert att.n == N_ATT_DVE

            dve.wait_ge(o_added, NB * OUTS + 2)
            own.wait()
            norm_stats(1)
            dve.wait_ge(root_ready, 3)
            own(dve.reciprocal(nrm[:, 2, :], nrm[:, 1, :]))
            for t in range(NT):
                dve.tensor_scalar(xn_tok[:, t, :], res[:, t, :], mv[:, t, 0:1], nrm[:, 2, t:t + 1],
                                  ALU.subtract, ALU.mult).then_inc(tok_ready, 1)
            for b in range(NBLK):
                dve.wait_ge(u_ready, b + 1)
                own(dve.tensor_copy(blk(xn_hi, b), blk(u_t, b)))
                dve.nop().then_inc(hi_ready, 1)
                dve.tensor_tensor(blk(xn_lo, b), blk(u_t, b), blk(xn_hi, b).bitcast(F32), ALU.subtract
                                  ).then_inc(lo_ready, 1)
            dve.wait_ge(late_in, 16 * 8)
            top = rsm[:, 0, :, :]
            half_tiles = NT // 2
            for n in range(2):
                dve.wait_ge(logits_made, n + 1)
                own(dve.tensor_tensor(pair[:, n * half_tiles:(n + 1) * half_tiles, :],
                                      ps[n][:, :].rearrange("p (t e) -> p t e", e=E1),
                                      rbias[:, None, :].to_broadcast([P, half_tiles, E1]), ALU.add))
            for t in range(NT):
                dve.max(top[:, t, :], pair[:, t, :]).then_inc(dve_own, 1)
            own.n += NT
            own.wait()
            for t in range(NT):
                dve.match_replace(pair2[:, t, :], top[:, t, :], pair[:, t, :], -3.0e38).then_inc(dve_own, 1)
            own.n += NT
            own.wait()
            own(dve.tensor_tensor(pair2[:, :, :], pair[:, :, :], pair2[:, :, :], ALU.not_equal))
            own(dve.tensor_tensor(pair[:, :, :], pair[:, :, :], top[:, :, 0:1].to_broadcast([P, NT, E1]), ALU.subtract))
            dve.nop().then_inc(r1_arg, 1)
            dve.wait_ge(r1_exp, 1)
            own(dve.tensor_tensor(pair[:, :, :], pair[:, :, :], pair2[:, :, :], ALU.mult))
            own(dve.tensor_reduce(rrow[:, 0, :], pair[:, :, :], AX, ALU.add))
            own(dve.reciprocal(rrow[:, 1, :], rrow[:, 0, :]))
            own(dve.tensor_scalar(rrow[:, 1, :], rrow[:, 1, :], 0.5, None, ALU.mult))
            dve.wait_ge(turned, 3 * NBLK)
            for n in range(2):
                own(dve.tensor_tensor(xn_tok[:, :, n * E1:(n + 1) * E1], pair[:, :, :],
                                      rrow[:, 1, :, None].to_broadcast([P, NT, E1]), ALU.mult))
            dve.nop().then_inc(cw_ready, 1)
            for b in range(NBLK):
                dve.wait_ge(cw_turned, b + 1)
                dve.wait_ge(cw_copied, b + 1)
                own(dve.tensor_copy(blk(cw_hm, b), ps[b % 2][:, :]))
                own(dve.tensor_tensor(cwt[:, :], ps[b % 2][:, :], blk(cw_hm, b), ALU.subtract))
                own(dve.tensor_copy(cw_mid[:, :], cwt[:, :]))
                own(dve.tensor_tensor(cw_l[0:E1, b * TB:(b + 1) * TB], cwt[0:E1, :], cw_mid[0:E1, :], ALU.subtract))
                own(dve.tensor_copy(cw_hm[E1:P, b * TB:(b + 1) * TB], cw_mid[E1:P, :]))
                dve.nop().then_inc(cw_split, 1)
            for b in range(NBLK):
                e, l, p = softplus_bufs[b]
                mask = at["theta"]
                dve.wait_ge(sp_exp, b + 1)
                dve.wait_ge(sp_poly, b + 1)
                own(dve.tensor_scalar(mask[:, :], e[:, :], 2.0 ** -6, None, ALU.is_lt))
                own(dve.copy_predicated(l[:, :], mask[:, :].bitcast(mybir.dt.uint32), p[:, :]))
                own(dve.scalar_tensor_tensor(blk(dt_t, b), blk(dt_t, b), 0.0, l[:, :], ALU.max, ALU.add))
                own(dve.tensor_tensor(blk(win_t, b), blk(dt_t, b), blk(u_t, b), ALU.mult))
                dve.nop().then_inc(win_ready, 1)

            dve.nop().then_inc(c1_done, 2)
            dve.nop().then_inc(hid_done, 2)
            dve.nop().then_inc(scanned, RING)

            def scan(i, s):
                dve.wait_ge(decay_ready, i * GSTEPS + s + 1)
                dve.wait_ge(weighted, i * GSTEPS + s + 1)
                dve.tensor_tensor_scan(state_ring[s % RING][:, :], decay_ring[s % RING][:, :],
                                       blk(win_t, s % NBLK), 0.0, ALU.mult, ALU.add).then_inc(scanned, 1)

            def group_turn(i, last):
                for s in range(GSTEPS):
                    g = i * GPI + s // NBLK
                    c = i * GSTEPS + s
                    dve.wait_ge(tanh_done, c + 3)
                    dve.wait_ge(cwx_made, c + 1)
                    dve.wait_ge(hid_done, c + 1)
                    dve.scalar_tensor_tensor(c1_ring[s % 2], sil[:, s % 2, :], 1.0, ps[2 + s % 2][:, :],
                                             ALU.add, ALU.mult).then_inc(c1_done, 1)
                    if s + 1 < GSTEPS:
                        scan(i, s + 1)
                    elif not last:
                        scan(i + 1, 0)
                    dve.wait_ge(c1_done, c + 3)
                    dve.wait_ge(g_out, c + 1)
                    dve.scalar_tensor_tensor(hid_ring[s % 2], ps[s % 2][:, :], vec_t[:, bass.ds(g + V_B1, 1)],
                                             c1_ring[s % 2], ALU.add, ALU.mult).then_inc(hid_done, 1)

            scan(0, 0)
            with dve.Fori(0, NG // GPI - 1) as i:
                group_turn(i, False)
            group_turn(NG // GPI - 1, True)

            dve.wait_ge(g_out, NG * NBLK + 2)
            dve.wait_ge(y_done, 1)
            for b in range(NBLK):
                own(dve.scalar_tensor_tensor(blk(y_t, b), ps[4 + b][:, :], sb2_sum[:, 0:1], blk(y_t, b),
                                             ALU.add, ALU.add))
                dve.nop().then_inc(sum_ready, 1)
            for b in range(NBLK):
                dve.wait_ge(sum_turned, b + 1)
                r = res[:, b * TPB:(b + 1) * TPB, :].rearrange("p t d -> p (t d)")
                dve.tensor_tensor(r, r, ps[b][:, :], ALU.add).then_inc(x2_ready, 1)

        @block.tensor
        def _(pe):
            pe.wait_ge(consts_ready, 1)
            pe.wait_ge(turn_in, 16 * 8)
            pe.transpose(ps[7][:, 0:N_VEC], vec_raw[:, :], ident[0:N_VEC, 0:N_VEC])
            pe.transpose(ps[7][:, P:P + 3 * E0], turn_raw[0:3 * E0, 0, :], ident[0:3 * E0, 0:3 * E0])
            pe.transpose(ps[7][:, 2 * P:3 * P], turn_raw[:, 1, :], ident[:, :]).then_inc(small_turned, 1)

            def turn_tiles(src, bank, first):
                for t in range(NT):
                    pe.wait_ge(tok_ready, first + t + 1)
                    ins = pe.transpose(ps[bank + t // TPB][:, (t % TPB) * P:(t % TPB + 1) * P], src[:, t, :], ident[:, :])
                    if t % TPB == TPB - 1:
                        ins.then_inc(turned, 1)

            turn_tiles(xn_tok, 0, 0)
            pe.wait_ge(small_copied, 1)
            turn_tiles(xr_tok, 4, NT)
            pe.wait_ge(hi_ready, NBLK)
            pe.wait_ge(lo_ready, NBLK)
            for t in range(NT):
                ins = product(pe, ps[0][:, t * 3 * E0:(t + 1) * 3 * E0],
                              xn_hi[:, t * P:(t + 1) * P], xn_lo[:, t * P:(t + 1) * P],
                              turn_hi[:, 0, 0:3 * E0], turn_lo[:, 0, 0:3 * E0])
            ins.then_inc(qkv_made, 1)

            def turn_expert(j, part, base):
                if part < 2:
                    if part == 0:
                        pe.wait_ge(e_in[j], turn_expert.loads)
                    for n, (f0, m) in enumerate(FT):
                        ins = pe.transpose(ps[6 + part][:, f0:f0 + m], e_raw1[j][0:m, part * NF + n, :],
                                           ident[0:m, 0:m])
                    ins.then_inc(e_turned, 1)
                else:
                    pe.wait_ge(e_hi_ready, base * PREP_HI + 1)
                    pe.wait_ge(e_lo_ready, base * PREP_LO + 1)
                    for n, (f0, m) in enumerate(FT):
                        ins = pe.transpose(ps[6][0:m, n * P:(n + 1) * P], e_raw2[j][:, f0:f0 + m], ident[:, :])
                    ins.then_inc(e_turned, 1)

            pe.wait_ge(hi_ready, 2 * NBLK)
            pe.wait_ge(lo_ready, 2 * NBLK)
            turn_expert.loads = 80
            for part in range(3):
                turn_expert(0, part, 0)

            def hidden(i, s):
                j, r = divmod(s, NBLK * NF)
                tb, ft = divmod(r, NF)
                f0, m = FT[ft]
                if r == 0:
                    pe.wait_ge(e_hi_ready, (i * EPI + j) * PREP_HI + PREP_HI)
                    pe.wait_ge(e_lo_ready, (i * EPI + j) * PREP_LO + PREP_LO)
                pe.wait_ge(silu_done, i * STEPS + s + 1)
                product(pe, ps[s % 2][0:m, :], e_hi[j][:, f0:f0 + m], e_lo[j][:, f0:f0 + m],
                        blk(xn_hi, tb), blk(xn_lo, tb)).then_inc(a_made, 1)
                pe.wait_ge(gated, i * STEPS + s + 1)
                product(pe, ps[2 + s % 2][0:m, :], e_hi[j][:, F + f0:F + f0 + m], e_lo[j][:, F + f0:F + f0 + m],
                        blk(xn_hi, tb), blk(xn_lo, tb)).then_inc(g_made, 1)

            def output(i, o):
                j, tb = divmod(o, NBLK)
                pe.wait_ge(gated, i * STEPS + o * NF + NF + 2)
                pe.wait_ge(o_added, i * OUTS + o + 1)
                for n in range(TPB):
                    for ft, (f0, m) in enumerate(FT):
                        ins = pe.matmul(ps[4 + o % 2][:, n * P:(n + 1) * P],
                                        hid[0:m, tb % 2, ft, n * P:(n + 1) * P], e_w2[j][0:m, ft, :],
                                        start=(ft == 0), stop=(ft == NF - 1))
                ins.then_inc(o_made, 1)

            def attention(i, s):
                def project(n, bank):
                    product(pe, ps[bank][:, :], proj_hi[:, n, :], proj_lo[:, n, :],
                            xr_hi[:, bass.ds(i * TB, TB)], xr_lo[:, bass.ds(i * TB, TB)]).then_inc(att_pe, 1)

                def act_step(n):
                    pe.wait_ge(att_act, i * N_ATT_ACT + 1 + n)

                def dve_step(n):
                    pe.wait_ge(att_dve, i * N_ATT_DVE + 1 + n)

                if s == 0:
                    dve_step(0)
                    pe.wait_ge(e_hi_ready, i * 2 * PREP_HI + PREP_HI)
                    pe.wait_ge(e_lo_ready, i * 2 * PREP_LO + PREP_LO)
                    project(0, 6)
                if s == 1:
                    project(1, 7)
                if s == 2:
                    act_step(1)
                    project(2, 6)
                if s == 3:
                    dve_step(1)
                    project(3, 7)
                if s == 5:
                    act_step(3)
                    turn_expert.loads = i * 80 + 80
                    turn_expert(1, 0, i * 2 + 1)
                    turn_expert(1, 1, i * 2 + 1)
                if s == 7:
                    turn_expert(1, 2, i * 2 + 1)
                if s == 13:
                    pe.wait_ge(e_hi_ready, i * 2 * PREP_HI + 2 * PREP_HI)
                    pe.wait_ge(e_lo_ready, i * 2 * PREP_LO + 2 * PREP_LO)
                    turn_expert.loads = i * 80 + 160
                    turn_expert(0, 0, i * 2 + 2)
                    turn_expert(0, 1, i * 2 + 2)
                if s == 15:
                    turn_expert(0, 2, i * 2 + 2)
                if s == 18:
                    pe.wait_ge(e_hi_ready, i * 2 * PREP_HI + 3 * PREP_HI)
                    pe.wait_ge(e_lo_ready, i * 2 * PREP_LO + 3 * PREP_LO)
                    project(4, 6)
                if s == 19:
                    project(5, 7)
                if s == 22:
                    act_step(14)
                    dve_step(28)
                    for n in range(TPB):
                        ins = pe.matmul(ps[6][:, n * P:(n + 1) * P], at["kv"][:, n * P:(n + 1) * P], wo_sb[:, :],
                                        start=True, stop=True)
                    ins.then_inc(att_pe, 1)

            pe.wait_ge(weights_split, 1)
            pe.wait_ge(qkv_copied, 1)
            pe.nop().then_inc(o_made, 2)
            AHEAD = 2
            for s in range(AHEAD):
                hidden(0, s)

            def turn(i, last):
                for s in range(STEPS):
                    attention(i, s)
                    if s + AHEAD < STEPS:
                        hidden(i, s + AHEAD)
                    elif not last:
                        hidden(i + 1, s + AHEAD - STEPS)
                    if s % NF == NF - 1:
                        output(i, s // NF)

            with pe.Fori(0, NB - 1) as i:
                turn(i, False)
            turn(NB - 1, True)

            turn_tiles(xn_tok, 0, 2 * NT)
            for b in range(NBLK):
                pe.wait_ge(hi_ready, 2 * NBLK + b + 1)
                pe.wait_ge(lo_ready, 2 * NBLK + b + 1)
                product(pe, ps[4 + b][:, :], turn_hi[:, 1, :], turn_lo[:, 1, :], blk(xn_hi, b), blk(xn_lo, b)
                        ).then_inc(dt_made, 1)
            pe.wait_ge(weights_split, 2)
            pe.wait_ge(late_in, 16 * 8)
            for t in range(NT):
                ins = product(pe, ps[t // 8][:, (t % 8) * E1:(t % 8 + 1) * E1],
                              xn_hi[:, t * P:(t + 1) * P], xn_lo[:, t * P:(t + 1) * P], rout_hi[:, :], rout_lo[:, :])
                if t % 8 == 7:
                    ins.then_inc(logits_made, 1)

            def shared_in(c):
                k, tb = divmod(c, NBLK)
                e, n = divmod(k, HS // P)
                if c >= 2:
                    pe.wait_ge(sh_silu, c - 1)
                product(pe, ps[2 + c % 2][:, :], sw1_hi[:, e, n * P:(n + 1) * P], sw1_lo[:, e, n * P:(n + 1) * P],
                        blk(xn_hi, tb), blk(xn_lo, tb)).then_inc(sh_made, 1)

            def shared_out(c):
                k, tb = divmod(c, NBLK)
                pe.wait_ge(sh_silu, c + 1)
                if k == 0:
                    pe.wait_ge(sp_exp, tb + 1)
                pe.matmul(ps[4 + tb][:, :], sw2_sb[:, k, :], hid[:, c % 2, 2, :], start=(k == 0), stop=False,
                          skip_group_check=True).then_inc(sh_used, 1)

            shared_in(0)
            for c in range(NSH * NBLK):
                if c + 1 < NSH * NBLK:
                    shared_in(c + 1)
                shared_out(c)
            pe.wait_ge(cw_ready, 1)
            for b in range(NBLK):
                if b >= 2:
                    pe.wait_ge(cw_copied, b - 1)
                    pe.wait_ge(cw_split, b - 1)
                for n in range(TPB):
                    ins = pe.transpose(ps[b % 2][:, n * P:(n + 1) * P], xn_tok[:, b * TPB + n, :], ident[:, :])
                ins.then_inc(cw_turned, 1)
            for b in range(NBLK):
                pe.wait_ge(cw_copied, b + 1)
                pe.matmul(ps[4 + b][:, :], b2_sb[:, :], cw_b2[:, b % 2, :], start=False, stop=False,
                          skip_group_check=True).then_inc(b2_used, 1)
            pe.wait_ge(cw_split, NBLK)

            def expert_in(i, s):
                j, tb = divmod(s, NBLK)
                if tb == 0:
                    pe.wait_ge(g_split, i * GPI + j + 1)
                pe.wait_ge(hid_done, i * GSTEPS + s + 1)
                product(pe, ps[s % 2][:, :], g_hi[j][:, :], g_lo[j][:, :], blk(xn_hi, tb), blk(xn_lo, tb)
                        ).then_inc(h_made, 1)
                pe.wait_ge(c1_done, i * GSTEPS + s + 1)
                w = sel[:, bass.ds((i * GPI + j) * P, P)]
                pe.matmul(ps[2 + s % 2][:, :], w, blk(cw_hm, tb), start=True, stop=False)
                pe.matmul(ps[2 + s % 2][:, :], w, blk(cw_l, tb), start=False, stop=True).then_inc(cwx_made, 1)

            def expert_out(i, s, last):
                j, tb = divmod(s, NBLK)
                if tb == 0:
                    pe.wait_ge(g_w2_in[j], i * 16 + 16)
                pe.wait_ge(hid_done, i * GSTEPS + s + 3)
                pe.matmul(ps[4 + tb][:, :], g_w2[j][:, :], hid_ring[s % 2], start=False,
                          stop=last and j == GPI - 1, skip_group_check=True).then_inc(g_out, 1)

            pe.nop().then_inc(g_out, 2)
            expert_in(0, 0)
            expert_in(0, 1)

            def group_turn(i, last):
                for s in range(GSTEPS):
                    if s + 2 < GSTEPS:
                        expert_in(i, s + 2)
                    elif not last:
                        expert_in(i + 1, s + 2 - GSTEPS)
                    expert_out(i, s, last)

            with pe.Fori(0, NG // GPI - 1) as i:
                group_turn(i, False)
            group_turn(NG // GPI - 1, True)
            for b in range(NBLK):
                pe.wait_ge(sum_ready, b + 1)
                for n in range(TPB):
                    ins = pe.transpose(ps[b][:, n * P:(n + 1) * P], y_t[:, b * TB + n * P:b * TB + (n + 1) * P],
                                       ident[:, :])
                ins.then_inc(sum_turned, 1)


_INS = ['L0_attn_x', 'L0_attn_wq', 'L0_attn_wk', 'L0_attn_wv', 'L0_attn_wa', 'L0_attn_wg', 'L0_attn_wo',
        'L0_attn_rms_scale', 'L0_ffn_wqkv', 'L0_ffn_w1', 'L0_ffn_w2', 'L1_attn_A_log', 'L1_attn_B_mat',
        'L1_attn_C_mat', 'L1_attn_D_vec', 'L1_attn_W_dt', 'L1_attn_b_dt', 'L1_ffn_router_w', 'L1_ffn_router_b',
        'L1_ffn_w1', 'L1_ffn_b1', 'L1_ffn_w2', 'L1_ffn_b2', 'L1_ffn_sw1', 'L1_ffn_sb1', 'L1_ffn_sw2',
        'L1_ffn_sb2']


def kernel(**inputs):
    import numpy as _np
    import concourse.bacc as _bacc
    from concourse import mybir as _mybir
    from concourse.bass_utils import run_bass_kernel_spmd as _run

    nc = _bacc.Bacc("TRN2", target_bir_lowering=False, num_devices=1)
    arrays, args = {}, []
    for name in _INS:
        a = _np.ascontiguousarray(inputs[name])
        arrays[f"in_{name}"] = a
        args.append(nc.dram_tensor(f"in_{name}", a.shape, _mybir.dt.from_np(a.dtype), kind="ExternalInput").ap())
    x = arrays["in_L0_attn_x"]
    args.append(nc.dram_tensor("out_0", x.shape, _mybir.dt.from_np(x.dtype), kind="ExternalOutput").ap())
    program(nc, *args)
    r = _run(nc, [arrays], core_ids=[0])
    return r.results[0]["out_0"]
```

```python
import math
from contextlib import ExitStack

import concourse.bass as bass
from concourse import mybir

ALU = mybir.AluOpType
ACT = mybir.ActivationFunctionType
AX = mybir.AxisListType.X
F32 = mybir.dt.float32
F32R = mybir.dt.float32r
BF16 = mybir.dt.bfloat16

P = 128
TB = 512
ROUND_TURN = 1.5 * 2.0 ** 10
ROUND_INT = 1.5 * 2.0 ** 23

V_RMS, V_D, V_BDT, V_SB2, V_SB1, V_B1 = 0, 1, 2, 3, 5, 9
N_VEC = 25


class Chain:

    def __init__(self, eng, sem, at=0):
        self.eng, self.sem, self.base, self.n = eng, sem, at, 0

    def __call__(self, ins):
        ins.then_inc(self.sem, 1)
        self.n += 1
        self.wait()

    def wait(self):
        self.eng.wait_ge(self.sem, self.base + self.n)


def program(nc, x, wq, wk, wv, wa, wg, wo, rms_scale, wqkv, w1, w2, A_log, B_mat, C_mat, D_vec, W_dt, b_dt,
            router_w, router_b, rw1, rb1, rw2, rb2, sw1, sb1, sw2, sb2, out):
    NB, T, D = x.shape
    NTOK = NB * T
    NT = NTOK // P
    TPB = TB // P
    E0, F2, _ = w1.shape
    F = F2 // 2
    FT = [(s, min(P, F - s)) for s in range(0, F, P)]
    NF = len(FT)
    E1, _, H1 = rw1.shape
    GE = P // H1
    NG = E1 // GE
    NS = A_log.shape[1]
    ES, _, HS = sw1.shape
    NSH = ES * HS // P
    LN_EPS, RMS_EPS = 1e-5, 1e-6
    assert D == P and T == TB and NS == NG and E0 == 2 * NB and NF == 3

    x_v = x.rearrange("b (c p) d -> p (b c) d", p=P)
    out_v = out.rearrange("b (c p) d -> p (b c) d", p=P)

    def row(a):
        return a.rearrange("(a d) -> a d", a=1)

    with ExitStack() as ctx:
        def sb(name, shape, dt=F32):
            return ctx.enter_context(nc.sbuf_tensor(name, shape, dt))

        def sem(name):
            return ctx.enter_context(nc.semaphore(name))

        ident = sb("ident", [P, P])
        sel = sb("sel", [P, NG * P], BF16)
        earlier = sb("earlier", [P, E0, E0])
        ones = sb("ones", [P, TB])
        half_pi = sb("half_pi", [P, 1])
        proj_raw = sb("proj_raw", [P, 6, P])
        proj_hi = sb("proj_hi", [P, 6, P], F32R)
        proj_lo = sb("proj_lo", [P, 6, P], F32R)
        wo_sb = sb("wo_sb", [P, P])
        turn_raw = sb("turn_raw", [P, 2, P])
        turn_hi = sb("turn_hi", [P, 2, P], F32R)
        turn_lo = sb("turn_lo", [P, 2, P], F32R)
        rout_raw = sb("rout_raw", [P, E1])
        rout_hi = sb("rout_hi", [P, E1], F32R)
        rout_lo = sb("rout_lo", [P, E1], F32R)
        rbias = sb("rbias", [P, E1])
        sw1_raw = sb("sw1_raw", [P, ES, HS])
        sw1_hi = sb("sw1_hi", [P, ES, HS], F32R)
        sw1_lo = sb("sw1_lo", [P, ES, HS], F32R)
        sw2_sb = sb("sw2_sb", [P, NSH, P])
        b2_sb = sb("b2_sb", [E1, P])
        vec_raw = sb("vec_raw", [N_VEC, P])
        vec_t = sb("vec_t", [P, N_VEC])
        b1_half = sb("b1_half", [P, NG])
        sb2_sum = sb("sb2_sum", [P, 1])
        ssm_raw = sb("ssm_raw", [P, 3, NS])
        ssm_a = sb("ssm_a", [P, NS])
        ssm_cb = sb("ssm_cb", [P, NS])

        res = sb("res", [P, NT, P])
        xn_tok = sb("xn_tok", [P, NT, P])
        xr_tok = sb("xr_tok", [P, NT, P])
        xn_hi = sb("xn_hi", [P, NTOK], F32R)
        xn_lo = sb("xn_lo", [P, NTOK], F32R)
        xr_hi = sb("xr_hi", [P, NTOK], F32R)
        xr_lo = sb("xr_lo", [P, NTOK], F32R)
        stats = sb("stats", [P, NT, 6])
        mv = sb("mv", [P, NT, 2])
        nrm = sb("nrm", [P, 6, NT])
        qkv = sb("qkv", [P, NT, 3 * E0])
        pair = sb("pair", [P, NT, E0 * E0])
        pair2 = sb("pair2", [P, NT, E0 * E0])
        rsm = sb("rsm", [P, 4, NT, E0])
        rrow = sb("rrow", [P, 3, NT])
        score0 = sb("score0", [P, NT, E0])
        e_raw1 = [sb(f"e_raw1_{j}", [P, 2 * NF, P]) for j in range(2)]
        e_raw2 = [sb(f"e_raw2_{j}", [P, F]) for j in range(2)]
        e_hi = [sb(f"e_hi_{j}", [P, F2], F32R) for j in range(2)]
        e_lo = [sb(f"e_lo_{j}", [P, F2], F32R) for j in range(2)]
        e_w2 = [sb(f"e_w2_{j}", [P, NF, P]) for j in range(2)]
        e_t = [sb(f"e_t_{j}", [P, F2]) for j in range(2)]
        e_w2_t = [sb(f"e_w2_t_{j}", [P, NF, P]) for j in range(2)]
        sil = sb("sil", [P, 2, TB])
        hid = sb("hid", [P, 2, NF, TB])
        at = {n: sb(f"at_{n}", [P, TB]) for n in (
            "k", "kv", "ar", "ai", "sq", "m2", "mag", "decay", "theta", "neg", "q", "s0", "s1")}
        u_t = xr_tok[:].rearrange("p a b -> p (a b)")
        y_t = xn_tok[:].rearrange("p a b -> p (a b)")
        dt_t = sb("dt_t", [P, NTOK])
        win_t = sb("win_t", [P, NTOK])
        cwt = sb("cwt", [P, TB])
        cw_b2 = sb("cw_b2", [E1, 2, TB])
        cw_hm = sb("cw_hm", [P, NTOK], BF16)
        cw_l = sb("cw_l", [P, NTOK], BF16)
        cw_mid = sb("cw_mid", [P, TB], BF16)
        g_raw1 = [sb(f"g_raw1_{j}", [P, GE, H1]) for j in range(2)]
        g_hi = [sb(f"g_hi_{j}", [P, P], F32R) for j in range(2)]
        g_lo = [sb(f"g_lo_{j}", [P, P], F32R) for j in range(2)]
        g_w2 = [sb(f"g_w2_{j}", [P, P]) for j in range(2)]

        psum = ctx.enter_context(nc.psum_tensor("psum", [P, 8, TB], F32))
        ps = [psum[:, n, :] for n in range(8)]

        x_in = [sem(f"x_in{b}") for b in range(NB)]
        turn_in, proj_in, late_in = sem("turn_in"), sem("proj_in"), sem("late_in")
        e_in = [sem(f"e_in{j}") for j in range(2)]
        g_in = [sem(f"g_in{j}") for j in range(2)]
        g_w2_in = [sem(f"g_w2_in{j}") for j in range(2)]
        dve_own, act_own, pool_own = sem("dve_own"), sem("act_own"), sem("pool_own")
        out_done = sem("out_done")
        consts_ready = sem("consts_ready")
        var_ready, root_ready = sem("var_ready"), sem("root_ready")
        tok_ready = sem("tok_ready")
        small_turned, small_copied = sem("small_turned"), sem("small_copied")
        weights_split = sem("weights_split")
        turned, hi_ready, lo_ready = sem("turned"), sem("hi_ready"), sem("lo_ready")
        qkv_made, qkv_copied = sem("qkv_made"), sem("qkv_copied")
        r0_arg, r0_exp = sem("r0_arg"), sem("r0_exp")
        e_turned, e_copied, e_split, w2_ready = sem("e_turned"), sem("e_copied"), sem("e_split"), sem("w2_ready")
        a_made, g_made, silu_done, gated = sem("a_made"), sem("g_made"), sem("silu_done"), sem("gated")
        o_made, o_added = sem("o_made"), sem("o_added")
        att_pe, att_act, att_dve = sem("att_pe"), sem("att_act"), sem("att_dve")
        dt_made, dt_left, sp_exp, sp_log = sem("dt_made"), sem("dt_left"), sem("sp_exp"), sem("sp_log")
        sp_poly, win_ready = sem("sp_poly"), sem("win_ready")
        logits_made, r1_arg, r1_exp = sem("logits_made"), sem("r1_arg"), sem("r1_exp")
        cw_ready, cw_turned, cw_copied, cw_split = sem("cw_ready"), sem("cw_turned"), sem("cw_copied"), sem("cw_split")
        sh_made, sh_silu, sh_used, b2_used = sem("sh_made"), sem("sh_silu"), sem("sh_used"), sem("b2_used")
        g_split, h_made, cwx_made = sem("g_split"), sem("h_made"), sem("cwx_made")
        tanh_done, c1_done, hid_done, g_out = sem("tanh_done"), sem("c1_done"), sem("hid_done"), sem("g_out")
        decay_ready, scanned, weighted, y_added = sem("decay_ready"), sem("scanned"), sem("weighted"), sem("y_added")
        y_done, sum_ready, sum_turned, x2_ready = (
            sem("y_done"), sem("sum_ready"), sem("sum_turned"), sem("x2_ready"))

        def product(pe, acc, w_hi, w_lo, m_hi, m_lo):
            pe.matmul(acc, w_hi, m_hi, start=True, stop=False)
            pe.matmul(acc, w_lo, m_hi, start=False, stop=False)
            return pe.matmul(acc, w_hi, m_lo, start=False, stop=True)

        def blk(buf, b):
            return buf[:, b * TB:(b + 1) * TB]

        act_passed, pool_passed = sem("act_passed"), sem("pool_passed")

        NBLK = NB
        EPI = 2
        STEPS = EPI * NBLK * NF
        OUTS = EPI * NBLK
        N_ATT_PE, N_ATT_ACT, N_ATT_DVE = 7, 15, 29
        CW_STEPS = (3, 4, 7, 8)
        GPI = 2
        GSTEPS = GPI * NBLK
        hid_ring = [hid[:, r, 0, :] for r in range(2)]
        c1_ring = [hid[:, r, 1, :] for r in range(2)]
        RING = 4
        decay_ring = [at[n] for n in ("k", "kv", "m2", "mag")]
        state_ring = [at[n] for n in ("ar", "ai", "decay", "theta")]
        term_ring = [at[n] for n in ("sq", "neg")]
        softplus_bufs = [[at[n] for n in names] for names in (
            ("s0", "s1", "q"), ("m2", "decay", "mag"), ("k", "kv", "ar"), ("ai", "neg", "sq"))]

        A = {n: a[:, :] for n, a in at.items()}

        block = ctx.enter_context(nc.Block())

        @block.sync
        def _(sp):
            def load_expert(e, j):
                for half in range(2):
                    r0 = half * F
                    sp.dma_start(e_raw1[j][:, half * NF:half * NF + 2, :],
                                 w1[e, r0:r0 + 2 * P, :].rearrange("... (c p) d -> ... p c d", p=P)
                                 ).then_inc(e_in[j], 16)
                    sp.dma_start(e_raw1[j][0:FT[2][1], half * NF + 2, :],
                                 w1[e, r0 + 2 * P:r0 + F, :]).then_inc(e_in[j], 16)
                sp.dma_start(e_raw2[j][:, :], w2[e, :, :]).then_inc(e_in[j], 16)

            def load_group(g, j):
                load_group_w1(g, j)
                load_group_w2(g, j)

            def load_group_w1(g, j):
                sp.dma_start(g_raw1[j][:, :, :], rw1[bass.ds(g * GE, GE), :, :].rearrange("e d h -> d e h")
                             ).then_inc(g_in[j], 16)

            def load_group_w2(g, j):
                sp.dma_start(g_w2[j][:, :], rw2[bass.ds(g * GE, GE), :, :].rearrange("e h d -> (e h) d")
                             ).then_inc(g_w2_in[j], 16)

            for b in range(NB):
                sp.dma_start(res[:, b * TPB:(b + 1) * TPB, :], x_v[:, b * TPB:(b + 1) * TPB, :]).then_inc(x_in[b], 16)
            sp.dma_start(turn_raw[0:3 * E0, 0, :], wqkv).then_inc(turn_in, 16)
            sp.dma_start(turn_raw[:, 1, :], W_dt).then_inc(turn_in, 16)
            sp.dma_start(vec_raw[V_RMS:V_RMS + 1, :], row(rms_scale)).then_inc(turn_in, 16)
            sp.dma_start(vec_raw[V_D:V_D + 1, :], row(D_vec)).then_inc(turn_in, 16)
            sp.dma_start(vec_raw[V_BDT:V_BDT + 1, :], row(b_dt)).then_inc(turn_in, 16)
            sp.dma_start(vec_raw[V_SB2:V_SB2 + ES, :], sb2).then_inc(turn_in, 16)
            sp.dma_start(vec_raw[V_SB1:V_SB1 + NSH, :], sb1.rearrange("e (c h) -> (e c) h", h=P)
                         ).then_inc(turn_in, 16)
            sp.dma_start(vec_raw[V_B1:V_B1 + NG, :], rb1.rearrange("(g e) h -> g (e h)", e=GE)
                         ).then_inc(turn_in, 16)
            load_expert(0, 0)
            for n, w in enumerate((wk, wv, None, None, wg, wq)):
                if w is not None:
                    sp.dma_start(proj_raw[:, n, :], w).then_inc(proj_in, 16)
            sp.dma_start(proj_raw[:, 2:4, :], wa.rearrange("d (c h) -> d c h", h=P)).then_inc(proj_in, 16)
            sp.dma_start(wo_sb[:, :], wo).then_inc(proj_in, 16)
            load_expert(1, 1)
            sp.dma_start(rout_raw[:, :], router_w).then_inc(late_in, 16)
            sp.dma_start(rbias[:, :], row(router_b).to_broadcast([P, E1])).then_inc(late_in, 16)
            sp.dma_start(sw1_raw[:, :, :], sw1.rearrange("e d h -> d e h")).then_inc(late_in, 16)
            sp.dma_start(sw2_sb[:, :, :], sw2.rearrange("e (c h) d -> h (e c) d", h=P)).then_inc(late_in, 16)
            sp.dma_start(b2_sb[:, :], rb2).then_inc(late_in, 16)
            for n, w in enumerate((A_log, B_mat, C_mat)):
                sp.dma_start(ssm_raw[:, n, :], w).then_inc(late_in, 16)
            load_group(0, 0)
            load_group(1, 1)
            with sp.Fori(0, NB - 1) as i:
                for j in range(EPI):
                    sp.wait_ge(e_turned, i * 2 * EPI + 2 * j + 2)
                    load_expert(i * EPI + EPI + j, j)
            with sp.Fori(0, NG // GPI - 1) as i:
                for j in range(GPI):
                    sp.wait_ge(g_split, i * GPI + j + 1)
                    load_group_w1(i * GPI + GPI + j, j)
                for j in range(GPI):
                    sp.wait_ge(g_out, i * GSTEPS + (j + 1) * NBLK + 2)
                    load_group_w2(i * GPI + GPI + j, j)
            for b in range(NB):
                sp.wait_ge(x2_ready, b + 1)
                sp.dma_start(out_v[:, b * TPB:(b + 1) * TPB, :], res[:, b * TPB:(b + 1) * TPB, :]
                             ).then_inc(out_done, 16)
            sp.wait_ge(out_done, 16 * NB)

        @block.gpsimd
        def _(pool):
            own = Chain(pool, pool_own)
            own(pool.memset(ident[:, :], 0.0))
            own(pool.affine_select(out=ident[:, :], in_=ident[:, :], compare_op=ALU.not_equal, fill=1.0,
                                   base=0, pattern=[[-1, P]], channel_multiplier=1))
            pool.nop().then_inc(consts_ready, 1)
            own(pool.memset(earlier[:, :, :], 0.0))
            own(pool.affine_select(out=earlier[:, :, :], in_=earlier[:, :, :], compare_op=ALU.is_ge, fill=1.0,
                                   base=0, pattern=[[-1, E0], [1, E0]], channel_multiplier=0))
            own(pool.memset(ones[:, :], 1.0))
            own(pool.memset(half_pi[:, :], math.pi / 2))
            for j in range(EPI):
                own(pool.memset(e_w2_t[j][:, :, :], 0.0))
            pool.nop().then_inc(consts_ready, 1)

            def split(src, hi, lo):
                own(pool.tensor_scalar(hi, src, 1.0, 0.0, ALU.mult, ALU.add))
                own(pool.tensor_tensor(lo, src, hi.bitcast(F32), ALU.subtract))

            pool.wait_ge(proj_in, 16 * 6)
            split(proj_raw[:, :, :], proj_hi[:, :, :], proj_lo[:, :, :])
            pool.nop().then_inc(weights_split, 1)
            def expert_w1(j):
                split(e_t[j][:, :], e_hi[j][:, :], e_lo[j][:, :])
                pool.nop().then_inc(e_split, 1)

            def expert_w2(j):
                own(pool.tensor_scalar(e_w2[j][:, :, :], e_w2_t[j][:, :, :], 1.0, 0.0, ALU.mult, ALU.add))
                pool.nop().then_inc(w2_ready, 1)

            for j in range(EPI):
                pool.wait_ge(e_copied, 2 * j + 2)
                expert_w1(j)
                expert_w2(j)
            own(pool.memset(sel[:, :], 0.0))
            sel_v = sel[:, :].rearrange("p (c h) -> p c h", h=H1)
            for first in (0, E1):
                own(pool.affine_select(out=sel_v, in_=sel_v, compare_op=ALU.not_equal, fill=1.0,
                                       base=-first, pattern=[[-1, E1], [0, H1]], channel_multiplier=1))
            own(pool.memset(cw_l[:, :], 0.0))
            pool.wait_ge(late_in, 16 * 8)
            split(rout_raw[:, :], rout_hi[:, :], rout_lo[:, :])
            split(sw1_raw[:, :, :], sw1_hi[:, :, :], sw1_lo[:, :, :])
            own(pool.tensor_tensor(ssm_cb[:, :], ssm_raw[:, 1, :], ssm_raw[:, 2, :], ALU.mult))
            pool.nop().then_inc(weights_split, 1)

            def split_group(j):
                split(g_raw1[j][:, :, :].rearrange("p e h -> p (e h)"), g_hi[j][:, :], g_lo[j][:, :])
                pool.nop().then_inc(g_split, 1)

            for j in range(GPI):
                pool.wait_ge(g_in[j], 16)
                split_group(j)

            n0 = own.n
            with pool.Fori(0, NB - 1) as i:
                own = Chain(pool, pool_own, i * 3 * EPI + n0)
                for j in range(EPI):
                    pool.wait_ge(e_copied, i * 2 * EPI + 2 * EPI + 2 * j + 1)
                    pool.wait_ge(g_made, i * STEPS + (j + 1) * NBLK * NF)
                    pool.nop().then_inc(pool_passed, 1)
                    expert_w1(j)
                    pool.wait_ge(e_copied, i * 2 * EPI + 2 * EPI + 2 * j + 2)
                    pool.wait_ge(o_made, i * OUTS + (j + 1) * NBLK + 2)
                    pool.nop().then_inc(pool_passed, 1)
                    expert_w2(j)
            own = Chain(pool, pool_own, n0 + (NB - 1) * 3 * EPI)

            for b in range(NBLK):
                pool.wait_ge(sp_exp, b + 1)
                e, _, p = softplus_bufs[b]
                own(pool.tensor_scalar(p[:, :], e[:, :], -1.0 / 4, 1.0 / 3, ALU.mult, ALU.add))
                own(pool.tensor_tensor(p[:, :], p[:, :], e[:, :], ALU.mult))
                own(pool.tensor_scalar(p[:, :], p[:, :], 1.0, -1.0 / 2, ALU.mult, ALU.add))
                own(pool.tensor_tensor(p[:, :], p[:, :], e[:, :], ALU.mult))
                own(pool.tensor_scalar(p[:, :], p[:, :], 1.0, 1.0, ALU.mult, ALU.add))
                own(pool.tensor_tensor(p[:, :], p[:, :], e[:, :], ALU.mult))
                pool.nop().then_inc(sp_poly, 1)
            pool.wait_ge(cw_turned, NBLK)
            own(pool.tensor_scalar(y_t, u_t, vec_t[:, V_D:V_D + 1], 0.0, ALU.mult, ALU.add))

            n0 = own.base + own.n

            def turn(i, last):
                own = Chain(pool, pool_own, i * (GSTEPS + 2 * GPI) + n0)
                for s in range(GSTEPS):
                    j, tb = divmod(s, NBLK)
                    pool.wait_ge(weighted, i * GSTEPS + s + 1 + RING)
                    pool.nop().then_inc(pool_passed, 1)
                    own(pool.tensor_tensor(blk(y_t, tb), blk(y_t, tb), term_ring[s % 2][:, :], ALU.add))
                    pool.nop().then_inc(y_added, 1)
                    if s % NBLK == NBLK - 1 and not last:
                        pool.wait_ge(g_in[j], i * 16 + 32)
                        pool.wait_ge(h_made, i * GSTEPS + (j + 1) * NBLK)
                        own_split(own, j)

            def own_split(own, j):
                src = g_raw1[j][:, :, :].rearrange("p e h -> p (e h)")
                pool.nop().then_inc(pool_passed, 1)
                own(pool.tensor_scalar(g_hi[j][:, :], src, 1.0, 0.0, ALU.mult, ALU.add))
                own(pool.tensor_tensor(g_lo[j][:, :], src, g_hi[j][:, :].bitcast(F32), ALU.subtract))
                pool.nop().then_inc(g_split, 1)

            pool.nop().then_inc(y_added, 2)
            with pool.Fori(0, NG // GPI - 1) as i:
                turn(i, False)
            turn(NG // GPI - 1, True)
            pool.nop().then_inc(y_done, 1)

        @block.scalar
        def _(act):
            act.wait_ge(var_ready, 1)
            act.activation(nrm[:, 1, :], nrm[:, 0, :], ACT.Sqrt).then_inc(root_ready, 1)
            act.wait_ge(var_ready, 2)
            act.activation(nrm[:, 4, :], nrm[:, 3, :], ACT.Sqrt).then_inc(root_ready, 1)
            for b in range(NBLK):
                act.wait_ge(turned, b + 1)
                act.activation(blk(xn_hi, b), ps[b][:, :], ACT.Copy).then_inc(hi_ready, 1)

            def copy_w1(j, before):
                act.wait_ge(e_turned, before + 1)
                own(act.activation(e_t[j][:, :].rearrange("p (n f) -> p n f", f=F), psum[:, 6:8, 0:F], ACT.Copy))
                act.nop().then_inc(e_copied, 1)

            def copy_w2(j, before, bank):
                act.wait_ge(e_turned, before + 2)
                own(act.activation(e_w2_t[j][:, 0:2, :], ps[bank][:, 0:2 * P].rearrange("p (c d) -> p c d", d=P),
                                   ACT.Copy))
                own(act.activation(e_w2_t[j][0:FT[2][1], 2, :], ps[bank][0:FT[2][1], 2 * P:3 * P], ACT.Copy))
                act.nop().then_inc(e_copied, 1)

            own = Chain(act, act_own)
            act.wait_ge(consts_ready, 2)
            for j in range(EPI):
                copy_w1(j, 2 * j)
                copy_w2(j, 2 * j, 4 + j)
            act.wait_ge(r0_arg, 1)
            act.activation(pair[:, :, :], pair[:, :, :], ACT.Exp).then_inc(r0_exp, 1)
            for b in range(NBLK):
                act.wait_ge(turned, NBLK + b + 1)
                act.activation(blk(xr_hi, b), ps[4 + b][:, :], ACT.Identity,
                               scale=vec_t[:, V_RMS:V_RMS + 1]).then_inc(hi_ready, 1)
            act.wait_ge(r0_arg, 2)
            act.activation(rsm[:, 1, :, :], rsm[:, 1, :, :], ACT.Exp).then_inc(r0_exp, 1)

            act.nop().then_inc(silu_done, 2)
            act.nop().then_inc(att_act, 1)
            n0 = own.n

            def turn(i, last):
                nonlocal own
                att = Chain(act, att_act, i * N_ATT_ACT + 1)
                own = Chain(act, act_own, i * 3 * EPI + n0)

                def pe_step(n):
                    act.wait_ge(att_pe, i * N_ATT_PE + n)

                def dve_step(n):
                    act.wait_ge(att_dve, i * N_ATT_DVE + 1 + n)

                def attention(s):
                    if s == 2:
                        pe_step(2)
                        att(act.activation(A["k"], ps[6][:, :], ACT.Copy))
                    if s == 5:
                        pe_step(3)
                        att(act.activation(A["ar"], ps[6][:, :], ACT.Copy))
                        att(act.activation(A["sq"], A["ar"], ACT.Square))
                    if s == 6:
                        pe_step(4)
                        att(act.activation(A["ai"], ps[7][:, :], ACT.Copy))
                        att(act.activation(A["m2"], A["ai"], ACT.Square))
                        att(act.activation(A["neg"], A["ar"], ACT.Abs))
                    if s == 8:
                        pe_step(5)
                        dve_step(3)
                        att(act.activation(A["sq"], ps[6][:, :], ACT.Silu))
                        att(act.activation(A["mag"], A["m2"], ACT.Sqrt))
                    if s == 9:
                        pe_step(6)
                        att(act.activation(A["q"], ps[7][:, :], ACT.Copy))
                    if s == 11:
                        dve_step(6)
                        att(act.activation(A["decay"], A["mag"], ACT.Sigmoid))
                        att(act.activation(A["theta"], A["k"], ACT.Arctan))
                    if s == 16:
                        dve_step(18)
                        att(act.activation(A["m2"], A["theta"], ACT.Abs))
                        att(act.activation(A["mag"], A["theta"], ACT.Sin, scale=math.pi))
                        att(act.activation(A["k"], A["m2"], ACT.Sin, scale=-math.pi, bias=half_pi[:, 0:1]))
                        att(act.activation(A["theta"], A["mag"], ACT.Square))

                for s in range(STEPS):
                    M = FT[s % NF][1]
                    act.wait_ge(a_made, i * STEPS + s + 1)
                    act.wait_ge(gated, i * STEPS + s + 1)
                    act.activation(sil[0:M, s % 2, :], ps[s % 2][0:M, :], ACT.Silu).then_inc(silu_done, 1)
                    attention(s)
                    if last:
                        continue
                    copied = (i + 1) * 2 * EPI
                    if s == 12:
                        act.wait_ge(e_split, i * EPI + 1)
                        copy_w1(0, copied)
                    if s == 15:
                        act.wait_ge(w2_ready, i * EPI + 1)
                        copy_w2(0, copied, 6)
                    if s == 18:
                        act.wait_ge(e_split, i * EPI + 2)
                        copy_w1(1, copied + 2)
                    if s == 21:
                        act.wait_ge(w2_ready, i * EPI + 2)
                        copy_w2(1, copied + 2, 7)
                assert att.n == N_ATT_ACT

            with act.Fori(0, NB - 1) as i:
                turn(i, False)
            turn(NB - 1, True)
            own = Chain(act, act_own, n0 + (NB - 1) * 3 * EPI)

            act.wait_ge(late_in, 16 * 8)
            act.wait_ge(var_ready, 3)
            act.activation(nrm[:, 1, :], nrm[:, 0, :], ACT.Sqrt).then_inc(root_ready, 1)
            for b in range(NBLK):
                act.wait_ge(turned, 2 * NBLK + b + 1)
                own(act.activation(blk(u_t, b), ps[b][:, :], ACT.Copy))
                act.activation(blk(xn_hi, b), blk(u_t, b), ACT.Copy).then_inc(hi_ready, 1)
            own(act.activation(ssm_a[:, :], ssm_raw[:, 0, :], ACT.Exp))
            own(act.activation(ssm_a[:, :], ssm_a[:, :], ACT.Copy, scale=-1.0))
            own(act.activation(b1_half[:, :], vec_t[:, V_B1:V_B1 + NG], ACT.Copy, scale=0.5))
            for b in range(NBLK):
                act.wait_ge(dt_made, b + 1)
                own(act.activation(blk(dt_t, b), ps[4 + b][:, :], ACT.Identity, bias=vec_t[:, V_BDT:V_BDT + 1]))
                act.nop().then_inc(dt_left, 1)
            for b in range(NBLK):
                e = softplus_bufs[b][0]
                own(act.activation(e[:, :], blk(dt_t, b), ACT.Abs))
                own(act.activation(e[:, :], e[:, :], ACT.Exp, scale=-1.0))
                act.nop().then_inc(sp_exp, 1)
            for b in range(NBLK):
                e, l, _ = softplus_bufs[b]
                act.activation(l[:, :], e[:, :], ACT.Ln, bias=1.0).then_inc(sp_log, 1)
            act.wait_ge(r1_arg, 1)
            act.activation(pair[:, :, :], pair[:, :, :], ACT.Exp).then_inc(r1_exp, 1)

            def copy_cw(b):
                act.wait_ge(cw_turned, b + 1)
                if b >= 2:
                    act.wait_ge(b2_used, b - 1)
                act.activation(cw_b2[:, b % 2, :], ps[b % 2][0:E1, :], ACT.Copy, scale=2.0).then_inc(cw_copied, 1)

            for c in range(NSH * NBLK):
                k, tb = divmod(c, NBLK)
                for b, at_step in enumerate(CW_STEPS):
                    if c == at_step:
                        copy_cw(b)
                act.wait_ge(sh_made, c + 1)
                if c >= 2:
                    act.wait_ge(sh_used, c - 1)
                act.activation(hid[:, c % 2, 2, :], ps[2 + c % 2][:, :], ACT.Silu,
                               bias=vec_t[:, V_SB1 + k:V_SB1 + k + 1]).then_inc(sh_silu, 1)

            act.activation(nrm[:, 5, 0:1], nrm[:, 0, 0:1], ACT.Exp)
            act.nop().then_inc(tanh_done, 2)
            act.nop().then_inc(weighted, RING)

            def decay(i, s):
                act.wait_ge(scanned, i * GSTEPS + s + 1)
                act.nop().then_inc(act_passed, 1)
                act.activation(decay_ring[s % RING][:, :], blk(dt_t, s % NBLK), ACT.Exp,
                               scale=ssm_a[:, bass.ds(i * GPI + s // NBLK, 1)]).then_inc(decay_ready, 1)

            def group_turn(i, last):
                for s in range(GSTEPS):
                    g = i * GPI + s // NBLK
                    act.wait_ge(h_made, i * GSTEPS + s + 1)
                    act.wait_ge(c1_done, i * GSTEPS + s + 1)
                    act.nop().then_inc(act_passed, 1)
                    act.activation(sil[:, s % 2, :], ps[s % 2][:, :], ACT.Tanh, scale=0.5,
                                   bias=b1_half[:, bass.ds(g, 1)]).then_inc(tanh_done, 1)
                    if s + 2 < GSTEPS:
                        decay(i, s + 2)
                    elif not last:
                        decay(i + 1, s + 2 - GSTEPS)
                    act.wait_ge(scanned, i * GSTEPS + s + 1 + RING)
                    act.wait_ge(y_added, i * GSTEPS + s + 1)
                    act.nop().then_inc(act_passed, 1)
                    act.activation(term_ring[s % 2][:, :], state_ring[s % RING][:, :], ACT.Copy,
                                   scale=ssm_cb[:, bass.ds(g, 1)]).then_inc(weighted, 1)

            act.wait_ge(win_ready, NBLK)
            for s in range(2):
                decay(0, s)
            with act.Fori(0, NG // GPI - 1) as i:
                group_turn(i, False)
            group_turn(NG // GPI - 1, True)

        @block.vector
        def _(dve):
            own = Chain(dve, dve_own)

            def norm_stats(layer):
                for t in range(NT):
                    if layer == 0 and t % TPB == 0:
                        dve.wait_ge(x_in[t // TPB], 16)
                    dve.bn_stats(stats[:, t, :], res[:, t, :]).then_inc(dve_own, 1)
                own.n += NT
                own.wait()
                for t in range(NT):
                    dve.bn_aggr(mv[:, t, :], stats[:, t, :]).then_inc(dve_own, 1)
                own.n += NT
                own.wait()
                own(dve.tensor_scalar(nrm[:, 0, :], mv[:, :, 1], LN_EPS, None, ALU.add))
                dve.nop().then_inc(var_ready, 1)

            norm_stats(0)
            dve.wait_ge(small_turned, 1)
            own(dve.tensor_copy(vec_t[:, :], ps[7][:, 0:N_VEC]))
            own(dve.tensor_copy(turn_hi[:, 0, 0:3 * E0], ps[7][:, P:P + 3 * E0]))
            own(dve.tensor_copy(turn_hi[:, 1, :], ps[7][:, 2 * P:3 * P]))
            own(dve.tensor_tensor(turn_lo[:, 0, 0:3 * E0], ps[7][:, P:P + 3 * E0],
                                  turn_hi[:, 0, 0:3 * E0].bitcast(F32), ALU.subtract))
            own(dve.tensor_tensor(turn_lo[:, 1, :], ps[7][:, 2 * P:3 * P], turn_hi[:, 1, :].bitcast(F32),
                                  ALU.subtract))
            own(dve.tensor_tensor(sb2_sum[:, :], vec_t[:, V_SB2:V_SB2 + 1], vec_t[:, V_SB2 + 1:V_SB2 + 2], ALU.add))
            dve.nop().then_inc(small_copied, 1)
            dve.wait_ge(root_ready, 1)
            own(dve.reciprocal(nrm[:, 2, :], nrm[:, 1, :]))
            own(dve.tensor_tensor(nrm[:, 3, :], mv[:, :, 1], nrm[:, 2, :], ALU.mult))
            own(dve.tensor_tensor(nrm[:, 3, :], nrm[:, 3, :], nrm[:, 2, :], ALU.mult))
            own(dve.tensor_scalar(nrm[:, 3, :], nrm[:, 3, :], RMS_EPS, None, ALU.add))
            dve.nop().then_inc(var_ready, 1)
            for t in range(NT):
                dve.tensor_scalar(xn_tok[:, t, :], res[:, t, :], mv[:, t, 0:1], nrm[:, 2, t:t + 1],
                                  ALU.subtract, ALU.mult).then_inc(tok_ready, 1)
            for b in range(NBLK):
                dve.wait_ge(hi_ready, b + 1)
                dve.tensor_tensor(blk(xn_lo, b), ps[b][:, :], blk(xn_hi, b).bitcast(F32), ALU.subtract
                                  ).then_inc(lo_ready, 1)
            dve.wait_ge(root_ready, 2)
            own(dve.reciprocal(nrm[:, 5, :], nrm[:, 4, :]))
            own(dve.tensor_tensor(nrm[:, 5, :], nrm[:, 5, :], nrm[:, 2, :], ALU.mult))
            for t in range(NT):
                dve.tensor_scalar(xr_tok[:, t, :], res[:, t, :], mv[:, t, 0:1], nrm[:, 5, t:t + 1],
                                  ALU.subtract, ALU.mult).then_inc(tok_ready, 1)
            dve.wait_ge(qkv_made, 1)
            own(dve.tensor_copy(qkv[:, :, :].rearrange("p t c -> p (t c)"), ps[0][:, 0:NT * 3 * E0]))
            dve.nop().then_inc(qkv_copied, 1)
            dve.nop().then_inc(gated, 2)
            def over_e(a):
                return a[:, :, :, None].to_broadcast([P, NT, E0, E0])

            def over_j(a):
                return a[:, :, None, :].to_broadcast([P, NT, E0, E0])

            pr = pair[:, :, :].rearrange("p t (e j) -> p t e j", j=E0)
            pr2 = pair2[:, :, :].rearrange("p t (e j) -> p t e j", j=E0)
            q, k, v = (qkv[:, :, n * E0:(n + 1) * E0] for n in range(3))
            lg, ex, den, rank = (rsm[:, n, :, :] for n in range(4))
            own(dve.tensor_tensor(pr, over_e(q), over_j(k), ALU.mult))
            own(dve.tensor_reduce(den, pr, AX, ALU.max))
            own(dve.tensor_tensor(pr, pr, over_e(den), ALU.subtract))
            dve.nop().then_inc(r0_arg, 1)
            for b in range(NBLK):
                dve.wait_ge(hi_ready, NBLK + b + 1)
                dve.scalar_tensor_tensor(blk(xr_lo, b), ps[4 + b][:, :], vec_t[:, V_RMS:V_RMS + 1],
                                         blk(xr_hi, b).bitcast(F32), ALU.mult, ALU.subtract).then_inc(lo_ready, 1)
            dve.wait_ge(r0_exp, 1)
            own(dve.tensor_reduce(den, pr, AX, ALU.add))
            own(dve.tensor_tensor(pr, pr, over_j(v), ALU.mult))
            own(dve.tensor_reduce(lg, pr, AX, ALU.add))
            own(dve.reciprocal(den, den))
            own(dve.tensor_tensor(lg, lg, den, ALU.mult))
            own(dve.tensor_tensor(pr, over_j(lg), over_e(lg), ALU.is_gt))
            own(dve.tensor_tensor(pr2, over_j(lg), over_e(lg), ALU.is_equal))
            dve.wait_ge(consts_ready, 2)
            own(dve.tensor_tensor(pr2, pr2, earlier[:, None, :, :].to_broadcast([P, NT, E0, E0]), ALU.mult))
            own(dve.tensor_tensor(pr, pr, pr2, ALU.add))
            own(dve.tensor_reduce(rank, pr, AX, ALU.add))
            own(dve.tensor_scalar(rank, rank, 1.5, None, ALU.is_lt))
            own(dve.tensor_reduce(rrow[:, 0, :], lg, AX, ALU.max))
            own(dve.tensor_tensor(ex, lg, rrow[:, 0, :, None].to_broadcast([P, NT, E0]), ALU.subtract))
            dve.nop().then_inc(r0_arg, 1)
            dve.wait_ge(r0_exp, 2)
            own(dve.tensor_tensor(ex, ex, rank, ALU.mult))
            own(dve.tensor_reduce(rrow[:, 1, :], ex, AX, ALU.add))
            own(dve.reciprocal(rrow[:, 2, :], rrow[:, 1, :]))
            own(dve.tensor_tensor(score0[:, :, :], ex, rrow[:, 2, :, None].to_broadcast([P, NT, E0]), ALU.mult))

            dve.nop().then_inc(o_added, 2)
            dve.nop().then_inc(att_dve, 1)
            with dve.Fori(0, NB) as i:
                att = Chain(dve, att_dve, i * N_ATT_DVE + 1)

                def pe_step(n):
                    dve.wait_ge(att_pe, i * N_ATT_PE + n)

                def act_step(n):
                    dve.wait_ge(att_act, i * N_ATT_ACT + 1 + n)

                def attention(s):
                    if s == 2:
                        pe_step(1)
                        act_step(1)
                        att(dve.tensor_tensor(A["kv"], ps[7][:, :], A["k"], ALU.mult))
                    if s == 6:
                        act_step(5)
                        att(dve.tensor_tensor(A["m2"], A["m2"], A["sq"], ALU.add))
                        att(dve.tensor_scalar(A["m2"], A["m2"], 2.0 ** -110, 2.0 ** 117, ALU.max, ALU.min))
                    if s == 9:
                        act_step(8)
                        att(dve.tensor_tensor(A["k"], A["neg"], A["mag"], ALU.add))
                        att(dve.reciprocal(A["m2"], A["k"]))
                        att(dve.tensor_tensor(A["k"], A["ai"], A["m2"], ALU.mult))
                    if s == 10:
                        att(dve.tensor_scalar(A["neg"], A["ar"], 0.0, -2.0, ALU.is_lt, ALU.mult))
                        att(dve.tensor_scalar(A["m2"], A["neg"], 1.0, 1.0 / math.pi, ALU.add, ALU.mult))
                    if s == 11:
                        act_step(9)
                        att(dve.tensor_tensor(A["q"], A["q"], A["sq"], ALU.mult))
                    if s == 12:
                        act_step(11)
                        att(dve.tensor_tensor(A["theta"], A["theta"], A["m2"], ALU.mult))
                        att(dve.scalar_tensor_tensor(A["theta"], A["neg"], -0.25, A["theta"], ALU.mult, ALU.add))
                        att(dve.tensor_scalar(A["ar"], A["theta"], ROUND_TURN, ROUND_TURN, ALU.add, ALU.subtract))
                    if s == 13:
                        att(dve.tensor_tensor(A["ai"], A["theta"], A["ar"], ALU.subtract))
                        att(dve.tensor_tensor_scan(A["k"], ones[:, :], A["ar"], 0.0, ALU.mult, ALU.add))
                        att(dve.tensor_tensor_scan(A["theta"], ones[:, :], A["ai"], 0.0, ALU.mult, ALU.add))
                    if s == 14:
                        att(dve.tensor_scalar(A["ar"], A["k"], ROUND_INT, ROUND_INT, ALU.add, ALU.subtract))
                        att(dve.tensor_tensor(A["k"], A["k"], A["ar"], ALU.subtract))
                        att(dve.tensor_tensor(A["theta"], A["k"], A["theta"], ALU.add))
                    if s == 16:
                        act_step(15)
                        att(dve.scalar_tensor_tensor(A["neg"], A["mag"], 2.0, A["k"], ALU.mult, ALU.mult))
                        att(dve.tensor_scalar(A["m2"], A["theta"], -2.0, 1.0, ALU.mult, ALU.add))
                    if s == 17:
                        att(dve.tensor_tensor(A["k"], A["kv"], A["m2"], ALU.mult))
                        att(dve.tensor_tensor(A["mag"], A["kv"], A["neg"], ALU.mult))
                    if s == 18:
                        att(dve.tensor_tensor_scan(A["ar"], A["decay"], A["k"], 0.0, ALU.mult, ALU.add))
                        att(dve.tensor_tensor_scan(A["ai"], A["decay"], A["mag"], 0.0, ALU.mult, ALU.add))
                    if s == 19:
                        att(dve.tensor_tensor(A["ar"], A["ar"], A["m2"], ALU.mult))
                        att(dve.tensor_tensor(A["ai"], A["ai"], A["neg"], ALU.mult))
                        att(dve.tensor_tensor(A["ar"], A["ar"], A["ai"], ALU.add))
                    if s == 20:
                        att(dve.tensor_tensor(A["kv"], A["ar"], A["q"], ALU.mult))
                    if s == 23:
                        pe_step(7)
                        dve.wait_ge(o_added, i * OUTS + OUTS + 1)
                        r = res[:, bass.ds(i * TPB, TPB), :].rearrange("p t d -> p (t d)")
                        att(dve.tensor_tensor(r, r, ps[6][:, :], ALU.add))

                def add_output(o):
                    j, tb = divmod(o, NBLK)
                    dve.wait_ge(o_made, i * OUTS + o + 3)
                    dve.wait_ge(o_added, i * OUTS + o + 1)
                    for n in range(TPB):
                        t = tb * TPB + n
                        ins = dve.scalar_tensor_tensor(
                            res[:, t, :], ps[4 + o % 2][:, n * P:(n + 1) * P],
                            score0[:, t, bass.ds(i * EPI + j, 1)], res[:, t, :], ALU.mult, ALU.add)
                    ins.then_inc(o_added, 1)

                for s in range(STEPS):
                    tb, ft = divmod(s % (NBLK * NF), NF)
                    M = FT[ft][1]
                    dve.wait_ge(g_made, i * STEPS + s + 1)
                    dve.wait_ge(silu_done, i * STEPS + s + 3)
                    dve.wait_ge(o_made, i * OUTS + s // NF + 1)
                    dve.tensor_tensor(hid[0:M, tb % 2, ft, :], sil[0:M, s % 2, :], ps[2 + s % 2][0:M, :],
                                      ALU.mult).then_inc(gated, 1)
                    if s % NF == 2 and s >= 5:
                        add_output((s - 5) // NF)
                    attention(s)
                add_output(OUTS - 1)
                assert att.n == N_ATT_DVE

            dve.wait_ge(o_added, NB * OUTS + 2)
            own.wait()
            norm_stats(1)
            dve.wait_ge(root_ready, 3)
            own(dve.reciprocal(nrm[:, 2, :], nrm[:, 1, :]))
            for t in range(NT):
                dve.tensor_scalar(xn_tok[:, t, :], res[:, t, :], mv[:, t, 0:1], nrm[:, 2, t:t + 1],
                                  ALU.subtract, ALU.mult).then_inc(tok_ready, 1)
            for b in range(NBLK):
                dve.wait_ge(hi_ready, 2 * NBLK + b + 1)
                dve.tensor_tensor(blk(xn_lo, b), blk(u_t, b), blk(xn_hi, b).bitcast(F32), ALU.subtract
                                  ).then_inc(lo_ready, 1)
            dve.wait_ge(late_in, 16 * 8)
            top = rsm[:, 0, :, :]
            half_tiles = NT // 2
            for n in range(2):
                dve.wait_ge(logits_made, n + 1)
                own(dve.tensor_tensor(pair[:, n * half_tiles:(n + 1) * half_tiles, :],
                                      ps[n][:, :].rearrange("p (t e) -> p t e", e=E1),
                                      rbias[:, None, :].to_broadcast([P, half_tiles, E1]), ALU.add))
            for t in range(NT):
                dve.max(top[:, t, :], pair[:, t, :]).then_inc(dve_own, 1)
            own.n += NT
            own.wait()
            for t in range(NT):
                dve.match_replace(pair2[:, t, :], top[:, t, :], pair[:, t, :], -3.0e38).then_inc(dve_own, 1)
            own.n += NT
            own.wait()
            own(dve.tensor_tensor(pair2[:, :, :], pair[:, :, :], pair2[:, :, :], ALU.not_equal))
            own(dve.tensor_tensor(pair[:, :, :], pair[:, :, :], top[:, :, 0:1].to_broadcast([P, NT, E1]), ALU.subtract))
            dve.nop().then_inc(r1_arg, 1)
            dve.wait_ge(r1_exp, 1)
            own(dve.tensor_tensor(pair[:, :, :], pair[:, :, :], pair2[:, :, :], ALU.mult))
            own(dve.tensor_reduce(rrow[:, 0, :], pair[:, :, :], AX, ALU.add))
            own(dve.reciprocal(rrow[:, 1, :], rrow[:, 0, :]))
            own(dve.tensor_scalar(rrow[:, 1, :], rrow[:, 1, :], 0.5, None, ALU.mult))
            dve.wait_ge(turned, 3 * NBLK)
            for n in range(2):
                own(dve.tensor_tensor(xn_tok[:, :, n * E1:(n + 1) * E1], pair[:, :, :],
                                      rrow[:, 1, :, None].to_broadcast([P, NT, E1]), ALU.mult))
            dve.nop().then_inc(cw_ready, 1)

            def split_cw(b):
                dve.wait_ge(cw_turned, b + 1)
                dve.wait_ge(cw_copied, b + 1)
                own(dve.tensor_copy(blk(cw_hm, b), ps[b % 2][:, :]))
                own(dve.tensor_tensor(cwt[:, :], ps[b % 2][:, :], blk(cw_hm, b), ALU.subtract))
                own(dve.tensor_copy(cw_mid[:, :], cwt[:, :]))
                own(dve.tensor_tensor(cw_l[0:E1, b * TB:(b + 1) * TB], cwt[0:E1, :], cw_mid[0:E1, :], ALU.subtract))
                own(dve.tensor_copy(cw_hm[E1:P, b * TB:(b + 1) * TB], cw_mid[E1:P, :]))
                dve.nop().then_inc(cw_split, 1)

            def softplus(b):
                e, l, p = softplus_bufs[b]
                mask = at["theta"]
                dve.wait_ge(sp_log, b + 1)
                dve.wait_ge(sp_poly, b + 1)
                own(dve.tensor_scalar(mask[:, :], e[:, :], 2.0 ** -6, None, ALU.is_lt))
                own(dve.copy_predicated(l[:, :], mask[:, :].bitcast(mybir.dt.uint32), p[:, :]))
                own(dve.scalar_tensor_tensor(blk(dt_t, b), blk(dt_t, b), 0.0, l[:, :], ALU.max, ALU.add))
                own(dve.tensor_tensor(blk(win_t, b), blk(dt_t, b), blk(u_t, b), ALU.mult))
                dve.nop().then_inc(win_ready, 1)

            for half in (0, 2):
                split_cw(half)
                split_cw(half + 1)
                softplus(half)
                softplus(half + 1)

            dve.nop().then_inc(c1_done, 2)
            dve.nop().then_inc(hid_done, 2)
            dve.nop().then_inc(scanned, RING)

            def scan(i, s):
                dve.wait_ge(decay_ready, i * GSTEPS + s + 1)
                dve.wait_ge(weighted, i * GSTEPS + s + 1)
                dve.tensor_tensor_scan(state_ring[s % RING][:, :], decay_ring[s % RING][:, :],
                                       blk(win_t, s % NBLK), 0.0, ALU.mult, ALU.add).then_inc(scanned, 1)

            def group_turn(i, last):
                for s in range(GSTEPS):
                    g = i * GPI + s // NBLK
                    c = i * GSTEPS + s
                    dve.wait_ge(tanh_done, c + 3)
                    dve.wait_ge(cwx_made, c + 1)
                    dve.wait_ge(hid_done, c + 1)
                    dve.scalar_tensor_tensor(c1_ring[s % 2], sil[:, s % 2, :], 1.0, ps[2 + s % 2][:, :],
                                             ALU.add, ALU.mult).then_inc(c1_done, 1)
                    if s + 1 < GSTEPS:
                        scan(i, s + 1)
                    elif not last:
                        scan(i + 1, 0)
                    dve.wait_ge(c1_done, c + 3)
                    dve.wait_ge(g_out, c + 1)
                    dve.scalar_tensor_tensor(hid_ring[s % 2], ps[s % 2][:, :], vec_t[:, bass.ds(g + V_B1, 1)],
                                             c1_ring[s % 2], ALU.add, ALU.mult).then_inc(hid_done, 1)

            scan(0, 0)
            with dve.Fori(0, NG // GPI - 1) as i:
                group_turn(i, False)
            group_turn(NG // GPI - 1, True)

            dve.wait_ge(g_out, NG * NBLK + 2)
            dve.wait_ge(y_done, 1)
            for b in range(NBLK):
                own(dve.scalar_tensor_tensor(blk(y_t, b), ps[4 + b][:, :], sb2_sum[:, 0:1], blk(y_t, b),
                                             ALU.add, ALU.add))
                dve.nop().then_inc(sum_ready, 1)
            for b in range(NBLK):
                dve.wait_ge(sum_turned, b + 1)
                r = res[:, b * TPB:(b + 1) * TPB, :].rearrange("p t d -> p (t d)")
                dve.tensor_tensor(r, r, ps[b][:, :], ALU.add).then_inc(x2_ready, 1)

        @block.tensor
        def _(pe):
            pe.wait_ge(consts_ready, 1)
            pe.wait_ge(turn_in, 16 * 8)
            pe.transpose(ps[7][:, 0:N_VEC], vec_raw[:, :], ident[0:N_VEC, 0:N_VEC])
            pe.transpose(ps[7][:, P:P + 3 * E0], turn_raw[0:3 * E0, 0, :], ident[0:3 * E0, 0:3 * E0])
            pe.transpose(ps[7][:, 2 * P:3 * P], turn_raw[:, 1, :], ident[:, :]).then_inc(small_turned, 1)

            def turn_tiles(src, bank, first):
                for t in range(NT):
                    pe.wait_ge(tok_ready, first + t + 1)
                    ins = pe.transpose(ps[bank + t // TPB][:, (t % TPB) * P:(t % TPB + 1) * P], src[:, t, :], ident[:, :])
                    if t % TPB == TPB - 1:
                        ins.then_inc(turned, 1)

            turn_tiles(xn_tok, 0, 0)
            def turn_w1(j, loads):
                pe.wait_ge(e_in[j], loads)
                for half in range(2):
                    for n, (f0, m) in enumerate(FT):
                        ins = pe.transpose(ps[6 + half][:, f0:f0 + m], e_raw1[j][0:m, half * NF + n, :],
                                           ident[0:m, 0:m])
                ins.then_inc(e_turned, 1)

            def turn_w2(j, before, bank):
                pe.wait_ge(e_copied, before + 1)
                for n, (f0, m) in enumerate(FT):
                    ins = pe.transpose(ps[bank][0:m, n * P:(n + 1) * P], e_raw2[j][:, f0:f0 + m], ident[:, :])
                ins.then_inc(e_turned, 1)

            pe.wait_ge(small_copied, 1)
            turn_w1(0, 80)
            turn_w2(0, 0, 4)
            for t in range(NT):
                pe.wait_ge(hi_ready, t // TPB + 1)
                pe.wait_ge(lo_ready, t // TPB + 1)
                ins = product(pe, ps[0][:, t * 3 * E0:(t + 1) * 3 * E0],
                              xn_hi[:, t * P:(t + 1) * P], xn_lo[:, t * P:(t + 1) * P],
                              turn_hi[:, 0, 0:3 * E0], turn_lo[:, 0, 0:3 * E0])
            ins.then_inc(qkv_made, 1)
            turn_w1(1, 80)
            turn_w2(1, 2, 5)
            pe.wait_ge(e_copied, 2 * EPI)
            turn_tiles(xr_tok, 4, NT)
            pe.wait_ge(hi_ready, 2 * NBLK)
            pe.wait_ge(lo_ready, 2 * NBLK)

            def hidden(i, s):
                j, r = divmod(s, NBLK * NF)
                tb, ft = divmod(r, NF)
                f0, m = FT[ft]
                if r == 0:
                    pe.wait_ge(e_split, i * EPI + j + 1)
                pe.wait_ge(silu_done, i * STEPS + s + 1)
                product(pe, ps[s % 2][0:m, :], e_hi[j][:, f0:f0 + m], e_lo[j][:, f0:f0 + m],
                        blk(xn_hi, tb), blk(xn_lo, tb)).then_inc(a_made, 1)
                pe.wait_ge(gated, i * STEPS + s + 1)
                product(pe, ps[2 + s % 2][0:m, :], e_hi[j][:, F + f0:F + f0 + m], e_lo[j][:, F + f0:F + f0 + m],
                        blk(xn_hi, tb), blk(xn_lo, tb)).then_inc(g_made, 1)

            def output(i, o):
                j, tb = divmod(o, NBLK)
                if tb == 0:
                    pe.wait_ge(w2_ready, i * EPI + j + 1)
                pe.wait_ge(gated, i * STEPS + o * NF + NF + 2)
                pe.wait_ge(o_added, i * OUTS + o + 1)
                for n in range(TPB):
                    for ft, (f0, m) in enumerate(FT):
                        ins = pe.matmul(ps[4 + o % 2][:, n * P:(n + 1) * P],
                                        hid[0:m, tb % 2, ft, n * P:(n + 1) * P], e_w2[j][0:m, ft, :],
                                        start=(ft == 0), stop=(ft == NF - 1))
                ins.then_inc(o_made, 1)

            def attention(i, s, last):
                def project(n, bank):
                    product(pe, ps[bank][:, :], proj_hi[:, n, :], proj_lo[:, n, :],
                            xr_hi[:, bass.ds(i * TB, TB)], xr_lo[:, bass.ds(i * TB, TB)]).then_inc(att_pe, 1)

                def act_step(n):
                    pe.wait_ge(att_act, i * N_ATT_ACT + 1 + n)

                def dve_step(n):
                    pe.wait_ge(att_dve, i * N_ATT_DVE + 1 + n)

                copied = (i + 1) * 2 * EPI
                if s == 0:
                    act_step(0)
                    pe.wait_ge(e_copied, copied)
                    project(1, 7)
                if s == 1:
                    dve_step(0)
                    project(0, 6)
                if s == 3:
                    act_step(1)
                    project(2, 6)
                if s == 4:
                    dve_step(1)
                    project(3, 7)
                if s == 6:
                    act_step(2)
                    project(4, 6)
                if s == 7:
                    act_step(4)
                    project(5, 7)
                if not last:
                    if s == 10:
                        act_step(9)
                        turn_w1(0, i * 80 + 160)
                    if s == 13:
                        turn_w2(0, copied, 6)
                    if s == 16:
                        pe.wait_ge(e_copied, copied + 2)
                        turn_w1(1, i * 80 + 160)
                    if s == 19:
                        turn_w2(1, copied + 2, 7)
                if s == 22:
                    act_step(7)
                    dve_step(28)
                    if not last:
                        pe.wait_ge(e_copied, copied + 3)
                    for n in range(TPB):
                        ins = pe.matmul(ps[6][:, n * P:(n + 1) * P], at["kv"][:, n * P:(n + 1) * P], wo_sb[:, :],
                                        start=True, stop=True)
                    ins.then_inc(att_pe, 1)

            pe.wait_ge(weights_split, 1)
            pe.wait_ge(qkv_copied, 1)
            pe.nop().then_inc(o_made, 2)
            AHEAD = 2
            for s in range(AHEAD):
                hidden(0, s)

            def turn(i, last):
                for s in range(STEPS):
                    attention(i, s, last)
                    if s + AHEAD < STEPS:
                        hidden(i, s + AHEAD)
                    elif not last:
                        hidden(i + 1, s + AHEAD - STEPS)
                    if s % NF == NF - 1:
                        output(i, s // NF)

            with pe.Fori(0, NB - 1) as i:
                turn(i, False)
            turn(NB - 1, True)

            turn_tiles(xn_tok, 0, 2 * NT)
            pe.wait_ge(weights_split, 2)
            pe.wait_ge(late_in, 16 * 8)
            for b in range(NBLK):
                pe.wait_ge(hi_ready, 2 * NBLK + b + 1)
                pe.wait_ge(lo_ready, 2 * NBLK + b + 1)
                product(pe, ps[4 + b][:, :], turn_hi[:, 1, :], turn_lo[:, 1, :], blk(xn_hi, b), blk(xn_lo, b)
                        ).then_inc(dt_made, 1)
            for b in range(NBLK):
                for t in range(b * TPB, (b + 1) * TPB):
                    ins = product(pe, ps[t // 8][:, (t % 8) * E1:(t % 8 + 1) * E1],
                                  xn_hi[:, t * P:(t + 1) * P], xn_lo[:, t * P:(t + 1) * P], rout_hi[:, :], rout_lo[:, :])
                if b % 2:
                    ins.then_inc(logits_made, 1)

            def shared_in(c):
                k, tb = divmod(c, NBLK)
                e, n = divmod(k, HS // P)
                if c >= 2:
                    pe.wait_ge(sh_silu, c - 1)
                product(pe, ps[2 + c % 2][:, :], sw1_hi[:, e, n * P:(n + 1) * P], sw1_lo[:, e, n * P:(n + 1) * P],
                        blk(xn_hi, tb), blk(xn_lo, tb)).then_inc(sh_made, 1)

            def shared_out(c):
                k, tb = divmod(c, NBLK)
                pe.wait_ge(sh_silu, c + 1)
                if k == 0:
                    pe.wait_ge(dt_left, tb + 1)
                pe.matmul(ps[4 + tb][:, :], sw2_sb[:, k, :], hid[:, c % 2, 2, :], start=(k == 0), stop=False,
                          skip_group_check=True).then_inc(sh_used, 1)

            def turn_cw(b):
                pe.wait_ge(cw_ready, 1)
                if b >= 2:
                    pe.wait_ge(cw_copied, b - 1)
                    pe.wait_ge(cw_split, b - 1)
                for n in range(TPB):
                    ins = pe.transpose(ps[b % 2][:, n * P:(n + 1) * P], xn_tok[:, b * TPB + n, :], ident[:, :])
                ins.then_inc(cw_turned, 1)

            def second_biases(b):
                pe.wait_ge(cw_copied, b + 1)
                pe.matmul(ps[4 + b][:, :], b2_sb[:, :], cw_b2[:, b % 2, :], start=False, stop=False,
                          skip_group_check=True).then_inc(b2_used, 1)

            shared_in(0)
            for c in range(NSH * NBLK):
                for b, at_step in enumerate(CW_STEPS):
                    if c == at_step:
                        turn_cw(b)
                if c + 1 < NSH * NBLK:
                    shared_in(c + 1)
                shared_out(c)
                for b, at_step in enumerate(CW_STEPS):
                    if c == max(at_step, NBLK) + 1 + b % 2:
                        second_biases(b)
            pe.wait_ge(cw_split, NBLK)

            def expert_in(i, s):
                j, tb = divmod(s, NBLK)
                if tb == 0:
                    pe.wait_ge(g_split, i * GPI + j + 1)
                pe.wait_ge(hid_done, i * GSTEPS + s + 1)
                product(pe, ps[s % 2][:, :], g_hi[j][:, :], g_lo[j][:, :], blk(xn_hi, tb), blk(xn_lo, tb)
                        ).then_inc(h_made, 1)
                pe.wait_ge(c1_done, i * GSTEPS + s + 1)
                w = sel[:, bass.ds((i * GPI + j) * P, P)]
                pe.matmul(ps[2 + s % 2][:, :], w, blk(cw_hm, tb), start=True, stop=False)
                pe.matmul(ps[2 + s % 2][:, :], w, blk(cw_l, tb), start=False, stop=True).then_inc(cwx_made, 1)

            def expert_out(i, s, last):
                j, tb = divmod(s, NBLK)
                if tb == 0:
                    pe.wait_ge(g_w2_in[j], i * 16 + 16)
                pe.wait_ge(hid_done, i * GSTEPS + s + 3)
                pe.matmul(ps[4 + tb][:, :], g_w2[j][:, :], hid_ring[s % 2], start=False,
                          stop=last and j == GPI - 1, skip_group_check=True).then_inc(g_out, 1)

            pe.nop().then_inc(g_out, 2)
            expert_in(0, 0)
            expert_in(0, 1)

            def group_turn(i, last):
                for s in range(GSTEPS):
                    if s + 2 < GSTEPS:
                        expert_in(i, s + 2)
                    elif not last:
                        expert_in(i + 1, s + 2 - GSTEPS)
                    expert_out(i, s, last)

            with pe.Fori(0, NG // GPI - 1) as i:
                group_turn(i, False)
            group_turn(NG // GPI - 1, True)
            for b in range(NBLK):
                pe.wait_ge(sum_ready, b + 1)
                for n in range(TPB):
                    ins = pe.transpose(ps[b][:, n * P:(n + 1) * P], y_t[:, b * TB + n * P:b * TB + (n + 1) * P],
                                       ident[:, :])
                ins.then_inc(sum_turned, 1)


_INS = ['L0_attn_x', 'L0_attn_wq', 'L0_attn_wk', 'L0_attn_wv', 'L0_attn_wa', 'L0_attn_wg', 'L0_attn_wo',
        'L0_attn_rms_scale', 'L0_ffn_wqkv', 'L0_ffn_w1', 'L0_ffn_w2', 'L1_attn_A_log', 'L1_attn_B_mat',
        'L1_attn_C_mat', 'L1_attn_D_vec', 'L1_attn_W_dt', 'L1_attn_b_dt', 'L1_ffn_router_w', 'L1_ffn_router_b',
        'L1_ffn_w1', 'L1_ffn_b1', 'L1_ffn_w2', 'L1_ffn_b2', 'L1_ffn_sw1', 'L1_ffn_sb1', 'L1_ffn_sw2',
        'L1_ffn_sb2']


def kernel(**inputs):
    import numpy as _np
    import concourse.bacc as _bacc
    from concourse import mybir as _mybir
    from concourse.bass_utils import run_bass_kernel_spmd as _run

    nc = _bacc.Bacc("TRN2", target_bir_lowering=False, num_devices=1)
    arrays, args = {}, []
    for name in _INS:
        a = _np.ascontiguousarray(inputs[name])
        arrays[f"in_{name}"] = a
        args.append(nc.dram_tensor(f"in_{name}", a.shape, _mybir.dt.from_np(a.dtype), kind="ExternalInput").ap())
    x = arrays["in_L0_attn_x"]
    args.append(nc.dram_tensor("out_0", x.shape, _mybir.dt.from_np(x.dtype), kind="ExternalOutput").ap())
    program(nc, *args)
    r = _run(nc, [arrays], core_ids=[0])
    return r.results[0]["out_0"]
```

```python
import math
from contextlib import ExitStack

import concourse.bass as bass
from concourse import mybir

ALU = mybir.AluOpType
ACT = mybir.ActivationFunctionType
AX = mybir.AxisListType.X
F32 = mybir.dt.float32
F32R = mybir.dt.float32r
BF16 = mybir.dt.bfloat16

P = 128
TB = 512
ROUND_TURN = 1.5 * 2.0 ** 10
ROUND_INT = 1.5 * 2.0 ** 23

V_RMS, V_D, V_BDT, V_SB2, V_SB1, V_B1 = 0, 1, 2, 3, 5, 9
N_VEC = 25


class Chain:

    def __init__(self, eng, sem, at=0):
        self.eng, self.sem, self.base, self.n = eng, sem, at, 0

    def __call__(self, ins):
        ins.then_inc(self.sem, 1)
        self.n += 1
        self.wait()

    def wait(self):
        self.eng.wait_ge(self.sem, self.base + self.n)


def program(nc, x, wq, wk, wv, wa, wg, wo, rms_scale, wqkv, w1, w2, A_log, B_mat, C_mat, D_vec, W_dt, b_dt,
            router_w, router_b, rw1, rb1, rw2, rb2, sw1, sb1, sw2, sb2, out):
    NB, T, D = x.shape
    NTOK = NB * T
    NT = NTOK // P
    TPB = TB // P
    E0, F2, _ = w1.shape
    F = F2 // 2
    FT = [(s, min(P, F - s)) for s in range(0, F, P)]
    NF = len(FT)
    E1, _, H1 = rw1.shape
    GE = P // H1
    NG = E1 // GE
    NS = A_log.shape[1]
    ES, _, HS = sw1.shape
    NSH = ES * HS // P
    LN_EPS, RMS_EPS = 1e-5, 1e-6
    TOPK = 2
    assert D == P and T == TB and NS == NG and E0 == 2 * NB and NF == 3

    x_v = x.rearrange("b (c p) d -> p (b c) d", p=P)
    out_v = out.rearrange("b (c p) d -> p (b c) d", p=P)

    def row(a):
        return a.rearrange("(a d) -> a d", a=1)

    with ExitStack() as ctx:
        def sb(name, shape, dt=F32):
            return ctx.enter_context(nc.sbuf_tensor(name, shape, dt))

        def sem(name):
            return ctx.enter_context(nc.semaphore(name))

        ident = sb("ident", [P, P])
        sel = sb("sel", [P, NG * P], BF16)
        ones = sb("ones", [P, TB])
        half_pi = sb("half_pi", [P, 1])
        warm = sb("warm", [P, 3])
        proj_raw = sb("proj_raw", [P, 6, P])
        proj_hi = sb("proj_hi", [P, 6, P], F32R)
        proj_lo = sb("proj_lo", [P, 6, P], F32R)
        wo_sb = sb("wo_sb", [P, P])
        turn_raw = sb("turn_raw", [P, 2, P])
        turn_hi = sb("turn_hi", [P, 2, P], F32R)
        turn_lo = sb("turn_lo", [P, 2, P], F32R)
        rout_raw = sb("rout_raw", [P, E1])
        rout_hi = sb("rout_hi", [P, E1], F32R)
        rout_lo = sb("rout_lo", [P, E1], F32R)
        rbias = sb("rbias", [E1, 1])
        sw1_raw = sb("sw1_raw", [P, ES, HS])
        sw1_hi = sb("sw1_hi", [P, ES, HS], F32R)
        sw1_lo = sb("sw1_lo", [P, ES, HS], F32R)
        sw2_sb = sb("sw2_sb", [P, NSH, P])
        b2_sb = sb("b2_sb", [E1, P])
        vec_raw = sb("vec_raw", [N_VEC, P])
        vec_t = sb("vec_t", [P, N_VEC])
        b1_half = sb("b1_half", [P, NG])
        sb2_sum = sb("sb2_sum", [P, 1])
        ssm_raw = sb("ssm_raw", [P, 3, NS])
        ssm_a = sb("ssm_a", [P, NS])
        ssm_cb = sb("ssm_cb", [P, NS])

        res = sb("res", [P, NT, P])
        xn_tok = sb("xn_tok", [P, NT, P])
        xr_tok = sb("xr_tok", [P, NT, P])
        xn_hi = sb("xn_hi", [P, NTOK], F32R)
        xn_lo = sb("xn_lo", [P, NTOK], F32R)
        xr_hi = sb("xr_hi", [P, NTOK], F32R)
        xr_lo = sb("xr_lo", [P, NTOK], F32R)
        stats = sb("stats", [P, NT, 6])
        mv = sb("mv", [P, NT, 2])
        nrm = sb("nrm", [P, 6, NT])
        qkv = sb("qkv", [P, NT, 3 * E0])
        pair = sb("pair", [P, NT, E0 * E0])
        pair2 = sb("pair2", [P, NT, E0 * E0])
        rsm = sb("rsm", [P, 4, NT, E0])
        rrow = sb("rrow", [P, 3, NT])
        score0 = sb("score0", [P, NT, E0])
        e_raw1 = [sb(f"e_raw1_{j}", [P, 2 * NF, P]) for j in range(2)]
        e_raw2 = [sb(f"e_raw2_{j}", [P, F]) for j in range(2)]
        e_hi = [sb(f"e_hi_{j}", [P, F2], F32R) for j in range(2)]
        e_lo = [sb(f"e_lo_{j}", [P, F2], F32R) for j in range(2)]
        e_w2 = [sb(f"e_w2_{j}", [P, NF, P]) for j in range(2)]
        e_t = [sb(f"e_t_{j}", [P, F2]) for j in range(2)]
        e_w2_t = [sb(f"e_w2_t_{j}", [P, NF, P]) for j in range(2)]
        sil = sb("sil", [P, 2, TB])
        hid = sb("hid", [P, 2, NF, TB])
        at = {n: sb(f"at_{n}", [P, TB]) for n in (
            "k", "kv", "ar", "ai", "sq", "m2", "mag", "decay", "theta", "neg", "q", "s0", "s1")}
        u_t = xr_tok[:].rearrange("p a b -> p (a b)")
        y_t = xn_tok[:].rearrange("p a b -> p (a b)")
        dt_t = sb("dt_t", [P, NTOK])
        win_t = sb("win_t", [P, NTOK])
        cw_b2 = sb("cw_b2", [E1, 2, TB])
        cw_hl = sb("cw_hl", [P, NTOK], F32R)
        sel_now = [sb(f"sel_now_{j}", [P, P], F32R) for j in range(2)]
        g_raw1 = [sb(f"g_raw1_{j}", [P, GE, H1]) for j in range(2)]
        g_hi = [sb(f"g_hi_{j}", [P, P], F32R) for j in range(2)]
        g_lo = [sb(f"g_lo_{j}", [P, P], F32R) for j in range(2)]
        g_w2 = [sb(f"g_w2_{j}", [P, P]) for j in range(2)]

        psum = ctx.enter_context(nc.psum_tensor("psum", [P, 8, TB], F32))
        ps = [psum[:, n, :] for n in range(8)]

        x_in = [sem(f"x_in{b}") for b in range(NB)]
        turn_in, proj_in, late_in = sem("turn_in"), sem("proj_in"), sem("late_in")
        e_in = [sem(f"e_in{j}") for j in range(2)]
        g_in = [sem(f"g_in{j}") for j in range(2)]
        g_w2_in = [sem(f"g_w2_in{j}") for j in range(2)]
        dve_own, act_own, pool_own = sem("dve_own"), sem("act_own"), sem("pool_own")
        out_done = sem("out_done")
        consts_ready = sem("consts_ready")
        var_ready, root_ready, rms_ready = sem("var_ready"), sem("root_ready"), sem("rms_ready")
        tok_ready = sem("tok_ready")
        small_turned, small_hi, small_copied = sem("small_turned"), sem("small_hi"), sem("small_copied")
        weights_split = sem("weights_split")
        turned, hi_ready, lo_ready = sem("turned"), sem("hi_ready"), sem("lo_ready")
        qkv_t_made, qkv_t_copied = sem("qkv_t_made"), sem("qkv_t_copied")
        qkv_made, qkv_copied = sem("qkv_made"), sem("qkv_copied")
        r0_arg, r0_exp = sem("r0_arg"), sem("r0_exp")
        e_turned, e_copied, e_split, w2_ready = sem("e_turned"), sem("e_copied"), sem("e_split"), sem("w2_ready")
        a_made, g_made, silu_done, gated = sem("a_made"), sem("g_made"), sem("silu_done"), sem("gated")
        o_made, o_added = sem("o_made"), sem("o_added")
        att_pe, att_act, att_dve, att_pool = sem("att_pe"), sem("att_act"), sem("att_dve"), sem("att_pool")
        dt_made, dt_left, sp_exp, sp_log = sem("dt_made"), sem("dt_left"), sem("sp_exp"), sem("sp_log")
        sp_poly, win_ready = sem("sp_poly"), sem("win_ready")
        lg_made, lg_biased = sem("lg_made"), sem("lg_biased")
        logits_made, r1_arg, r1_exp = sem("logits_made"), sem("r1_arg"), sem("r1_exp")
        cw_ready, cw_turned, cw_copied, cw_split = sem("cw_ready"), sem("cw_turned"), sem("cw_copied"), sem("cw_split")
        sh_made, sh_silu, sh_used, b2_used = sem("sh_made"), sem("sh_silu"), sem("sh_used"), sem("b2_used")
        g_split, h_made, cwx_made = sem("g_split"), sem("h_made"), sem("cwx_made")
        tanh_done, c1_done, hid_done, g_out = sem("tanh_done"), sem("c1_done"), sem("hid_done"), sem("g_out")
        decay_ready, scanned, weighted, y_added = sem("decay_ready"), sem("scanned"), sem("weighted"), sem("y_added")
        y_done, sum_ready, sum_turned, x2_ready = (
            sem("y_done"), sem("sum_ready"), sem("sum_turned"), sem("x2_ready"))

        def product(pe, acc, w_hi, w_lo, m_hi, m_lo):
            pe.matmul(acc, w_hi, m_hi, start=True, stop=False)
            pe.matmul(acc, w_lo, m_hi, start=False, stop=False)
            return pe.matmul(acc, w_hi, m_lo, start=False, stop=True)

        def blk(buf, b):
            return buf[:, b * TB:(b + 1) * TB]

        act_passed, pool_passed = sem("act_passed"), sem("pool_passed")

        NBLK = NB
        EPI = 2
        STEPS = EPI * NBLK * NF
        OUTS = EPI * NBLK
        N_ATT_PE, N_ATT_ACT, N_ATT_DVE, N_ATT_POOL = 7, 16, 25, 4
        CW_STEPS = (4, 4, 5, 5)
        POOL_LOGS = 2
        GPI = 2
        GSTEPS = GPI * NBLK
        hid_ring = [hid[:, r, 0, :] for r in range(2)]
        c1_ring = [hid[:, r, 1, :] for r in range(2)]
        RING = 4
        decay_ring = [at[n] for n in ("k", "kv", "m2", "mag")]
        state_ring = [at[n] for n in ("ar", "ai", "decay", "theta")]
        term_ring = [at[n] for n in ("sq", "neg", "q", "s0")]
        softplus_bufs = [[at[n] for n in names] for names in (
            ("s0", "s1", "q"), ("m2", "decay", "mag"), ("k", "kv", "ar"), ("ai", "neg", "sq"))]

        A = {n: a[:, :] for n, a in at.items()}
        qkv_t = hid[:, :, :, :].rearrange("p a b t -> p (a b t)")[0:3 * E0, :]

        block = ctx.enter_context(nc.Block())

        @block.sync
        def _(sp):
            def load_expert(e, j):
                for half in range(2):
                    r0 = half * F
                    sp.dma_start(e_raw1[j][:, half * NF:half * NF + 2, :],
                                 w1[e, r0:r0 + 2 * P, :].rearrange("... (c p) d -> ... p c d", p=P)
                                 ).then_inc(e_in[j], 16)
                    sp.dma_start(e_raw1[j][0:FT[2][1], half * NF + 2, :],
                                 w1[e, r0 + 2 * P:r0 + F, :]).then_inc(e_in[j], 16)
                sp.dma_start(e_raw2[j][:, :], w2[e, :, :]).then_inc(e_in[j], 16)

            def load_group(g, j):
                load_group_w1(g, j)
                load_group_w2(g, j)

            def load_group_w1(g, j):
                sp.dma_start(g_raw1[j][:, :, :], rw1[bass.ds(g * GE, GE), :, :].rearrange("e d h -> d e h")
                             ).then_inc(g_in[j], 16)

            def load_group_w2(g, j):
                sp.dma_start(g_w2[j][:, :], rw2[bass.ds(g * GE, GE), :, :].rearrange("e h d -> (e h) d")
                             ).then_inc(g_w2_in[j], 16)

            for b in range(NB):
                sp.dma_start(res[:, b * TPB:(b + 1) * TPB, :], x_v[:, b * TPB:(b + 1) * TPB, :]).then_inc(x_in[b], 16)
            sp.dma_start(turn_raw[0:3 * E0, 0, :], wqkv).then_inc(turn_in, 16)
            sp.dma_start(turn_raw[:, 1, :], W_dt).then_inc(turn_in, 16)
            sp.dma_start(vec_raw[V_RMS:V_RMS + 1, :], row(rms_scale)).then_inc(turn_in, 16)
            sp.dma_start(vec_raw[V_D:V_D + 1, :], row(D_vec)).then_inc(turn_in, 16)
            sp.dma_start(vec_raw[V_BDT:V_BDT + 1, :], row(b_dt)).then_inc(turn_in, 16)
            sp.dma_start(vec_raw[V_SB2:V_SB2 + ES, :], sb2).then_inc(turn_in, 16)
            sp.dma_start(vec_raw[V_SB1:V_SB1 + NSH, :], sb1.rearrange("e (c h) -> (e c) h", h=P)
                         ).then_inc(turn_in, 16)
            sp.dma_start(vec_raw[V_B1:V_B1 + NG, :], rb1.rearrange("(g e) h -> g (e h)", e=GE)
                         ).then_inc(turn_in, 16)
            load_expert(0, 0)
            for n, w in enumerate((wk, wv, None, None, wg, wq)):
                if w is not None:
                    sp.dma_start(proj_raw[:, n, :], w).then_inc(proj_in, 16)
            sp.dma_start(proj_raw[:, 2:4, :], wa.rearrange("d (c h) -> d c h", h=P)).then_inc(proj_in, 16)
            sp.dma_start(wo_sb[:, :], wo).then_inc(proj_in, 16)
            load_expert(1, 1)
            sp.dma_start(rout_raw[:, :], router_w).then_inc(late_in, 16)
            sp.dma_start(rbias[:, :], router_b.rearrange("(e a) -> e a", a=1)).then_inc(late_in, 16)
            sp.dma_start(sw1_raw[:, :, :], sw1.rearrange("e d h -> d e h")).then_inc(late_in, 16)
            sp.dma_start(sw2_sb[:, :, :], sw2.rearrange("e (c h) d -> h (e c) d", h=P)).then_inc(late_in, 16)
            sp.dma_start(b2_sb[:, :], rb2).then_inc(late_in, 16)
            for n, w in enumerate((A_log, B_mat, C_mat)):
                sp.dma_start(ssm_raw[:, n, :], w).then_inc(late_in, 16)
            load_group(0, 0)
            load_group(1, 1)
            with sp.Fori(0, NB - 1) as i:
                for j in range(EPI):
                    sp.wait_ge(e_turned, i * 2 * EPI + 2 * j + 2)
                    load_expert(i * EPI + EPI + j, j)
            with sp.Fori(0, NG // GPI - 1) as i:
                for j in range(GPI):
                    sp.wait_ge(g_split, i * GPI + j + 1)
                    load_group_w1(i * GPI + GPI + j, j)
                for j in range(GPI):
                    sp.wait_ge(g_out, i * GSTEPS + (j + 1) * NBLK + 2)
                    load_group_w2(i * GPI + GPI + j, j)
            for b in range(NB):
                sp.wait_ge(x2_ready, b + 1)
                sp.dma_start(out_v[:, b * TPB:(b + 1) * TPB, :], res[:, b * TPB:(b + 1) * TPB, :]
                             ).then_inc(out_done, 16)
            sp.wait_ge(out_done, 16 * NB)

        @block.gpsimd
        def _(pool):
            own = Chain(pool, pool_own)
            own(pool.memset(ident[:, :], 0.0))
            own(pool.affine_select(out=ident[:, :], in_=ident[:, :], compare_op=ALU.not_equal, fill=1.0,
                                   base=0, pattern=[[-1, P]], channel_multiplier=1))
            pool.nop().then_inc(consts_ready, 1)
            own(pool.memset(ones[:, :], 1.0))
            own(pool.memset(half_pi[:, :], math.pi / 2))
            for j in range(EPI):
                own(pool.memset(e_w2_t[j][:, :, :], 0.0))
            pool.nop().then_inc(consts_ready, 1)

            def split(src, hi, lo):
                own(pool.tensor_scalar(hi, src, 1.0, 0.0, ALU.mult, ALU.add))
                own(pool.tensor_tensor(lo, src, hi.bitcast(F32), ALU.subtract))

            pool.wait_ge(proj_in, 16 * 6)
            split(proj_raw[:, :, :], proj_hi[:, :, :], proj_lo[:, :, :])
            pool.nop().then_inc(weights_split, 1)
            def expert_w1(j):
                split(e_t[j][:, :], e_hi[j][:, :], e_lo[j][:, :])
                pool.nop().then_inc(e_split, 1)

            def expert_w2(j):
                own(pool.tensor_scalar(e_w2[j][:, :, :], e_w2_t[j][:, :, :], 1.0, 0.0, ALU.mult, ALU.add))
                pool.nop().then_inc(w2_ready, 1)

            for j in range(EPI):
                pool.wait_ge(e_copied, 2 * j + 2)
                expert_w1(j)
                expert_w2(j)
            own(pool.memset(sel[:, :], 0.0))
            sel_v = sel[:, :].rearrange("p (c h) -> p c h", h=H1)
            for first in (0, E1):
                own(pool.affine_select(out=sel_v, in_=sel_v, compare_op=ALU.not_equal, fill=1.0,
                                       base=-first, pattern=[[-1, E1], [0, H1]], channel_multiplier=1))
            pool.wait_ge(late_in, 16 * 8)
            split(rout_raw[:, :], rout_hi[:, :], rout_lo[:, :])
            split(sw1_raw[:, :, :], sw1_hi[:, :, :], sw1_lo[:, :, :])
            own(pool.tensor_tensor(ssm_cb[:, :], ssm_raw[:, 1, :], ssm_raw[:, 2, :], ALU.mult))
            pool.nop().then_inc(weights_split, 1)

            def split_group(j):
                split(g_raw1[j][:, :, :].rearrange("p e h -> p (e h)"), g_hi[j][:, :], g_lo[j][:, :])
                own(pool.tensor_copy(sel_now[j][:, :], sel[:, j * P:(j + 1) * P]))
                pool.nop().then_inc(g_split, 1)

            for j in range(GPI):
                pool.wait_ge(g_in[j], 16)
                split_group(j)

            n0 = own.n

            def turn(i, last):
                nonlocal own
                own = Chain(pool, pool_own, i * 3 * EPI + n0)

                def attend(out, a, b, op):
                    pool.nop().then_inc(pool_passed, 1)
                    pool.tensor_tensor(out, a, b, op).then_inc(att_pool, 1)

                def dve_step(n):
                    pool.wait_ge(att_dve, i * N_ATT_DVE + 1 + n)

                def next_expert(j):
                    pool.wait_ge(e_copied, i * 2 * EPI + 2 * EPI + 2 * j + 1)
                    pool.wait_ge(g_made, i * STEPS + (j + 1) * NBLK * NF)
                    pool.nop().then_inc(pool_passed, 1)
                    expert_w1(j)
                    pool.wait_ge(e_copied, i * 2 * EPI + 2 * EPI + 2 * j + 2)
                    pool.wait_ge(o_made, i * OUTS + (j + 1) * NBLK + 2)
                    pool.nop().then_inc(pool_passed, 1)
                    expert_w2(j)

                pool.wait_ge(att_act, i * N_ATT_ACT + 1 + 9)
                attend(A["q"], A["q"], A["sq"], ALU.mult)
                dve_step(12)
                attend(A["ai"], A["theta"], A["ar"], ALU.subtract)
                if not last:
                    next_expert(0)
                dve_step(18)
                attend(A["mag"], A["kv"], A["neg"], ALU.mult)
                dve_step(20)
                attend(A["ai"], A["ai"], A["neg"], ALU.mult)
                if not last:
                    next_expert(1)

            with pool.Fori(0, NB - 1) as i:
                turn(i, False)
            turn(NB - 1, True)
            own = Chain(pool, pool_own, n0 + (NB - 1) * 3 * EPI)

            for b in range(POOL_LOGS):
                pool.wait_ge(sp_exp, b + 1)
                e, _, p = softplus_bufs[b]
                own(pool.tensor_scalar(p[:, :], e[:, :], -1.0 / 4, 1.0 / 3, ALU.mult, ALU.add))
                own(pool.tensor_tensor(p[:, :], p[:, :], e[:, :], ALU.mult))
                own(pool.tensor_scalar(p[:, :], p[:, :], 1.0, -1.0 / 2, ALU.mult, ALU.add))
                own(pool.tensor_tensor(p[:, :], p[:, :], e[:, :], ALU.mult))
                own(pool.tensor_scalar(p[:, :], p[:, :], 1.0, 1.0, ALU.mult, ALU.add))
                own(pool.tensor_tensor(p[:, :], p[:, :], e[:, :], ALU.mult))
                pool.nop().then_inc(sp_poly, 1)
            pool.wait_ge(cw_turned, NBLK)
            own(pool.tensor_scalar(y_t, u_t, vec_t[:, V_D:V_D + 1], 0.0, ALU.mult, ALU.add))

            n0 = own.base + own.n

            def group_turn(i, last):
                own = Chain(pool, pool_own, i * (GSTEPS + 3 * GPI) + n0)
                for s in range(GSTEPS):
                    j, tb = divmod(s, NBLK)
                    pool.wait_ge(weighted, i * GSTEPS + s + 1 + RING)
                    pool.nop().then_inc(pool_passed, 1)
                    own(pool.tensor_tensor(blk(y_t, tb), blk(y_t, tb), term_ring[s % RING][:, :], ALU.add))
                    pool.nop().then_inc(y_added, 1)
                    if s % NBLK == NBLK - 1 and not last:
                        pool.wait_ge(g_in[j], i * 16 + 32)
                        pool.wait_ge(cwx_made, i * GSTEPS + (j + 1) * NBLK)
                        own_split(own, i, j)

            def own_split(own, i, j):
                src = g_raw1[j][:, :, :].rearrange("p e h -> p (e h)")
                pool.nop().then_inc(pool_passed, 1)
                own(pool.tensor_scalar(g_hi[j][:, :], src, 1.0, 0.0, ALU.mult, ALU.add))
                own(pool.tensor_tensor(g_lo[j][:, :], src, g_hi[j][:, :].bitcast(F32), ALU.subtract))
                own(pool.tensor_copy(sel_now[j][:, :], sel[:, bass.ds((i * GPI + GPI + j) * P, P)]))
                pool.nop().then_inc(g_split, 1)

            pool.nop().then_inc(y_added, RING)
            with pool.Fori(0, NG // GPI - 1) as i:
                group_turn(i, False)
            group_turn(NG // GPI - 1, True)
            pool.nop().then_inc(y_done, 1)

        @block.scalar
        def _(act):
            act.wait_ge(var_ready, 1)
            act.activation(nrm[:, 1, :], nrm[:, 0, :], ACT.Sqrt).then_inc(root_ready, 1)
            own = Chain(act, act_own)
            act.wait_ge(small_turned, 1)
            own(act.activation(vec_t[:, :], ps[7][:, 0:N_VEC], ACT.Copy))
            own(act.activation(turn_hi[:, 0, 0:3 * E0], ps[7][:, P:P + 3 * E0], ACT.Copy))
            own(act.activation(turn_hi[:, 1, :], ps[7][:, 2 * P:3 * P], ACT.Copy))
            act.nop().then_inc(small_hi, 1)
            act.wait_ge(var_ready, 2)
            act.activation(nrm[:, 4, :], nrm[:, 3, :], ACT.Sqrt).then_inc(root_ready, 1)
            for b in range(NBLK):
                act.wait_ge(turned, b + 1)
                act.activation(blk(xn_hi, b), ps[b][:, :], ACT.Copy).then_inc(hi_ready, 1)

            def copy_w1(j, before):
                act.wait_ge(e_turned, before + 1)
                own(act.activation(e_t[j][:, :].rearrange("p (n f) -> p n f", f=F), psum[:, 6:8, 0:F], ACT.Copy))
                act.nop().then_inc(e_copied, 1)

            def copy_w2(j, before, bank):
                act.wait_ge(e_turned, before + 2)
                own(act.activation(e_w2_t[j][:, 0:2, :], ps[bank][:, 0:2 * P].rearrange("p (c d) -> p c d", d=P),
                                   ACT.Copy))
                own(act.activation(e_w2_t[j][0:FT[2][1], 2, :], ps[bank][0:FT[2][1], 2 * P:3 * P], ACT.Copy))
                act.nop().then_inc(e_copied, 1)

            act.wait_ge(consts_ready, 2)
            for b in range(NBLK):
                act.wait_ge(qkv_t_made, b + 1)
                act.activation(blk(qkv_t, b), ps[b][0:3 * E0, :], ACT.Copy).then_inc(qkv_t_copied, 1)
            act.nop().then_inc(silu_done, 2)
            act.nop().then_inc(att_act, 1)
            copy_w1(0, 0)
            copy_w2(0, 0, 4)
            act.wait_ge(r0_arg, 1)
            act.activation(pair[:, :, :], pair[:, :, :], ACT.Exp).then_inc(r0_exp, 1)
            act.wait_ge(rms_ready, 1)
            act.wait_ge(tok_ready, NT)
            for t in range(NT):
                act.activation(xr_tok[:, t, :], xn_tok[:, t, :], ACT.Copy, scale=nrm[:, 5, t:t + 1]
                               ).then_inc(tok_ready, 1)
            copy_w1(1, 2)
            copy_w2(1, 2, 5)
            for b in range(NBLK):
                act.wait_ge(turned, NBLK + b + 1)
                act.activation(blk(xr_hi, b), ps[4 + b][:, :], ACT.Identity,
                               scale=vec_t[:, V_RMS:V_RMS + 1]).then_inc(hi_ready, 1)
            act.wait_ge(r0_arg, 2)
            act.activation(rsm[:, 1, :, :], rsm[:, 1, :, :], ACT.Exp).then_inc(r0_exp, 1)
            act.wait_ge(late_in, 16 * 8)
            own(act.activation(ssm_a[:, :], ssm_raw[:, 0, :], ACT.Exp))
            own(act.activation(ssm_a[:, :], ssm_a[:, :], ACT.Copy, scale=-1.0))
            own(act.activation(b1_half[:, :], vec_t[:, V_B1:V_B1 + NG], ACT.Copy, scale=0.5))

            n0 = own.n

            def turn(i, last):
                nonlocal own
                att = Chain(act, att_act, i * N_ATT_ACT + 1)
                own = Chain(act, act_own, i * 3 * EPI + n0)

                def pe_step(n):
                    act.wait_ge(att_pe, i * N_ATT_PE + n)

                def dve_step(n):
                    act.wait_ge(att_dve, i * N_ATT_DVE + 1 + n)

                def attention(s):
                    if s == 2:
                        pe_step(2)
                        att(act.activation(A["k"], ps[6][:, :], ACT.Copy))
                    if s == 5:
                        pe_step(3)
                        att(act.activation(A["ar"], ps[6][:, :], ACT.Copy))
                        att(act.activation(A["sq"], A["ar"], ACT.Square))
                    if s == 6:
                        pe_step(4)
                        att(act.activation(A["ai"], ps[7][:, :], ACT.Copy))
                        att(act.activation(A["m2"], A["ai"], ACT.Square))
                        att(act.activation(A["neg"], A["ar"], ACT.Abs))
                    if s == 8:
                        pe_step(5)
                        dve_step(3)
                        att(act.activation(A["sq"], ps[6][:, :], ACT.Silu))
                        att(act.activation(A["mag"], A["m2"], ACT.Sqrt))
                    if s == 9:
                        pe_step(6)
                        att(act.activation(A["q"], ps[7][:, :], ACT.Copy))
                    if s == 11:
                        att(act.activation(A["decay"], A["mag"], ACT.Sigmoid))
                        dve_step(7)
                        att(act.activation(A["theta"], A["k"], ACT.Arctan))
                    if s == 17:
                        dve_step(17)
                        att(act.activation(A["m2"], A["theta"], ACT.Abs))
                        att(act.activation(A["mag"], A["theta"], ACT.Sin, scale=math.pi))
                        att(act.activation(A["k"], A["m2"], ACT.Sin, scale=-math.pi, bias=half_pi[:, 0:1]))
                        att(act.activation(A["theta"], A["mag"], ACT.Square))
                        att(act.activation(A["m2"], A["theta"], ACT.Copy, scale=-2.0, bias=1.0))

                for s in range(STEPS):
                    M = FT[s % NF][1]
                    act.wait_ge(a_made, i * STEPS + s + 1)
                    act.wait_ge(gated, i * STEPS + s + 1)
                    act.activation(sil[0:M, s % 2, :], ps[s % 2][0:M, :], ACT.Silu).then_inc(silu_done, 1)
                    attention(s)
                    if last:
                        continue
                    copied = (i + 1) * 2 * EPI
                    if s == 12:
                        act.wait_ge(e_split, i * EPI + 1)
                        copy_w1(0, copied)
                    if s == 15:
                        act.wait_ge(w2_ready, i * EPI + 1)
                        copy_w2(0, copied, 6)
                    if s == 18:
                        act.wait_ge(e_split, i * EPI + 2)
                        copy_w1(1, copied + 2)
                    if s == 21:
                        act.wait_ge(w2_ready, i * EPI + 2)
                        copy_w2(1, copied + 2, 7)
                assert att.n == N_ATT_ACT

            with act.Fori(0, NB - 1) as i:
                turn(i, False)
            turn(NB - 1, True)
            own = Chain(act, act_own, n0 + (NB - 1) * 3 * EPI)

            act.activation(warm[:, 0:1], half_pi[:, :], ACT.Sqrt)
            act.wait_ge(var_ready, 3)
            act.activation(nrm[:, 1, :], nrm[:, 0, :], ACT.Sqrt).then_inc(root_ready, 1)
            act.activation(warm[:, 1:2], half_pi[:, :], ACT.Exp)
            for b in range(NBLK):
                act.wait_ge(turned, 2 * NBLK + b + 1)
                own(act.activation(blk(u_t, b), ps[b][:, :], ACT.Copy))
                act.activation(blk(xn_hi, b), blk(u_t, b), ACT.Copy).then_inc(hi_ready, 1)
            for b in range(NBLK):
                act.wait_ge(dt_made, b + 1)
                own(act.activation(blk(dt_t, b), ps[4 + b][:, :], ACT.Identity, bias=vec_t[:, V_BDT:V_BDT + 1]))
                act.nop().then_inc(dt_left, 1)
            def copy_cw(b):
                act.wait_ge(cw_split, b + 1)
                if b >= 2:
                    act.wait_ge(b2_used, b - 1)
                act.activation(cw_b2[:, b % 2, :], ps[b % 2][0:E1, :], ACT.Copy, scale=2.0).then_inc(cw_copied, 1)

            for c in range(NSH * NBLK):
                k, tb = divmod(c, NBLK)
                if c == NBLK:
                    act.wait_ge(r1_arg, 1)
                    act.activation(pair[:, :, :], pair[:, :, :], ACT.Exp).then_inc(r1_exp, 1)
                    for b in range(NBLK):
                        e = softplus_bufs[b][0]
                        own(act.activation(e[:, :], blk(dt_t, b), ACT.Abs))
                        own(act.activation(e[:, :], e[:, :], ACT.Exp, scale=-1.0))
                        act.nop().then_inc(sp_exp, 1)
                    for b in range(NBLK):
                        e, l, _ = softplus_bufs[b]
                        act.activation(l[:, :], e[:, :], ACT.Ln, bias=1.0).then_inc(sp_log, 1)
                for b, at_step in enumerate(CW_STEPS):
                    if c == at_step:
                        copy_cw(b)
                act.wait_ge(sh_made, c + 1)
                if c >= 2:
                    act.wait_ge(sh_used, c - 1)
                act.activation(hid[:, c % 2, 2, :], ps[2 + c % 2][:, :], ACT.Silu,
                               bias=vec_t[:, V_SB1 + k:V_SB1 + k + 1]).then_inc(sh_silu, 1)

            act.activation(warm[:, 2:3], half_pi[:, :], ACT.Exp)
            act.nop().then_inc(tanh_done, 2)
            act.nop().then_inc(weighted, RING)

            def decay(i, s):
                act.wait_ge(scanned, i * GSTEPS + s + 1)
                act.nop().then_inc(act_passed, 1)
                act.activation(decay_ring[s % RING][:, :], blk(dt_t, s % NBLK), ACT.Exp,
                               scale=ssm_a[:, bass.ds(i * GPI + s // NBLK, 1)]).then_inc(decay_ready, 1)

            def group_turn(i, last):
                for s in range(GSTEPS):
                    g = i * GPI + s // NBLK
                    act.wait_ge(h_made, i * GSTEPS + s + 1)
                    act.wait_ge(c1_done, i * GSTEPS + s + 1)
                    act.nop().then_inc(act_passed, 1)
                    act.activation(sil[:, s % 2, :], ps[s % 2][:, :], ACT.Tanh, scale=0.5,
                                   bias=b1_half[:, bass.ds(g, 1)]).then_inc(tanh_done, 1)
                    if s + 2 < GSTEPS:
                        decay(i, s + 2)
                    elif not last:
                        decay(i + 1, s + 2 - GSTEPS)
                    act.wait_ge(scanned, i * GSTEPS + s + 1 + RING)
                    act.wait_ge(y_added, i * GSTEPS + s + 1)
                    act.nop().then_inc(act_passed, 1)
                    act.activation(term_ring[s % RING][:, :], state_ring[s % RING][:, :], ACT.Copy,
                                   scale=ssm_cb[:, bass.ds(g, 1)]).then_inc(weighted, 1)

            act.wait_ge(win_ready, NBLK)
            for s in range(2):
                decay(0, s)
            with act.Fori(0, NG // GPI - 1) as i:
                group_turn(i, False)
            group_turn(NG // GPI - 1, True)

        @block.vector
        def _(dve):
            own = Chain(dve, dve_own)

            def norm_stats(layer, done=0):
                for t in range(done, NT):
                    if layer == 0 and t % TPB == 0:
                        dve.wait_ge(x_in[t // TPB], 16)
                    dve.bn_stats(stats[:, t, :], res[:, t, :]).then_inc(dve_own, 1)
                own.n += NT - done
                own.wait()
                for t in range(done, NT):
                    dve.bn_aggr(mv[:, t, :], stats[:, t, :]).then_inc(dve_own, 1)
                own.n += NT - done
                own.wait()
                own(dve.tensor_scalar(nrm[:, 0, :], mv[:, :, 1], LN_EPS, None, ALU.add))
                dve.nop().then_inc(var_ready, 1)

            norm_stats(0)
            dve.wait_ge(root_ready, 1)
            own(dve.reciprocal(nrm[:, 2, :], nrm[:, 1, :]))
            own(dve.tensor_tensor(nrm[:, 3, :], mv[:, :, 1], nrm[:, 2, :], ALU.mult))
            own(dve.tensor_tensor(nrm[:, 3, :], nrm[:, 3, :], nrm[:, 2, :], ALU.mult))
            own(dve.tensor_scalar(nrm[:, 3, :], nrm[:, 3, :], RMS_EPS, None, ALU.add))
            dve.nop().then_inc(var_ready, 1)
            for t in range(NT):
                dve.tensor_scalar(xn_tok[:, t, :], res[:, t, :], mv[:, t, 0:1], nrm[:, 2, t:t + 1],
                                  ALU.subtract, ALU.mult).then_inc(tok_ready, 1)
            dve.wait_ge(small_turned, 1)
            dve.wait_ge(small_hi, 1)
            own(dve.tensor_tensor(turn_lo[:, 0, 0:3 * E0], ps[7][:, P:P + 3 * E0],
                                  turn_hi[:, 0, 0:3 * E0].bitcast(F32), ALU.subtract))
            own(dve.tensor_tensor(turn_lo[:, 1, :], ps[7][:, 2 * P:3 * P], turn_hi[:, 1, :].bitcast(F32),
                                  ALU.subtract))
            own(dve.tensor_tensor(sb2_sum[:, :], vec_t[:, V_SB2:V_SB2 + 1], vec_t[:, V_SB2 + 1:V_SB2 + 2], ALU.add))
            dve.nop().then_inc(small_copied, 1)
            for b in range(NBLK):
                dve.wait_ge(hi_ready, b + 1)
                dve.tensor_tensor(blk(xn_lo, b), ps[b][:, :], blk(xn_hi, b).bitcast(F32), ALU.subtract
                                  ).then_inc(lo_ready, 1)
            dve.wait_ge(qkv_made, 1)
            own(dve.tensor_copy(qkv[:, :, :].rearrange("p t c -> p (t c)"), ps[0][:, 0:NT * 3 * E0]))
            dve.nop().then_inc(qkv_copied, 1)
            dve.nop().then_inc(gated, 2)
            dve.nop().then_inc(att_dve, 1)
            def over_e(a):
                return a[:, :, :, None].to_broadcast([P, NT, E0, E0])

            def over_j(a):
                return a[:, :, None, :].to_broadcast([P, NT, E0, E0])

            pr = pair[:, :, :].rearrange("p t (e j) -> p t e j", j=E0)
            q, k, v = (qkv[:, :, n * E0:(n + 1) * E0] for n in range(3))
            lg, ex, den, chosen = (rsm[:, n, :, :] for n in range(4))
            own(dve.tensor_tensor(pr, over_e(q), over_j(k), ALU.mult))
            own(dve.tensor_reduce(den, pr, AX, ALU.max))
            own(dve.tensor_tensor(pr, pr, over_e(den), ALU.subtract))
            dve.nop().then_inc(r0_arg, 1)
            dve.wait_ge(root_ready, 2)
            own(dve.reciprocal(nrm[:, 5, :], nrm[:, 4, :]))
            dve.nop().then_inc(rms_ready, 1)
            dve.wait_ge(r0_exp, 1)
            own(dve.tensor_reduce(den, pr, AX, ALU.add))
            own(dve.tensor_tensor(pr, pr, over_j(v), ALU.mult))
            own(dve.tensor_reduce(lg, pr, AX, ALU.add))
            own(dve.reciprocal(den, den))
            own(dve.tensor_tensor(lg, lg, den, ALU.mult))
            best, rest = den, chosen
            for t in range(NT):
                dve.max(best[:, t, :], lg[:, t, :]).then_inc(dve_own, 1)
            own.n += NT
            own.wait()
            own(dve.tensor_tensor(ex, lg, best[:, :, 0:1].to_broadcast([P, NT, E0]), ALU.subtract))
            dve.nop().then_inc(r0_arg, 1)
            own(dve.memset(best[:, :, TOPK:E0], 3.0e38))
            for t in range(NT):
                dve.match_replace(rest[:, t, :], best[:, t, :], lg[:, t, :], -3.0e38).then_inc(dve_own, 1)
            own.n += NT
            own.wait()
            own(dve.tensor_tensor(chosen, lg, rest, ALU.not_equal))
            for b in range(NBLK):
                dve.wait_ge(hi_ready, NBLK + b + 1)
                dve.scalar_tensor_tensor(blk(xr_lo, b), ps[4 + b][:, :], vec_t[:, V_RMS:V_RMS + 1],
                                         blk(xr_hi, b).bitcast(F32), ALU.mult, ALU.subtract).then_inc(lo_ready, 1)
            dve.wait_ge(r0_exp, 2)
            own(dve.tensor_tensor(ex, ex, chosen, ALU.mult))
            own(dve.tensor_reduce(rrow[:, 1, :], ex, AX, ALU.add))
            own(dve.reciprocal(rrow[:, 2, :], rrow[:, 1, :]))
            own(dve.tensor_tensor(score0[:, :, :], ex, rrow[:, 2, :, None].to_broadcast([P, NT, E0]), ALU.mult))

            dve.nop().then_inc(o_added, 2)
            def gate(i, s):
                tb, ft = divmod(s % (NBLK * NF), NF)
                M = FT[ft][1]
                dve.wait_ge(g_made, i * STEPS + s + 1)
                dve.wait_ge(silu_done, i * STEPS + s + 3)
                dve.wait_ge(o_made, i * OUTS + s // NF + 1)
                dve.tensor_tensor(hid[0:M, tb % 2, ft, :], sil[0:M, s % 2, :], ps[2 + s % 2][0:M, :],
                                  ALU.mult).then_inc(gated, 1)

            def turn(i, last):
                att = Chain(dve, att_dve, i * N_ATT_DVE + 1)

                def pe_step(n):
                    dve.wait_ge(att_pe, i * N_ATT_PE + n)

                def act_step(n):
                    dve.wait_ge(att_act, i * N_ATT_ACT + 1 + n)

                def pool_step(n):
                    dve.wait_ge(att_pool, i * N_ATT_POOL + n)

                def attention(s):
                    if s == 2:
                        pe_step(1)
                        act_step(1)
                        att(dve.tensor_tensor(A["kv"], ps[7][:, :], A["k"], ALU.mult))
                    if s == 6:
                        act_step(5)
                        att(dve.tensor_tensor(A["m2"], A["m2"], A["sq"], ALU.add))
                        att(dve.tensor_scalar(A["m2"], A["m2"], 2.0 ** -110, 2.0 ** 117, ALU.max, ALU.min))
                    if s == 9:
                        act_step(8)
                        att(dve.tensor_tensor(A["k"], A["neg"], A["mag"], ALU.add))
                        att(dve.reciprocal(A["m2"][:, 0:TB // 2], A["k"][:, 0:TB // 2]))
                    if s == 10:
                        att(dve.reciprocal(A["m2"][:, TB // 2:TB], A["k"][:, TB // 2:TB]))
                        att(dve.tensor_tensor(A["k"], A["ai"], A["m2"], ALU.mult))
                    if s == 12:
                        att(dve.tensor_scalar(A["neg"], A["ar"], 0.0, -2.0, ALU.is_lt, ALU.mult))
                        att(dve.tensor_scalar(A["m2"], A["neg"], 1.0, 1.0 / math.pi, ALU.add, ALU.mult))
                        act_step(11)
                        att(dve.tensor_tensor(A["theta"], A["theta"], A["m2"], ALU.mult))
                        att(dve.scalar_tensor_tensor(A["theta"], A["neg"], -0.25, A["theta"], ALU.mult, ALU.add))
                    if s == 13:
                        att(dve.tensor_scalar(A["ar"], A["theta"], ROUND_TURN, ROUND_TURN, ALU.add, ALU.subtract))
                        att(dve.tensor_tensor_scan(A["k"], ones[:, :], A["ar"], 0.0, ALU.mult, ALU.add))
                    if s == 14:
                        pool_step(2)
                        att(dve.tensor_tensor_scan(A["theta"], ones[:, :], A["ai"], 0.0, ALU.mult, ALU.add))
                    if s == 15:
                        att(dve.tensor_scalar(A["ar"], A["k"], ROUND_INT, ROUND_INT, ALU.add, ALU.subtract))
                        att(dve.tensor_tensor(A["k"], A["k"], A["ar"], ALU.subtract))
                        att(dve.tensor_tensor(A["theta"], A["k"], A["theta"], ALU.add))
                    if s == 17:
                        act_step(16)
                        att(dve.scalar_tensor_tensor(A["neg"], A["mag"], 2.0, A["k"], ALU.mult, ALU.mult))
                    if s == 18:
                        att(dve.tensor_tensor(A["k"], A["kv"], A["m2"], ALU.mult))
                    if s == 19:
                        pool_step(3)
                        att(dve.tensor_tensor_scan(A["ai"], A["decay"], A["mag"], 0.0, ALU.mult, ALU.add))
                        att(dve.tensor_tensor_scan(A["ar"], A["decay"], A["k"], 0.0, ALU.mult, ALU.add))
                    if s == 20:
                        att(dve.tensor_tensor(A["ar"], A["ar"], A["m2"], ALU.mult))
                    if s == 21:
                        pool_step(4)
                        att(dve.tensor_tensor(A["ar"], A["ar"], A["ai"], ALU.add))
                        att(dve.tensor_tensor(A["kv"], A["ar"], A["q"], ALU.mult))
                    if s == STEPS:
                        pe_step(7)
                        dve.wait_ge(o_added, i * OUTS + OUTS + 1)
                        r = res[:, bass.ds(i * TPB, TPB), :].rearrange("p t d -> p (t d)")
                        att(dve.tensor_tensor(r, r, ps[6][:, :], ALU.add))

                def add_output(o):
                    j, tb = divmod(o, NBLK)
                    dve.wait_ge(o_made, i * OUTS + o + 3)
                    dve.wait_ge(o_added, i * OUTS + o + 1)
                    for n in range(TPB):
                        t = tb * TPB + n
                        ins = dve.scalar_tensor_tensor(
                            res[:, t, :], ps[4 + o % 2][:, n * P:(n + 1) * P],
                            score0[:, t, bass.ds(i * EPI + j, 1)], res[:, t, :], ALU.mult, ALU.add)
                    ins.then_inc(o_added, 1)

                for s in range(2, STEPS):
                    gate(i, s)
                    if s % NF == 2 and s >= 5:
                        add_output((s - 5) // NF)
                    attention(s)
                if last:
                    done = (NBLK - 1) * TPB
                    dve.wait_ge(o_added, NB * OUTS + 1)
                    for t in range(done):
                        dve.bn_stats(stats[:, t, :], res[:, t, :]).then_inc(dve_own, 1)
                    own.n += done
                    own.wait()
                    for t in range(done):
                        dve.bn_aggr(mv[:, t, :], stats[:, t, :]).then_inc(dve_own, 1)
                    own.n += done
                if not last:
                    gate(i + 1, 0)
                attention(STEPS)
                if not last:
                    gate(i + 1, 1)
                add_output(OUTS - 1)
                assert att.n == N_ATT_DVE

            for s in range(2):
                gate(0, s)
            with dve.Fori(0, NB - 1) as i:
                turn(i, False)
            turn(NB - 1, True)

            dve.wait_ge(o_added, NB * OUTS + 2)
            own.wait()
            norm_stats(1, (NBLK - 1) * TPB)
            dve.wait_ge(root_ready, 3)
            own(dve.reciprocal(nrm[:, 2, :], nrm[:, 1, :]))
            for t in range(NT):
                dve.tensor_scalar(xn_tok[:, t, :], res[:, t, :], mv[:, t, 0:1], nrm[:, 2, t:t + 1],
                                  ALU.subtract, ALU.mult).then_inc(tok_ready, 1)
            for b in range(NBLK):
                dve.wait_ge(hi_ready, 2 * NBLK + b + 1)
                dve.tensor_tensor(blk(xn_lo, b), blk(u_t, b), blk(xn_hi, b).bitcast(F32), ALU.subtract
                                  ).then_inc(lo_ready, 1)
            dve.wait_ge(late_in, 16 * 8)
            top = rsm[:, 0, :, :]
            for b in range(NBLK):
                dve.wait_ge(lg_made, b + 1)
                if b >= 2:
                    dve.wait_ge(logits_made, b - 1)
                dve.tensor_scalar(cw_b2[:, b % 2, :], ps[b][0:E1, :], rbias[:, 0:1], None, ALU.add
                                  ).then_inc(lg_biased, 1)
            logits = psum[:, 0:2, :].rearrange("p b (t e) -> p (b t) e", e=E1)
            dve.wait_ge(logits_made, NBLK)
            for t in range(NT):
                dve.max(top[:, t, :], logits[:, t, :]).then_inc(dve_own, 1)
            own.n += NT
            own.wait()
            for t in range(NT):
                dve.match_replace(pair2[:, t, :], top[:, t, :], logits[:, t, :], -3.0e38).then_inc(dve_own, 1)
            own.n += NT
            own.wait()
            own(dve.tensor_tensor(pair2[:, :, :], logits, pair2[:, :, :], ALU.not_equal))
            own(dve.tensor_tensor(pair[:, :, :], logits, top[:, :, 0:1].to_broadcast([P, NT, E1]), ALU.subtract))
            dve.nop().then_inc(r1_arg, 1)
            dve.wait_ge(r1_exp, 1)
            own(dve.tensor_tensor(pair[:, :, :], pair[:, :, :], pair2[:, :, :], ALU.mult))
            own(dve.tensor_reduce(rrow[:, 0, :], pair[:, :, :], AX, ALU.add))
            own(dve.reciprocal(rrow[:, 1, :], rrow[:, 0, :]))
            own(dve.tensor_scalar(rrow[:, 1, :], rrow[:, 1, :], 0.5, None, ALU.mult))
            dve.wait_ge(turned, 3 * NBLK)
            for n in range(2):
                own(dve.tensor_tensor(xn_tok[:, :, n * E1:(n + 1) * E1], pair[:, :, :],
                                      rrow[:, 1, :, None].to_broadcast([P, NT, E1]), ALU.mult))
            dve.nop().then_inc(cw_ready, 1)

            def split_cw(b):
                dve.wait_ge(cw_turned, b + 1)
                own(dve.tensor_copy(blk(cw_hl, b), ps[b % 2][:, :]))
                low = cw_hl[E1:P, b * TB:(b + 1) * TB]
                own(dve.tensor_tensor(low, ps[b % 2][E1:P, :], low.bitcast(F32), ALU.subtract))
                dve.nop().then_inc(cw_split, 1)

            def softplus(b):
                e, l, p = softplus_bufs[b]
                mask = at["theta"]
                dve.wait_ge(sp_log, b + 1)
                if b < POOL_LOGS:
                    dve.wait_ge(sp_poly, b + 1)
                own(dve.tensor_scalar(mask[:, :], e[:, :], 2.0 ** -6, None, ALU.is_lt))
                own(dve.copy_predicated(l[:, :], mask[:, :].bitcast(mybir.dt.uint32), p[:, :]))
                own(dve.scalar_tensor_tensor(blk(dt_t, b), blk(dt_t, b), 0.0, l[:, :], ALU.max, ALU.add))
                own(dve.tensor_tensor(blk(win_t, b), blk(dt_t, b), blk(u_t, b), ALU.mult))
                dve.nop().then_inc(win_ready, 1)

            for b in range(NBLK):
                split_cw(b)
            for b in range(POOL_LOGS, NBLK):
                e, _, p = softplus_bufs[b]
                dve.wait_ge(sp_exp, b + 1)
                own(dve.tensor_scalar(p[:, :], e[:, :], -1.0 / 4, None, ALU.mult))
                for c in (1.0 / 3, -1.0 / 2, 1.0):
                    own(dve.scalar_tensor_tensor(p[:, :], p[:, :], c, e[:, :], ALU.add, ALU.mult))
            for b in range(NBLK):
                softplus(b)

            dve.nop().then_inc(c1_done, 2)
            dve.nop().then_inc(hid_done, 2)
            dve.nop().then_inc(scanned, RING)

            def scan(i, s):
                dve.wait_ge(decay_ready, i * GSTEPS + s + 1)
                dve.wait_ge(weighted, i * GSTEPS + s + 1)
                dve.tensor_tensor_scan(state_ring[s % RING][:, :], decay_ring[s % RING][:, :],
                                       blk(win_t, s % NBLK), 0.0, ALU.mult, ALU.add).then_inc(scanned, 1)

            def group_turn(i, last):
                for s in range(GSTEPS):
                    g = i * GPI + s // NBLK
                    c = i * GSTEPS + s
                    dve.wait_ge(tanh_done, c + 3)
                    dve.wait_ge(cwx_made, c + 1)
                    dve.wait_ge(hid_done, c + 1)
                    dve.scalar_tensor_tensor(c1_ring[s % 2], sil[:, s % 2, :], 1.0, ps[2 + s % 2][:, :],
                                             ALU.add, ALU.mult).then_inc(c1_done, 1)
                    if s + 1 < GSTEPS:
                        scan(i, s + 1)
                    elif not last:
                        scan(i + 1, 0)
                    dve.wait_ge(c1_done, c + 3)
                    dve.wait_ge(g_out, c + 1)
                    dve.scalar_tensor_tensor(hid_ring[s % 2], ps[s % 2][:, :], vec_t[:, bass.ds(g + V_B1, 1)],
                                             c1_ring[s % 2], ALU.add, ALU.mult).then_inc(hid_done, 1)

            scan(0, 0)
            with dve.Fori(0, NG // GPI - 1) as i:
                group_turn(i, False)
            group_turn(NG // GPI - 1, True)

            dve.wait_ge(g_out, NG * NBLK + 2)
            dve.wait_ge(y_done, 1)
            for b in range(NBLK):
                own(dve.scalar_tensor_tensor(blk(y_t, b), ps[4 + b][:, :], sb2_sum[:, 0:1], blk(y_t, b),
                                             ALU.add, ALU.add))
                dve.nop().then_inc(sum_ready, 1)
            for b in range(NBLK):
                dve.wait_ge(sum_turned, b + 1)
                r = res[:, b * TPB:(b + 1) * TPB, :].rearrange("p t d -> p (t d)")
                dve.tensor_tensor(r, r, ps[b][:, :], ALU.add).then_inc(x2_ready, 1)

        @block.tensor
        def _(pe):
            pe.wait_ge(consts_ready, 1)
            pe.wait_ge(turn_in, 16 * 8)
            pe.transpose(ps[7][:, 0:N_VEC], vec_raw[:, :], ident[0:N_VEC, 0:N_VEC])
            pe.transpose(ps[7][:, P:P + 3 * E0], turn_raw[0:3 * E0, 0, :], ident[0:3 * E0, 0:3 * E0])
            pe.transpose(ps[7][:, 2 * P:3 * P], turn_raw[:, 1, :], ident[:, :]).then_inc(small_turned, 1)

            def turn_tiles(src, bank, first):
                for t in range(NT):
                    pe.wait_ge(tok_ready, first + t + 1)
                    ins = pe.transpose(ps[bank + t // TPB][:, (t % TPB) * P:(t % TPB + 1) * P], src[:, t, :], ident[:, :])
                    if t % TPB == TPB - 1:
                        ins.then_inc(turned, 1)

            turn_tiles(xn_tok, 0, 0)
            def turn_w1(j, loads):
                pe.wait_ge(e_in[j], loads)
                for half in range(2):
                    for n, (f0, m) in enumerate(FT):
                        ins = pe.transpose(ps[6 + half][:, f0:f0 + m], e_raw1[j][0:m, half * NF + n, :],
                                           ident[0:m, 0:m])
                ins.then_inc(e_turned, 1)

            def turn_w2(j, before, bank):
                pe.wait_ge(e_copied, before + 1)
                for n, (f0, m) in enumerate(FT):
                    ins = pe.transpose(ps[bank][0:m, n * P:(n + 1) * P], e_raw2[j][:, f0:f0 + m], ident[:, :])
                ins.then_inc(e_turned, 1)

            pe.wait_ge(small_copied, 1)
            for b in range(NBLK):
                pe.wait_ge(hi_ready, b + 1)
                pe.wait_ge(lo_ready, b + 1)
                product(pe, ps[b][0:3 * E0, :], turn_hi[:, 0, 0:3 * E0], turn_lo[:, 0, 0:3 * E0],
                        blk(xn_hi, b), blk(xn_lo, b)).then_inc(qkv_t_made, 1)
            for t in range(NT):
                pe.wait_ge(qkv_t_copied, t // TPB + 1)
                ins = pe.transpose(ps[0][:, t * 3 * E0:(t + 1) * 3 * E0], qkv_t[:, t * P:(t + 1) * P],
                                   ident[0:3 * E0, 0:3 * E0])
            ins.then_inc(qkv_made, 1)
            turn_w1(0, 80)
            turn_w2(0, 0, 4)
            pe.wait_ge(e_copied, 1)
            turn_w1(1, 80)
            turn_w2(1, 2, 5)
            pe.wait_ge(e_copied, 2 * EPI)
            turn_tiles(xr_tok, 4, NT)

            def hidden(i, s):
                j, r = divmod(s, NBLK * NF)
                tb, ft = divmod(r, NF)
                f0, m = FT[ft]
                if r == 0:
                    pe.wait_ge(e_split, i * EPI + j + 1)
                pe.wait_ge(silu_done, i * STEPS + s + 1)
                product(pe, ps[s % 2][0:m, :], e_hi[j][:, f0:f0 + m], e_lo[j][:, f0:f0 + m],
                        blk(xn_hi, tb), blk(xn_lo, tb)).then_inc(a_made, 1)
                pe.wait_ge(gated, i * STEPS + s + 1)
                product(pe, ps[2 + s % 2][0:m, :], e_hi[j][:, F + f0:F + f0 + m], e_lo[j][:, F + f0:F + f0 + m],
                        blk(xn_hi, tb), blk(xn_lo, tb)).then_inc(g_made, 1)

            def output(i, o, tiles):
                j, tb = divmod(o, NBLK)
                if tb == 0:
                    pe.wait_ge(w2_ready, i * EPI + j + 1)
                pe.wait_ge(gated, i * STEPS + o * NF + NF + 2)
                pe.wait_ge(o_added, i * OUTS + o + 1)
                for n in tiles:
                    for ft, (f0, m) in enumerate(FT):
                        ins = pe.matmul(ps[4 + o % 2][:, n * P:(n + 1) * P],
                                        hid[0:m, tb % 2, ft, n * P:(n + 1) * P], e_w2[j][0:m, ft, :],
                                        start=(ft == 0), stop=(ft == NF - 1))
                if TPB - 1 in tiles:
                    ins.then_inc(o_made, 1)

            def attention(i, s, last):
                def project(n, bank):
                    product(pe, ps[bank][:, :], proj_hi[:, n, :], proj_lo[:, n, :],
                            xr_hi[:, bass.ds(i * TB, TB)], xr_lo[:, bass.ds(i * TB, TB)]).then_inc(att_pe, 1)

                def act_step(n):
                    pe.wait_ge(att_act, i * N_ATT_ACT + 1 + n)

                def dve_step(n):
                    pe.wait_ge(att_dve, i * N_ATT_DVE + 1 + n)

                copied = (i + 1) * 2 * EPI
                if s == 0:
                    act_step(0)
                    pe.wait_ge(e_copied, copied)
                    project(1, 7)
                if s == 1:
                    dve_step(0)
                    project(0, 6)
                if s == 3:
                    act_step(1)
                    project(2, 6)
                if s == 4:
                    dve_step(1)
                    project(3, 7)
                if s == 6:
                    act_step(2)
                    project(4, 6)
                if s == 7:
                    act_step(4)
                    project(5, 7)
                if not last:
                    if s == 10:
                        act_step(9)
                        turn_w1(0, i * 80 + 160)
                    if s == 13:
                        turn_w2(0, copied, 6)
                    if s == 16:
                        pe.wait_ge(e_copied, copied + 2)
                        turn_w1(1, i * 80 + 160)
                    if s == 19:
                        turn_w2(1, copied + 2, 7)
                if s == 23:
                    act_step(7)
                    dve_step(24)
                    if not last:
                        pe.wait_ge(e_copied, copied + 3)
                    for n in range(TPB):
                        ins = pe.matmul(ps[6][:, n * P:(n + 1) * P], at["kv"][:, n * P:(n + 1) * P], wo_sb[:, :],
                                        start=True, stop=True)
                    ins.then_inc(att_pe, 1)

            pe.wait_ge(qkv_copied, 1)
            pe.nop().then_inc(o_made, 2)
            AHEAD = 2
            for s in range(AHEAD):
                hidden(0, s)
            pe.wait_ge(weights_split, 1)
            pe.wait_ge(hi_ready, 2 * NBLK)
            pe.wait_ge(lo_ready, 2 * NBLK)

            def turn(i, last):
                for s in range(STEPS):
                    attention(i, s, last)
                    if s + AHEAD < STEPS:
                        hidden(i, s + AHEAD)
                    elif not last:
                        hidden(i + 1, s + AHEAD - STEPS)
                    if s % NF == NF - 1:
                        output(i, s // NF, range(TPB // 2))
                    if s % NF == 0 and s > 0:
                        output(i, s // NF - 1, range(TPB // 2, TPB))
                    if s == STEPS - 1:
                        output(i, OUTS - 1, range(TPB // 2, TPB))

            with pe.Fori(0, NB - 1) as i:
                turn(i, False)
            turn(NB - 1, True)

            turn_tiles(xn_tok, 0, 2 * NT)
            pe.wait_ge(weights_split, 2)
            pe.wait_ge(late_in, 16 * 8)
            for b in range(NBLK):
                pe.wait_ge(hi_ready, 2 * NBLK + b + 1)
                pe.wait_ge(lo_ready, 2 * NBLK + b + 1)
                product(pe, ps[b][0:E1, :], rout_hi[:, :], rout_lo[:, :], blk(xn_hi, b), blk(xn_lo, b)
                        ).then_inc(lg_made, 1)
                product(pe, ps[4 + b][:, :], turn_hi[:, 1, :], turn_lo[:, 1, :], blk(xn_hi, b), blk(xn_lo, b)
                        ).then_inc(dt_made, 1)
            for b in range(NBLK):
                pe.wait_ge(lg_biased, b + 1)
                for n in range(TPB):
                    t = b * TPB + n
                    ins = pe.transpose(ps[t // 8][:, (t % 8) * E1:(t % 8 + 1) * E1],
                                       cw_b2[:, b % 2, n * P:(n + 1) * P], ident[0:E1, 0:E1])
                ins.then_inc(logits_made, 1)

            def shared_in(c):
                k, tb = divmod(c, NBLK)
                e, n = divmod(k, HS // P)
                if c >= 2:
                    pe.wait_ge(sh_silu, c - 1)
                product(pe, ps[2 + c % 2][:, :], sw1_hi[:, e, n * P:(n + 1) * P], sw1_lo[:, e, n * P:(n + 1) * P],
                        blk(xn_hi, tb), blk(xn_lo, tb)).then_inc(sh_made, 1)

            def shared_out(c):
                k, tb = divmod(c, NBLK)
                pe.wait_ge(sh_silu, c + 1)
                if k == 0:
                    pe.wait_ge(dt_left, tb + 1)
                pe.matmul(ps[4 + tb][:, :], sw2_sb[:, k, :], hid[:, c % 2, 2, :], start=(k == 0), stop=False,
                          skip_group_check=True).then_inc(sh_used, 1)

            def turn_cw(b):
                pe.wait_ge(cw_ready, 1)
                if b >= 2:
                    pe.wait_ge(cw_copied, b - 1)
                    pe.wait_ge(cw_split, b - 1)
                for n in range(TPB):
                    ins = pe.transpose(ps[b % 2][:, n * P:(n + 1) * P], xn_tok[:, b * TPB + n, :], ident[:, :])
                ins.then_inc(cw_turned, 1)

            def second_biases(b):
                pe.wait_ge(cw_copied, b + 1)
                pe.matmul(ps[4 + b][:, :], b2_sb[:, :], cw_b2[:, b % 2, :], start=False, stop=False,
                          skip_group_check=True).then_inc(b2_used, 1)

            shared_in(0)
            for c in range(NSH * NBLK):
                if c == NBLK:
                    turn_cw(0)
                    turn_cw(1)
                    second_biases(0)
                    turn_cw(2)
                    second_biases(1)
                    turn_cw(3)
                if c + 1 < NSH * NBLK:
                    shared_in(c + 1)
                shared_out(c)
                if c == NBLK + 1:
                    second_biases(2)
                    second_biases(3)
            pe.wait_ge(cw_split, NBLK)

            def expert_in(i, s):
                j, tb = divmod(s, NBLK)
                if tb == 0:
                    pe.wait_ge(g_split, i * GPI + j + 1)
                pe.wait_ge(hid_done, i * GSTEPS + s + 1)
                product(pe, ps[s % 2][:, :], g_hi[j][:, :], g_lo[j][:, :], blk(xn_hi, tb), blk(xn_lo, tb)
                        ).then_inc(h_made, 1)
                pe.wait_ge(c1_done, i * GSTEPS + s + 1)
                pe.matmul(ps[2 + s % 2][:, :], sel_now[j][:, :], blk(cw_hl, tb), start=True, stop=True
                          ).then_inc(cwx_made, 1)

            def expert_out(i, s, last):
                j, tb = divmod(s, NBLK)
                if tb == 0:
                    pe.wait_ge(g_w2_in[j], i * 16 + 16)
                pe.wait_ge(hid_done, i * GSTEPS + s + 3)
                pe.matmul(ps[4 + tb][:, :], g_w2[j][:, :], hid_ring[s % 2], start=False,
                          stop=last and j == GPI - 1, skip_group_check=True).then_inc(g_out, 1)

            pe.nop().then_inc(g_out, 2)
            expert_in(0, 0)
            expert_in(0, 1)

            def group_turn(i, last):
                for s in range(GSTEPS):
                    if s + 2 < GSTEPS:
                        expert_in(i, s + 2)
                    elif not last:
                        expert_in(i + 1, s + 2 - GSTEPS)
                    expert_out(i, s, last)

            with pe.Fori(0, NG // GPI - 1) as i:
                group_turn(i, False)
            group_turn(NG // GPI - 1, True)
            for b in range(NBLK):
                pe.wait_ge(sum_ready, b + 1)
                for n in range(TPB):
                    ins = pe.transpose(ps[b][:, n * P:(n + 1) * P], y_t[:, b * TB + n * P:b * TB + (n + 1) * P],
                                       ident[:, :])
                ins.then_inc(sum_turned, 1)


_INS = ['L0_attn_x', 'L0_attn_wq', 'L0_attn_wk', 'L0_attn_wv', 'L0_attn_wa', 'L0_attn_wg', 'L0_attn_wo',
        'L0_attn_rms_scale', 'L0_ffn_wqkv', 'L0_ffn_w1', 'L0_ffn_w2', 'L1_attn_A_log', 'L1_attn_B_mat',
        'L1_attn_C_mat', 'L1_attn_D_vec', 'L1_attn_W_dt', 'L1_attn_b_dt', 'L1_ffn_router_w', 'L1_ffn_router_b',
        'L1_ffn_w1', 'L1_ffn_b1', 'L1_ffn_w2', 'L1_ffn_b2', 'L1_ffn_sw1', 'L1_ffn_sb1', 'L1_ffn_sw2',
        'L1_ffn_sb2']


def kernel(**inputs):
    import numpy as _np
    import concourse.bacc as _bacc
    from concourse import mybir as _mybir
    from concourse.bass_utils import run_bass_kernel_spmd as _run

    nc = _bacc.Bacc("TRN2", target_bir_lowering=False, num_devices=1)
    arrays, args = {}, []
    for name in _INS:
        a = _np.ascontiguousarray(inputs[name])
        arrays[f"in_{name}"] = a
        args.append(nc.dram_tensor(f"in_{name}", a.shape, _mybir.dt.from_np(a.dtype), kind="ExternalInput").ap())
    x = arrays["in_L0_attn_x"]
    args.append(nc.dram_tensor("out_0", x.shape, _mybir.dt.from_np(x.dtype), kind="ExternalOutput").ap())
    program(nc, *args)
    r = _run(nc, [arrays], core_ids=[0])
    return r.results[0]["out_0"]
```
